# Optimizing a Trainium2 kernel written in Bass

```python
import numpy as np
import jax
import jax.numpy as jnp

def _softmax(x, axis=-1):
    return jax.nn.softmax(x, axis=axis)

def _gelu(x):
    return jax.nn.gelu(x, approximate=True)

def _silu(x):
    return jax.nn.silu(x)

def _sigmoid(x):
    return jax.nn.sigmoid(x)

def _layernorm(x, axis=-1, eps=1e-05):
    m = jnp.mean(x, axis=axis, keepdims=True)
    v = jnp.var(x, axis=axis, keepdims=True)
    return (x - m) / jnp.sqrt(v + eps)

def _scatter_add(tgt, idx, src, axis=0):
    return tgt.at[idx].add(src)

def _segment_sum(src, seg, n):
    return jax.ops.segment_sum(src, seg, n)
kernel_name = 'mk_decoder_preln_d1_seqx_r8_8abb14'

def setup_inputs(seed: int=0):
    np.random.seed(seed)
    _w = jnp.asarray

    def _rec_inputs():
        import jax
        import jax.numpy as jnp
        _rk = jax.random.key(seed)
        x = -1.394e-06 + 0.9999 * jax.random.normal(jax.random.fold_in(_rk, 1), (64, 64, 128), jnp.float32)
        _lenS = 64 - jax.random.randint(jax.random.fold_in(_rk, 7), (64,), 0, max(1, 64 // 4) + 1, jnp.int32)
        _lenS2 = 64 - jax.random.randint(jax.random.fold_in(_rk, 8), (64,), 0, max(1, 64 // 4) + 1, jnp.int32)
        _ctx_1024P = jax.random.normal(jax.random.fold_in(_rk, 11), (64, 16, 128), jnp.float32)
        _ctx_1024c = jax.random.dirichlet(jax.random.fold_in(_rk, 511), 0.3 * jnp.ones((16,), jnp.float32), (64, 64))
        _ctx_1024t = jnp.einsum('bsk,bkd->bsd', _ctx_1024c, _ctx_1024P)
        _ctx_1024t = _ctx_1024t * jax.lax.rsqrt(jnp.mean(jnp.square(_ctx_1024t)) + 1e-12) * 0.953939
        ctx_1024 = -0.000292821 + 1.00034 * (_ctx_1024t + 0.3 * jax.random.normal(jax.random.fold_in(_rk, 611), (64, 64, 128), jnp.float32))
        return (x, ctx_1024)
    x, ctx_1024 = _rec_inputs()

    def _L0_attn_setup():
        import jax, jax.numpy as jnp
        import numpy as np
        import math
        B, S, D = (4, 256, 128)
        H, KV = (16, 4)
        HD = D // H
        GROUPS = H // KV

        def _alibi_slopes(n):
            start = 2.0 ** (-2.0 ** (-(math.log2(n) - 3)))
            return np.array([start * start ** i for i in range(n)], dtype=np.float32)
        key = jax.random.key(seed)
        ks = jax.random.split(key, 5)
        sc = 0.02
        return {'x': jax.random.normal(ks[0], (B, S, D), jnp.float32), 'Wq': jax.random.normal(ks[1], (D, H * HD), jnp.float32) * sc, 'Wk': jax.random.normal(ks[2], (D, KV * HD), jnp.float32) * sc, 'Wv': jax.random.normal(ks[3], (D, KV * HD), jnp.float32) * sc, 'Wo': jax.random.normal(ks[4], (H * HD, D), jnp.float32) * sc}
    _L0_attn_all = _L0_attn_setup()
    _L0_attn_in = {k: v for k, v in _L0_attn_all.items() if k in ('Wq', 'Wk', 'Wv', 'Wo')}
    del _L0_attn_all

    def _L0_xattn_setup():
        import jax, jax.numpy as jnp
        import numpy as np
        NEG_INF = -1e+30
        key = jax.random.key(seed)
        ks = jax.random.split(key, 7)
        B, S, D, H, HD = (2, 256, 128, 16, 64)
        scale = 1.0 / np.sqrt(D)
        return {'keys': jax.random.normal(ks[0], (B, S, D), dtype=jnp.float32), 'queries': jax.random.normal(ks[1], (B, S, D), dtype=jnp.float32), 'values': jax.random.normal(ks[2], (B, S, D), dtype=jnp.float32), 'Wq': jax.random.normal(ks[3], (H, D, HD), dtype=jnp.float32) * scale, 'Wk': jax.random.normal(ks[4], (H, D, HD), dtype=jnp.float32) * scale, 'Wv': jax.random.normal(ks[5], (H, D, HD), dtype=jnp.float32) * scale, 'Wo': jax.random.normal(ks[6], (H * HD, D), dtype=jnp.float32) * scale}
    _L0_xattn_all = _L0_xattn_setup()
    _L0_xattn_in = {k: v for k, v in _L0_xattn_all.items() if k in ('Wq', 'Wk', 'Wv', 'Wo')}
    del _L0_xattn_all

    def _L0_ffn_setup():
        import jax, jax.numpy as jnp
        import numpy as np
        B, S, F, E, K = (4, 128, 128, 8, 2)
        H = 4 * F
        key = jax.random.key(seed)
        ks = jax.random.split(key, 7)

        def xavier(k, shape):
            fan_in, fan_out = (shape[-2], shape[-1])
            scale = jnp.sqrt(6.0 / (fan_in + fan_out))
            return jax.random.uniform(k, shape, jnp.float32, -scale, scale)
        return {'x': jax.random.normal(ks[0], (B, S, F), jnp.float32), 'Wg': xavier(ks[1], (F, E)), 'bg': jnp.zeros((E,), jnp.float32), 'W1': xavier(ks[2], (E, F, H)), 'b1': jnp.zeros((E, H), jnp.float32), 'W2': xavier(ks[3], (E, H, F)), 'b2': jnp.zeros((E, F), jnp.float32)}
    _L0_ffn_all = _L0_ffn_setup()
    _L0_ffn_in = {k: v for k, v in _L0_ffn_all.items() if k in ('Wg', 'bg', 'W1', 'b1', 'W2', 'b2')}
    del _L0_ffn_all
    return {'x': x, 'ctx_1024': ctx_1024, 'L0_attn_Wq': _L0_attn_in['Wq'], 'L0_attn_Wk': _L0_attn_in['Wk'], 'L0_attn_Wv': _L0_attn_in['Wv'], 'L0_attn_Wo': _L0_attn_in['Wo'], 'L0_xattn_Wq': _L0_xattn_in['Wq'], 'L0_xattn_Wk': _L0_xattn_in['Wk'], 'L0_xattn_Wv': _L0_xattn_in['Wv'], 'L0_xattn_Wo': _L0_xattn_in['Wo'], 'L0_ffn_Wg': _L0_ffn_in['Wg'], 'L0_ffn_bg': _L0_ffn_in['bg'], 'L0_ffn_W1': _L0_ffn_in['W1'], 'L0_ffn_b1': _L0_ffn_in['b1'], 'L0_ffn_W2': _L0_ffn_in['W2'], 'L0_ffn_b2': _L0_ffn_in['b2']}

def reference(x, ctx_1024, L0_attn_Wq, L0_attn_Wk, L0_attn_Wv, L0_attn_Wo, L0_xattn_Wq, L0_xattn_Wk, L0_xattn_Wv, L0_xattn_Wo, L0_ffn_Wg, L0_ffn_bg, L0_ffn_W1, L0_ffn_b1, L0_ffn_W2, L0_ffn_b2):
    import jax
    import jax.numpy as jnp

    def _L0_attn_ref(x, Wq, Wk, Wv, Wo):
        import jax, jax.numpy as jnp
        import numpy as np
        import math
        B, S, D = (4, 256, 128)
        H, KV = (16, 4)
        HD = D // H
        GROUPS = H // KV

        def _alibi_slopes(n):
            start = 2.0 ** (-2.0 ** (-(math.log2(n) - 3)))
            return np.array([start * start ** i for i in range(n)], dtype=np.float32)
        b, s, _ = x.shape
        scale = HD ** (-0.5)
        q = (x @ Wq).reshape(b, s, H, HD).transpose(0, 2, 1, 3)
        k = (x @ Wk).reshape(b, s, KV, HD).transpose(0, 2, 1, 3)
        v = (x @ Wv).reshape(b, s, KV, HD).transpose(0, 2, 1, 3)
        k = jnp.repeat(k, GROUPS, axis=1)
        v = jnp.repeat(v, GROUPS, axis=1)
        attn = jnp.einsum('bhqd,bhkd->bhqk', q, k) * scale
        slopes = jnp.asarray(_alibi_slopes(H))
        pos = jnp.arange(s, dtype=jnp.float32)
        rel = pos[None, :] - pos[:, None]
        attn = attn + slopes[None, :, None, None] * rel[None, None, :, :]
        attn = jax.nn.softmax(attn, axis=-1)
        out = jnp.einsum('bhqk,bhkd->bhqd', attn, v)
        out = out.transpose(0, 2, 1, 3).reshape(b, s, H * HD)
        return out @ Wo

    def _L0_xattn_ref(keys, queries, values, Wq, Wk, Wv, Wo):
        import jax, jax.numpy as jnp
        import numpy as np
        NEG_INF = -1e+30
        B, S, D = keys.shape
        H, _, HD = Wq.shape
        q = jnp.einsum('bsd,hde->bhse', queries, Wq)
        k = jnp.einsum('bsd,hde->bhse', keys, Wk)
        v = jnp.einsum('bsd,hde->bhse', values, Wv)
        scores = jnp.einsum('bhqe,bhke->bhqk', q, k) / jnp.sqrt(jnp.float32(HD))
        tril = jnp.tril(jnp.ones((S, S), dtype=bool))
        scores = jnp.where(tril, scores, NEG_INF)
        attn = jax.nn.softmax(scores, axis=-1)
        out = jnp.einsum('bhqk,bhke->bhqe', attn, v)
        concat = out.transpose(0, 2, 1, 3).reshape(B, S, H * HD)
        return concat @ Wo

    def _L0_ffn_ref(x, Wg, bg, W1, b1, W2, b2):
        import jax, jax.numpy as jnp
        import numpy as np
        B, S, F, E, K = (4, 128, 128, 8, 2)
        H = 4 * F
        gate_probs = jax.nn.softmax(x @ Wg + bg, axis=-1)
        k = K
        _, top_idx = jax.lax.top_k(gate_probs, k)
        expert_mask = jax.nn.one_hot(top_idx, gate_probs.shape[-1], dtype=gate_probs.dtype).sum(-2)
        selected = gate_probs * expert_mask
        selected = selected / (selected.sum(-1, keepdims=True) + 1e-08)
        h = jax.nn.gelu(jnp.einsum('bsf,efh->bseh', x, W1) + b1)
        expert_out = jnp.einsum('bseh,ehf->bsef', h, W2) + b2[None, None]
        return jnp.einsum('bsef,bse->bsf', expert_out, selected)
    x = x + _L0_attn_ref(_layernorm(x, axis=-1), L0_attn_Wq, L0_attn_Wk, L0_attn_Wv, L0_attn_Wo)
    x = x + _L0_xattn_ref(ctx_1024, _layernorm(x, axis=-1), ctx_1024, L0_xattn_Wq, L0_xattn_Wk, L0_xattn_Wv, L0_xattn_Wo)
    x = x + _L0_ffn_ref(_layernorm(x, axis=-1), L0_ffn_Wg, L0_ffn_bg, L0_ffn_W1, L0_ffn_b1, L0_ffn_W2, L0_ffn_b2)
    return x

_drawn_inputs = setup_inputs


def setup_inputs(seed=0):
    import zlib

    import numpy as np

    out = dict(_drawn_inputs(seed))
    spreads = {'L0_ffn_bg': (0.0, 0.274), 'L0_ffn_b1': (0.0, 0.274), 'L0_ffn_b2': (0.0, 0.1)}
    factors = {'L0_attn_Wq': 8.0, 'L0_attn_Wk': 8.0, 'L0_attn_Wv': 4.337, 'L0_attn_Wo': 4.285}
    for name, (base, spread) in spreads.items():
        noise = np.random.default_rng([zlib.crc32(name.encode()), seed]).standard_normal(out[name].shape)
        drawn = base * np.exp(spread * noise) if base else spread * noise
        out[name] = jnp.asarray(drawn.astype(out[name].dtype))
    for name, factor in factors.items():
        out[name] = (out[name] * factor).astype(out[name].dtype)
    return out
```

```python
import concourse.bass as bass
from concourse import mybir
from contextlib import ExitStack

FP32 = mybir.dt.float32
FP32R = mybir.dt.float32r
BF16 = mybir.dt.bfloat16
ALU = mybir.AluOpType
ACT = mybir.ActivationFunctionType
AX = mybir.AxisListType

P = 128
BATCH, SEQ, D = 64, 64, 128
STEP = 4
TOK = STEP * SEQ
TPS = TOK // P
STEPS = BATCH // STEP
TILES = BATCH * SEQ // P
EPS = 1e-5
X_PARTS = [0, 1, 2, 3]

H1, G1, HD1 = 16, 4, 8
HG = H1 // G1
MAX_ROW, ALIBI_ROW = 96, 100


def live(i, n):
    return not isinstance(i, int) or 0 <= i < n


def wait(eng, sem, value):
    if not isinstance(value, int) or value > 0:
        eng.wait_ge(sem, value)


def cap(count, n):
    return min(count, n) if isinstance(count, int) else count


def pipeline(eng, first, last, body, ahead=2):
    lo, hi = 2, (STEPS - ahead) // 2 * 2
    for s in range(first, lo):
        body(s, s % 2)
    with eng.Fori(lo // 2, hi // 2) as pair:
        for parity in range(2):
            body(2 * pair + parity, parity)
    for s in range(hi, last):
        body(s, s % 2)


def self_attention(nc, x_sb, x_loaded, w, sem, sb, pb):
    f32 = lambda name, *shape: sb(name, [P, *shape], FP32)
    f32r = lambda name, *shape: sb(name, [P, *shape], FP32R)

    wq_raw, wk_raw = f32("sa_wq_raw", HG * P), f32("sa_wk_raw", G1 * P)
    wq_hi, wq_lo = f32r("sa_wq_hi", HG, P), f32r("sa_wq_lo", HG, P)
    wk_hi, wk_lo = f32r("sa_wk_hi", G1, P), f32r("sa_wk_lo", G1, P)
    wv, wo = f32("sa_wv", P), f32("sa_wo", P)
    ident, ones_gd = f32("sa_ident", P), f32("sa_ones", 2, 32)
    q_rows, k_rows = f32("sa_q_rows", STEP * HG * SEQ), f32("sa_k_rows", STEP * G1 * SEQ)
    half, eps = f32("sa_half", TPS), f32("sa_eps", TPS)
    zeros = f32("sa_zeros", STEP * HG * SEQ)
    stats, mean_var = f32("sa_stats", 2, TPS, 6), f32("sa_mean_var", 2, TPS, 2)
    var_eps, rstd = f32("sa_var_eps", TPS), f32("sa_rstd", 2, TPS)
    xn = f32("sa_xn", 2, TPS, P)
    xT, xT_hi, xT_lo = f32("sa_xT", 2, TOK), f32r("sa_xT_hi", 2, TOK), f32r("sa_xT_lo", 2, TOK)
    q_st = f32r("sa_q_st", 2, STEP, HG, SEQ)
    k_st = f32r("sa_k_st", 2, STEP, G1, SEQ)
    v_bd = f32("sa_v_bd", 2, STEP, 96)
    z = f32("sa_z", 2, 2, P)
    probs = f32("sa_probs", 2, 2, HG * SEQ)
    recip, att = f32("sa_recip", HG * SEQ), f32("sa_att", 2, HG, SEQ)
    attT = f32("sa_attT", 2, TOK)

    ps_t = pb("ps_t")
    ps_proj = [pb("ps_proj0"), pb("ps_proj1")]
    ps_s, ps_z, ps_st = pb("ps_s"), pb("ps_z"), pb("ps_st")
    ps_pv = [pb("ps_pv0"), pb("ps_pv1")]

    s_wload = sem("sa_weights_loaded")
    s_prep = sem("sa_weights_split")
    s_zero = sem("sa_zeroed")
    s_stats, s_aggr = sem("sa_stats_done"), sem("sa_mean_var_done")
    s_vare, s_rstd, s_xn = sem("sa_var_eps_done"), sem("sa_rstd_done"), sem("sa_xn_done")
    s_T, s_V, s_proj = sem("sa_transposed"), sem("sa_v_product"), sem("sa_qk_product")
    s_xTf, s_xThi, s_xTlo = sem("sa_xT_copied"), sem("sa_xT_hi_done"), sem("sa_xT_lo_done")
    s_vbd = sem("sa_v_placed")
    s_hi, s_lo = sem("sa_qk_hi_done"), sem("sa_qk_lo_done")
    s_S, s_max, s_Z, s_rows = sem("sa_scores"), sem("sa_max"), sem("sa_max_transposed"), sem("sa_max_rows")
    s_ST, s_exp, s_PV = sem("sa_scoresT"), sem("sa_exp_done"), sem("sa_pv_product")
    s_rec, s_att = sem("sa_reciprocal"), sem("sa_normalised")
    s_move = [sem("sa_att_moved_even"), sem("sa_att_moved_odd")]
    s_out = [sem("sa_att_out_even"), sem("sa_att_out_odd")]
    moved = lambda s, par: 8 * (s - par) + 16
    by_batch, by_head = [], []
    for n in ("even", "odd"):
        scratch = nc.dram_tensor(f"sa_scratch_{n}", (HG, 32, STEP, SEQ), FP32).ap()
        by_batch.append(scratch.rearrange("h r b q -> r h b q"))
        by_head.append(scratch.rearrange("h r b q -> (h r) (b q)"))
    s_Wo, s_res, s_reset = sem("sa_out_product"), sem("sa_residual"), sem("sa_max_rows_reset")

    LOADS = 9

    with nc.Block() as block:

        @block.sync
        def _(sp):
            for dst, src in ((wq_raw[:, :], w["sa_wq"]), (wk_raw[:, :], w["sa_wk"]), (wv[:, :], w["sa_wv"]),
                             (ident[:, :], w["ident"]), (z[:, :, :, :], w["sa_z"]),
                             (q_rows[:, :], w["sa_q_rows"]), (k_rows[:, :], w["sa_k_rows"]),
                             (ones_gd[:, :, :], w["sa_ones"]), (wo[:, :], w["sa_wo"])):
                sp.dma_start(dst, src).then_inc(s_wload, 16)

            def body(s, par):
                if live(s - 1, STEPS):
                    wait(sp, s_att, s)
                    for b in range(STEP):
                        sp.dma_start(by_batch[1 - par][:, :, b, :], att[32 * b:32 * b + 32, 1 - par, :, :])\
                          .then_inc(s_out[1 - par], 16)
                    wait(sp, s_out[1 - par], STEP * moved(s - 1, 1 - par))
                    sp.dma_start(attT[:, 1 - par, :], by_head[1 - par]).then_inc(s_move[1 - par], 16)

            pipeline(sp, 1, STEPS + 1, body)

        @block.gpsimd
        def _(pool):
            nc.gpsimd.memset(half[:, :], -0.5).then_inc(s_zero, 1)
            nc.gpsimd.memset(v_bd[:, :, :, :], 0.0).then_inc(s_zero, 1)
            nc.gpsimd.memset(eps[:, :], EPS).then_inc(s_zero, 1)
            nc.gpsimd.memset(zeros[:, :], 0.0).then_inc(s_zero, 1)
            pool.wait_ge(s_zero, 4)

            def body(s, par):
                if live(s + 2, STEPS):
                    wait(pool, s_aggr, s + 3)
                    wait(pool, s_rstd, s + 2)
                    wait(pool, s_reset, s - 1)
                    nc.gpsimd.tensor_tensor(var_eps[:, :], mean_var[:, par, :, 1], eps[:, :], ALU.add).then_inc(s_vare, 1)
                    pool.wait_ge(s_vare, s + 3)
                    nc.gpsimd.tensor_tensor(rstd[:, par, :], var_eps[:, :], half[:, :], ALU.pow).then_inc(s_rstd, 1)
                if live(s - 1, STEPS) and live(s + 1, STEPS):
                    wait(pool, s_ST, STEP * s)
                    if live(s + 2, STEPS):
                        wait(pool, s_rstd, s + 3)
                    wait(pool, s_reset, s - 1)
                    nothing = zeros[MAX_ROW:ALIBI_ROW, :]
                    nc.gpsimd.tensor_tensor(q_st[MAX_ROW:ALIBI_ROW, 1 - par, :, :, :].rearrange("p b h q -> p (b h q)"),
                                            nothing, nothing, ALU.add).then_inc(s_reset, 1)

            pipeline(pool, -2, STEPS, body)

        @block.scalar
        def _(act):
            act.wait_ge(s_wload, 16 * LOADS)
            for par in range(2):
                nc.scalar.copy(q_st[MAX_ROW:P, par, :, :, :].rearrange("p b h q -> p (b h q)"),
                               q_rows[MAX_ROW:P, :]).then_inc(s_prep, 1)
                nc.scalar.copy(k_st[MAX_ROW:P, par, :, :, :].rearrange("p b h q -> p (b h q)"),
                               k_rows[MAX_ROW:P, :]).then_inc(s_prep, 1)

            def slot(s, par, b):
                n = STEP * s + b
                if live(n - 1, BATCH):
                    buf = par if b else 1 - par
                    wait(act, s_Z, n)
                    nc.scalar.copy(q_st[MAX_ROW:P, buf, (b - 1) % STEP, :, :].rearrange("p h q -> p (h q)"),
                                   ps_z[MAX_ROW:P, 0:256]).then_inc(s_rows, 1)
                if b == 1 and live(s + 1, STEPS):
                    wait(act, s_V, s + 2)
                    if isinstance(s, int) and s == -1:
                        act.wait_ge(s_zero, 4)
                    for g2 in range(2):
                        src = ps_t[64 * g2:64 * g2 + 64, :].rearrange("p (b r) -> p b r", b=STEP)[:, :, 0:32]
                        src = src.rearrange("p b (g c) -> p b g c", g=2)[:, :, :, HD1 * g2:HD1 * g2 + HD1]
                        dst = v_bd[64 * g2:64 * g2 + 64, 1 - par, :, :].rearrange("p b (g c) -> p b g c", g=2)
                        nc.scalar.copy(dst[:, :, :, HD1 * g2:HD1 * g2 + HD1], src).then_inc(s_vbd, 1)
                if b == 2 and live(s + 2, STEPS):
                    wait(act, s_T, s + 3)
                    nc.scalar.copy(xT[:, par, :], ps_t[:, 0:TOK]).then_inc(s_xTf, 1)
                    nc.scalar.copy(xT_hi[:, par, :], ps_t[:, 0:TOK]).then_inc(s_xThi, 1)
                if live(n - 1, BATCH):
                    wait(act, s_ST, n)
                    nc.scalar.activation(probs[:, (b - 1) % 2, :, :].rearrange("p g n -> p (g n)"), ps_st[:, :],
                                         ACT.Exp).then_inc(s_exp, 1)
                if live(s + 1, STEPS):
                    wait(act, s_proj, n + STEP + 1)
                    st = (q_st, k_st)[b // 2]
                    dst = st[0:96, 1 - par, :, 2 * (b % 2):2 * (b % 2) + 2, :].rearrange("p b h q -> p h b q")
                    nc.scalar.copy(dst, ps_proj[b % 2][0:96, :].rearrange("p (h b q) -> p h b q", h=2, b=STEP))\
                      .then_inc(s_hi, 1)

            def body(s, par):
                for b in range(STEP):
                    slot(s, par, b)

            pipeline(act, -2, STEPS + 1, body)

        @block.vector
        def _(dve):
            dve.wait_ge(s_wload, 16 * LOADS)
            for raw, hi, lo, scale in ((wq_raw, wq_hi, wq_lo, HD1 ** -0.5), (wk_raw, wk_hi, wk_lo, 1.0)):
                flat = lambda t: t[:, :, :].rearrange("p a n -> p (a n)")
                nc.vector.tensor_scalar(raw[:, :], raw[:, :], scale, None, ALU.mult).then_inc(s_prep, 1)
                dve.wait_ge(s_prep, 5 if raw is wq_raw else 8)
                nc.vector.tensor_copy(flat(hi), raw[:, :]).then_inc(s_prep, 1)
                dve.wait_ge(s_prep, 6 if raw is wq_raw else 9)
                nc.vector.tensor_tensor(flat(lo), raw[:, :], flat(hi).bitcast(FP32), ALU.subtract).then_inc(s_prep, 1)

            def slot(s, par, b):
                n = STEP * s + b
                u = n + STEP - 1
                if b == 1 and live(s + 2, STEPS):
                    dve.wait_ge(s_stats, s + 3)
                if live(u, STEP * STEPS):
                    st, rows = ((q_st, 64), (q_st, 64), (k_st, 32), (k_st, 32))[(b - 1) % STEP]
                    buf = 1 - par if b else par
                    j = (b - 1) % 2
                    wait(dve, s_hi, u + 1)
                    dst = st[rows:rows + 32, buf, :, 2 * j:2 * j + 2, :].rearrange("p b h q -> p h b q")
                    nc.vector.tensor_tensor(dst, ps_proj[j][rows:rows + 32, :].rearrange("p (h b q) -> p h b q", h=2, b=STEP),
                                            dst.bitcast(FP32), ALU.subtract).then_inc(s_lo, 1)
                if b == 1 and live(s + 2, STEPS):
                    for t in range(TPS):
                        ins = nc.vector.bn_aggr(mean_var[:, par, t, :], stats[:, par, t, :])
                    ins.then_inc(s_aggr, 1)
                if live(n, BATCH):
                    wait(dve, s_S, n + 1)
                    nc.vector.tensor_reduce(z[:, b % 2, :, MAX_ROW:MAX_ROW + G1],
                                            ps_s[:, :].rearrange("p (a g k) -> p a g k", a=2, g=G1),
                                            axis=AX.X, op=ALU.max, negate=True).then_inc(s_max, 1)
                if b == 0 and live(s + 2, STEPS):
                    if isinstance(s, int) and s + 2 in X_PARTS:
                        dve.wait_ge(x_loaded[X_PARTS.index(s + 2)], 16)
                    for t in range(TPS):
                        ins = nc.vector.bn_stats(stats[:, par, t, :], x_sb[:, bass.ds(TPS * (s + 2) + t, 1), :].rearrange("p a n -> p (a n)"))
                    ins.then_inc(s_stats, 1)
                if b == 0 and live(s - 2, STEPS):
                    wait(dve, s_Wo, s - 1)
                    rows = x_sb[:, bass.ds(TPS * (s - 2), TPS), :]
                    nc.vector.tensor_tensor(rows, ps_t[:, 0:TOK].rearrange("p (t n) -> p t n", t=TPS), rows, ALU.add)\
                      .then_inc(s_res, 1)
                if b == 2 and live(s + 2, STEPS):
                    wait(dve, s_rstd, s + 3)
                    for t in range(TPS):
                        ins = nc.vector.tensor_scalar(xn[:, par, t, :], x_sb[:, bass.ds(TPS * (s + 2) + t, 1), :].rearrange("p a n -> p (a n)"),
                                                      mean_var[:, par, t, 0:1], rstd[:, par, t:t + 1],
                                                      ALU.subtract, ALU.mult)
                    ins.then_inc(s_xn, 1)
                if b == 1 and live(s - 1, STEPS):
                    wait(dve, s_PV, STEP * s)
                    acc = ps_pv[1 - par]
                    nc.vector.reciprocal(recip[:, :], acc[:, 256:512]).then_inc(s_rec, 1)
                    wait(dve, s_rec, s)
                    nc.vector.tensor_tensor(att[:, 1 - par, :, :].rearrange("p h q -> p (h q)"), acc[:, 0:256],
                                            recip[:, :], ALU.mult).then_inc(s_att, 1)
                if b == 3 and live(s + 2, STEPS):
                    wait(dve, s_xThi, s + 3)
                    wait(dve, s_xTf, s + 3)
                    nc.vector.tensor_tensor(xT_lo[:, par, :], xT[:, par, :], xT_hi[:, par, :].bitcast(FP32),
                                            ALU.subtract).then_inc(s_xTlo, 1)

            def body(s, par):
                for b in range(STEP):
                    slot(s, par, b)

            pipeline(dve, -2, STEPS + 3, body)

        @block.tensor
        def _(pe):
            pe.wait_ge(s_wload, 16 * LOADS)
            pe.wait_ge(s_prep, 10)

            def slot(s, par, b):
                n = STEP * s + b
                prev = par if b else 1 - par
                if live(n - 1, BATCH):
                    wait(pe, s_max, n)
                    for a in range(2):
                        ins = nc.tensor.transpose(ps_z[:, a * P:(a + 1) * P], z[:, (b - 1) % 2, a, :], ident[:, :])
                    ins.then_inc(s_Z, 1)
                if live(n, BATCH):
                    wait(pe, s_lo, STEP * (s + 1))
                    wait(pe, s_reset, s - 1)
                    for a in range(2):
                        ins = nc.tensor.matmul(ps_s[:, a * 256:(a + 1) * 256],
                                               q_st[:, par, b, 2 * a:2 * a + 2, :].rearrange("p h q -> p (h q)"),
                                               k_st[:, par, b, :, :].rearrange("p g k -> p (g k)"), start=True, stop=True)
                    ins.then_inc(s_S, 1)
                if live(n - 2, BATCH):
                    m, owner = (b - 2) % STEP, par if b >= 2 else 1 - par
                    wait(pe, s_exp, n - 1)
                    if b == 2:
                        wait(pe, s_att, s - 1)
                    rows = slice(32 * m, 32 * m + 32)
                    for out, weights in ((0, v_bd[:, owner, m, :]), (256, ones_gd[:, :, :].rearrange("p g c -> p (g c)"))):
                        for gp in range(2):
                            ins = nc.tensor.matmul(ps_pv[owner][rows, out:out + 256], weights[:, 32 * gp:32 * gp + 32],
                                                   probs[:, m % 2, gp, :], start=(gp == 0), stop=(gp == 1),
                                                   tile_position=(0, 32 * m), skip_group_check=True)
                    ins.then_inc(s_PV, 1)
                if b == 0 and live(s - 2, STEPS):
                    wait(pe, s_move[par], moved(s - 2, par))
                    wait(pe, s_xThi, cap(s + 2, STEPS))
                    for t in range(TPS):
                        ins = nc.tensor.matmul(ps_t[:, t * P:(t + 1) * P], attT[:, par, t * P:(t + 1) * P], wo[:, :],
                                               start=True, stop=True)
                    ins.then_inc(s_Wo, 1)
                if b == 1 and live(s + 1, STEPS):
                    wait(pe, s_xTf, s + 2)
                    wait(pe, s_xThi, s + 2)
                    wait(pe, s_res, s - 1)
                    for m in range(STEP):
                        for g2 in range(2):
                            ins = nc.tensor.matmul(ps_t[64 * g2:64 * g2 + 64, m * P:(m + 1) * P],
                                                   xT[:, 1 - par, m * SEQ:(m + 1) * SEQ], wv[:, :], start=True, stop=True)
                    ins.then_inc(s_V, 1)
                if b == 2 and live(s + 2, STEPS):
                    wait(pe, s_xn, s + 3)
                    wait(pe, s_vbd, 2 * (s + 2))
                    for t in range(TPS):
                        ins = nc.tensor.transpose(ps_t[:, t * P:(t + 1) * P], xn[:, par, t, :], ident[:, :])
                    ins.then_inc(s_T, 1)
                if live(n - 1, BATCH):
                    wait(pe, s_rows, n)
                    wait(pe, s_exp, n - 1)
                    for gp in range(2):
                        ins = nc.tensor.matmul(ps_st[:, gp * 256:(gp + 1) * 256],
                                               k_st[:, prev, (b - 1) % STEP, 2 * gp:2 * gp + 2, :].rearrange("p g k -> p (g k)"),
                                               q_st[:, prev, (b - 1) % STEP, :, :].rearrange("p h q -> p (h q)"),
                                               start=True, stop=True)
                    ins.then_inc(s_ST, 1)
                if live(s + 1, STEPS):
                    wait(pe, s_xTlo, s + 2)
                    wait(pe, s_lo, n + STEP - 1)
                    hi, lo = ((wq_hi, wq_lo), (wk_hi, wk_lo))[b // 2]
                    for j in range(2):
                        h = 2 * (b % 2) + j
                        out = ps_proj[b % 2][:, j * TOK:(j + 1) * TOK]
                        nc.tensor.matmul(out, hi[:, h, :], xT_hi[:, 1 - par, :], start=True, stop=False)
                        nc.tensor.matmul(out, lo[:, h, :], xT_hi[:, 1 - par, :], start=False, stop=False)
                        ins = nc.tensor.matmul(out, hi[:, h, :], xT_lo[:, 1 - par, :], start=False, stop=True)
                    ins.then_inc(s_proj, 1)

            def body(s, par):
                for b in range(STEP):
                    slot(s, par, b)

            pipeline(pe, -2, STEPS + 2, body)


H2, HD2 = 16, 64
HALF = H2 // 2
VW = HD2 + 1


def cross_attention(nc, x_sb, w, sem, sb, pb):
    f32 = lambda name, *shape: sb("ca_" + name, [P, *shape], FP32)
    f32r = lambda name, *shape: sb("ca_" + name, [P, *shape], FP32R)
    bf16 = lambda name, *shape: sb("ca_" + name, [P, *shape], BF16)

    wqT, wkT = f32("wqT", H2 // 2, P), f32("wkT", H2 // 2, P)
    a_hi, a_lo = f32r("a_hi", H2, P), f32r("a_lo", H2, P)
    a_raw = f32("a_raw", 4 * P)
    wv_hi, wv_lo = f32r("wv_hi", H2 * HD2), f32r("wv_lo", H2 * HD2)
    wo = f32("wo", 8, P)
    ident, ident_bf, mask_bf = f32("ident", P), bf16("ident_bf", P), bf16("mask_bf", HALF * SEQ)
    pick = f32r("pick", P)
    keys = f32("keys", 2, TOK)
    ctx_hi, ctx_lo = f32r("ctx_hi", 2, TOK), f32r("ctx_lo", 2, TOK)
    half, eps, zeros = f32("half", TPS), f32("eps", TPS), f32("zeros", TOK)
    stats, mean_var = f32("stats", 2, TPS, 6), f32("mean_var", 2, TPS, 2)
    var_eps, rstd = f32("var_eps", TPS), f32("rstd", 2, TPS)
    xn = f32("xn", 2, TPS, P)
    xT_hi, xT_lo = f32r("xT_hi", 2, TOK), f32r("xT_lo", 2, TOK)
    t_all = f32("t", 2, H2, TOK)
    v_bd = f32("v_bd", 2, TPS, H2, 2, VW)
    raw = f32("raw", 2, HALF * SEQ)
    neg_max = f32("neg_max", 2, 4, 2)
    rows = f32r("rows", 2, HALF * SEQ)
    probs = f32("probs", 2, HALF, SEQ)
    recip = f32("recip", 2, 2, 2)
    o = f32("o", 2, 2, 4, HD2)
    oT = f32("oT", 2, 2, 2, 2, 2, SEQ)
    wv_raw = t_all[:, 0, 0:4, :].rearrange("p h n -> p (h n)")
    mask_raw = t_all[:, 0, 4:6, :].rearrange("p h n -> p (h n)")
    pick_raw = t_all[:, 0, 6, 0:P]

    ps_st = [pb("st0"), pb("st1")]
    ps_p = [pb("p0"), pb("p1")]
    ps_pv = [pb("pv0"), pb("pv1")]
    ps_x, ps_m = pb("x"), pb("m")

    names = ("loaded prep zeroed a_product a_scaled a_split stats mean_var var_eps rstd xn transposed xT_hi xT_lo "
             "ctx_hi ctx_lo scores raw_copied scores_transposed max max_transposed max_rows shifted exp pv_product "
             "reciprocal normalised o_transposed o_copied out_product residual fill fill_act fill_dve").split()
    S = {n: sem("ca_" + n) for n in names}
    s_keys = [sem("ca_keys_even"), sem("ca_keys_odd")]
    LOADS = 7
    tile_of_x = lambda t: x_sb[:, bass.ds(t, 1), :].rearrange("p a n -> p (a n)")

    with nc.Block() as block:

        @block.sync
        def _(sp):
            for dst, src in ((wqT[:, :, :], w["ca_wqT"]), (wkT[:, :, :], w["ca_wkT"]), (wv_raw, w["ca_wv"]),
                             (ident[:, :], w["ident"]), (mask_raw, w["ca_mask"]), (pick_raw, w["ca_pick"]),
                             (wo[:, :, :], w["ca_wo"])):
                sp.dma_start(dst, src).then_inc(S["loaded"], 16)

            def body(s, par):
                if live(s + 2, STEPS):
                    wait(sp, S["scores"], 4 * (s + 1))
                    sp.dma_start(keys[:, par, :], w["ctxT"][:, bass.ds(TOK * (s + 2), TOK)]).then_inc(s_keys[par], 16)

            pipeline(sp, -2, STEPS, body, 3)

        @block.gpsimd
        def _(pool):
            nc.gpsimd.memset(half[:, :], -0.5).then_inc(S["zeroed"], 1)
            nc.gpsimd.memset(rows[:, :, :].bitcast(FP32), 0.0).then_inc(S["zeroed"], 1)
            nc.gpsimd.memset(v_bd[:, :, :, :, :, :], 0.0).then_inc(S["zeroed"], 1)
            nc.gpsimd.memset(eps[:, :], EPS).then_inc(S["zeroed"], 1)
            nc.gpsimd.memset(zeros[:, :], 0.0).then_inc(S["zeroed"], 1)
            pool.wait_ge(S["zeroed"], 5)
            for b in range(2):
                nc.gpsimd.memset(v_bd[64 * b:64 * b + 64, :, :, :, b, HD2:VW], 1.0).then_inc(S["zeroed"], 1)
            pool.wait_ge(S["zeroed"], 7)
            pool.wait_ge(S["loaded"], 16 * LOADS)

            def body(s, par):
                if live(s + 3, STEPS):
                    wait(pool, S["mean_var"], s + 4)
                    wait(pool, S["ctx_lo"], s + 2)
                    nc.gpsimd.tensor_tensor(var_eps[:, :], mean_var[:, 1 - par, :, 1], eps[:, :], ALU.add)\
                      .then_inc(S["var_eps"], 1)
                    pool.wait_ge(S["var_eps"], s + 4)
                    nc.gpsimd.tensor_tensor(rstd[:, 1 - par, :], var_eps[:, :], half[:, :], ALU.pow).then_inc(S["rstd"], 1)
                if live(s + 2, STEPS):
                    wait(pool, S["rstd"], cap(s + 4, STEPS))
                    wait(pool, S["ctx_lo"], s + 2)
                    wait(pool, S["fill"], 12 * (s + 1))
                    wait(pool, s_keys[par], 8 * (s + 2 - par) + 16)
                    src = keys[:, par, :]
                    nc.gpsimd.tensor_tensor(ctx_hi[:, par, :], src, zeros[:, :], ALU.add).then_inc(S["ctx_hi"], 1)
                    pool.wait_ge(S["ctx_hi"], s + 3)
                    nc.gpsimd.tensor_tensor(ctx_lo[:, par, :], src, ctx_hi[:, par, :].bitcast(FP32), ALU.subtract)\
                      .then_inc(S["ctx_lo"], 1)

            pipeline(pool, -3, STEPS, body, 3)

        @block.scalar
        def _(act):
            act.wait_ge(S["loaded"], 16 * LOADS)
            nc.scalar.copy(ident_bf[:, :], ident[:, :]).then_inc(S["prep"], 1)
            nc.scalar.copy(mask_bf[:, :], mask_raw).then_inc(S["prep"], 1)
            nc.scalar.copy(pick[:, :], pick_raw).then_inc(S["prep"], 1)
            nc.scalar.copy(wv_hi[:, :], wv_raw).then_inc(S["prep"], 1)
            for c in range(4):
                act.wait_ge(S["a_product"], c + 1)
                wait(act, S["a_split"], 2 * c)
                nc.scalar.mul(a_raw[:, :], ps_p[c % 2][:, :], HD2 ** -0.5).then_inc(S["a_scaled"], 1)

            def slot(s, par, u):
                n = 4 * s + u
                f = n + 4
                if live(n - 1, 4 * STEPS):
                    wait(act, S["shifted"], n)
                    wait(act, S["pv_product"], n - 2)
                    nc.scalar.activation(probs[:, (u - 1) % 2, :, :].rearrange("p h q -> p (h q)"), ps_st[(u - 1) % 2][:, :],
                                         ACT.Exp).then_inc(S["exp"], 1)
                if live(n, 4 * STEPS):
                    wait(act, S["scores"], n + 1)
                    nc.scalar.copy(raw[:, u % 2, :], ps_st[u % 2][:, :]).then_inc(S["raw_copied"], 1)
                if live(s + 1, STEPS):
                    wait(act, S["fill"], 3 * f + 1)
                    nc.scalar.copy(t_all[:, 1 - par, 4 * u:4 * u + 2, :].rearrange("p h n -> p (h n)"), ps_p[u % 2][:, :])\
                      .then_inc(S["fill_act"], 1)
                if u == 0 and live(s + 2, STEPS):
                    wait(act, S["transposed"], s + 3)
                    nc.scalar.copy(xT_hi[:, par, :], ps_m[:, 0:TOK]).then_inc(S["xT_hi"], 1)
                if live(n, 4 * STEPS):
                    wait(act, S["max_transposed"], n + 1)
                    nc.scalar.copy(rows[0:2, u % 2, :], ps_x[0:2, :]).then_inc(S["max_rows"], 1)
                if live(s + 1, STEPS):
                    wait(act, S["fill"], 3 * f + 3)
                    nc.scalar.copy(v_bd[0:64, 1 - par, u // 2, HALF * (u % 2):HALF * (u % 2) + HALF, 0, 0:HD2],
                                   ps_p[u % 2][0:64, :].rearrange("p (h d) -> p h d", h=HALF)).then_inc(S["fill_act"], 1)

            def body(s, par):
                for u in range(4):
                    slot(s, par, u)

            pipeline(act, -2, STEPS + 1, body)

        @block.vector
        def _(dve):
            dve.wait_ge(S["prep"], 4)
            nc.vector.tensor_tensor(wv_lo[:, :], wv_raw, wv_hi[:, :].bitcast(FP32), ALU.subtract).then_inc(S["prep"], 1)
            for c in range(4):
                dve.wait_ge(S["a_scaled"], c + 1)
                heads = lambda t: t[:, :, :].rearrange("p (a b) n -> p a b n", b=2)[:, 4 * (c // 2):4 * (c // 2) + 4, c % 2, :]
                full = a_raw[:, :].rearrange("p (a n) -> p a n", a=4)
                nc.vector.tensor_copy(heads(a_hi), full).then_inc(S["a_split"], 1)
                dve.wait_ge(S["a_split"], 2 * c + 1)
                nc.vector.tensor_tensor(heads(a_lo), full, heads(a_hi).bitcast(FP32), ALU.subtract).then_inc(S["a_split"], 1)

            def slot(s, par, u):
                n = 4 * s + u
                f = n + 4
                if live(n - 2, 4 * STEPS):
                    m, owner = (u - 2) % 4, par if u >= 2 else 1 - par
                    wait(dve, S["o_transposed"], n - 1)
                    wait(dve, S["out_product"], 2 * (s - (u < 2)) + m // 2 - 1)
                    dst = oT[:, m // 2, m % 2, :, :, :, :].rearrange("p j h b q -> p b j h q")
                    for b in range(2):
                        ins = nc.vector.tensor_copy(dst[:, b, :, :, :], ps_x[:, 256 * b:256 * b + 256]
                                                    .rearrange("p (j h q) -> p j h q", j=2, h=2))
                    ins.then_inc(S["o_copied"], 1)
                if u == 2 and live(s + 3, STEPS):
                    for t in range(TPS):
                        ins = nc.vector.bn_stats(stats[:, 1 - par, t, :], tile_of_x(TPS * (s + 3) + t))
                    ins.then_inc(S["stats"], 1)
                    dve.wait_ge(S["stats"], s + 4)
                if live(n, 4 * STEPS):
                    wait(dve, S["scores_transposed"], n + 1)
                    nc.vector.tensor_reduce(neg_max[:, u % 2, :, :], ps_x[:, :].rearrange("p (a b k) -> p a b k", a=4, b=2),
                                            axis=AX.X, op=ALU.max, negate=True).then_inc(S["max"], 1)
                if u == 2 and live(s + 3, STEPS):
                    for t in range(TPS):
                        ins = nc.vector.bn_aggr(mean_var[:, 1 - par, t, :], stats[:, 1 - par, t, :])
                    ins.then_inc(S["mean_var"], 1)
                if u == 3 and live(s + 3, STEPS):
                    wait(dve, S["rstd"], s + 4)
                    for t in range(TPS):
                        ins = nc.vector.tensor_scalar(xn[:, 1 - par, t, :], tile_of_x(TPS * (s + 3) + t),
                                                      mean_var[:, 1 - par, t, 0:1], rstd[:, 1 - par, t:t + 1],
                                                      ALU.subtract, ALU.mult)
                    ins.then_inc(S["xn"], 1)
                if live(n - 1, 4 * STEPS):
                    wait(dve, S["pv_product"], n)
                    for c in range(2):
                        acc = ps_pv[c][:, 0:4 * VW].rearrange("p (a b d) -> p a b d", a=2, b=2)
                        ins = nc.vector.reciprocal(recip[:, c, :, :], acc[:, :, :, HD2])
                    ins.then_inc(S["reciprocal"], 1)
                    dve.wait_ge(S["reciprocal"], n)
                    wait(dve, S["o_transposed"], n - 2)
                    for c in range(2):
                        acc = ps_pv[c][:, 0:4 * VW].rearrange("p (a b d) -> p a b d", a=2, b=2)
                        dst = o[:, (u - 1) % 2, :, 2 * c:2 * c + 2, :].rearrange("p b a d -> p a b d")
                        ins = nc.vector.tensor_tensor(dst, acc[:, :, :, 0:HD2],
                                                      recip[:, c, :, :].unsqueeze(3).broadcast_to([P, 2, 2, HD2]), ALU.mult)
                    ins.then_inc(S["normalised"], 1)
                if live(s + 1, STEPS):
                    wait(dve, S["fill"], 3 * f + 2)
                    nc.vector.tensor_copy(t_all[:, 1 - par, 4 * u + 2:4 * u + 4, :].rearrange("p h n -> p (h n)"),
                                          ps_p[(u + 1) % 2][:, :]).then_inc(S["fill_dve"], 1)
                if u == 0 and live(s + 2, STEPS):
                    wait(dve, S["xT_hi"], s + 3)
                    nc.vector.tensor_tensor(xT_lo[:, par, :], ps_m[:, 0:TOK], xT_hi[:, par, :].bitcast(FP32),
                                            ALU.subtract).then_inc(S["xT_lo"], 1)
                if live(s + 1, STEPS):
                    wait(dve, S["fill"], 3 * f + 3)
                    nc.vector.tensor_copy(v_bd[64:128, 1 - par, u // 2, HALF * (u % 2):HALF * (u % 2) + HALF, 1, 0:HD2],
                                          ps_p[u % 2][64:128, :].rearrange("p (h d) -> p h d", h=HALF)).then_inc(S["fill_dve"], 1)
                tile = {1: TPS * (s - 1) + 1, 3: TPS * s}.get(u)
                if tile is not None and live(tile, TILES):
                    wait(dve, S["out_product"], tile + 1)
                    row = tile_of_x(tile)
                    nc.vector.tensor_tensor(row, ps_m[:, 0:P], row, ALU.add).then_inc(S["residual"], 1)

            def body(s, par):
                for u in range(4):
                    slot(s, par, u)

            pipeline(dve, -3, STEPS + 1, body, 3)

        @block.tensor
        def _(pe):
            pe.wait_ge(S["loaded"], 16 * LOADS)
            for c in range(4):
                wait(pe, S["a_scaled"], c - 1)
                for j in range(4):
                    pair, r = 4 * (c // 2) + j, slice(64 * (c % 2), 64 * (c % 2) + 64)
                    ins = nc.tensor.matmul(ps_p[c % 2][:, j * P:(j + 1) * P], wqT[r, pair, :], wkT[r, pair, :],
                                           start=True, stop=True)
                ins.then_inc(S["a_product"], 1)
            pe.wait_ge(S["prep"], 5)
            pe.wait_ge(S["a_split"], 8)
            pe.wait_ge(S["zeroed"], 7)

            def t_fill(s, par, u, i):
                bank, f = ps_p[(u + i) % 2], 4 * s + u + 4
                if i == 0:
                    wait(pe, S["fill_dve"], 2 * f - 1)
                    wait(pe, S["xT_lo"], s + 2)
                else:
                    wait(pe, S["fill_act"], 2 * f)
                    wait(pe, S["fill_dve"], 2 * f)
                for j in range(2):
                    h, out = 4 * u + 2 * i + j, bank[:, j * TOK:(j + 1) * TOK]
                    nc.tensor.matmul(out, a_hi[:, h, :], xT_hi[:, 1 - par, :], start=True, stop=False)
                    nc.tensor.matmul(out, a_lo[:, h, :], xT_hi[:, 1 - par, :], start=False, stop=False)
                    ins = nc.tensor.matmul(out, a_hi[:, h, :], xT_lo[:, 1 - par, :], start=False, stop=True)
                ins.then_inc(S["fill"], 1)

            def v_fill(s, par, u):
                f = 4 * s + u + 4
                wait(pe, S["fill_act"], 2 * f + 1)
                wait(pe, S["ctx_lo"], s + 2)
                cols, tok = slice(512 * (u % 2), 512 * (u % 2) + 512), slice(P * (u // 2), P * (u // 2) + P)
                out = ps_p[u % 2][:, :]
                nc.tensor.matmul(out, ctx_hi[:, 1 - par, tok], wv_hi[:, cols], start=True, stop=False)
                nc.tensor.matmul(out, ctx_lo[:, 1 - par, tok], wv_hi[:, cols], start=False, stop=False)
                nc.tensor.matmul(out, ctx_hi[:, 1 - par, tok], wv_lo[:, cols], start=False, stop=True).then_inc(S["fill"], 1)

            def slot(s, par, u):
                n = 4 * s + u
                tile, hh = u // 2, u % 2
                st = ps_st[u % 2]
                if live(n, 4 * STEPS):
                    wait(pe, S["fill_act"], 8 * (s + 1))
                    wait(pe, S["fill_dve"], 8 * (s + 1))
                    wait(pe, S["exp"], n - 1)
                    nc.tensor.matmul(st[:, :], ident_bf[:, :], mask_bf[:, :], start=True, stop=False, skip_group_check=True)
                    for b in range(2):
                        tok = P * tile + SEQ * b
                        ins = nc.tensor.matmul(st[64 * b:64 * b + 64, :], keys[:, par, tok:tok + SEQ],
                                               t_all[:, par, HALF * hh:HALF * hh + HALF, tok:tok + SEQ],
                                               start=False, stop=True, skip_group_check=True)
                    ins.then_inc(S["scores"], 1)
                if live(n - 2, 4 * STEPS):
                    m = (u - 2) % 4
                    wait(pe, S["normalised"], n - 1)
                    wait(pe, S["max_rows"], cap(n, 4 * STEPS))
                    for b in range(2):
                        for j in range(2):
                            ins = nc.tensor.transpose(ps_x[:, (2 * b + j) * P:(2 * b + j + 1) * P],
                                                      o[:, m % 2, b, 2 * j:2 * j + 2, :].rearrange("p a d -> p (a d)"), ident[:, :])
                    ins.then_inc(S["o_transposed"], 1)
                if u == 0 and live(s + 2, STEPS):
                    wait(pe, S["xn"], s + 3)
                    wait(pe, S["residual"], 2 * s - 1)
                    for t in range(TPS):
                        ins = nc.tensor.transpose(ps_m[:, t * P:(t + 1) * P], xn[:, par, t, :], ident[:, :])
                    ins.then_inc(S["transposed"], 1)
                if live(s + 1, STEPS):
                    t_fill(s, par, u, 0)
                if live(n, 4 * STEPS):
                    wait(pe, S["raw_copied"], n + 1)
                    wait(pe, S["o_copied"], n - 1)
                    for a in range(4):
                        ins = nc.tensor.transpose(ps_x[:, a * P:(a + 1) * P], raw[:, u % 2, a * P:(a + 1) * P], ident[:, :])
                    ins.then_inc(S["scores_transposed"], 1)
                if live(n - 1, 4 * STEPS):
                    m, owner = (u - 1) % 4, par if u else 1 - par
                    wait(pe, S["exp"], n)
                    wait(pe, S["normalised"], n - 1)
                    for a in range(4):
                        for h2 in range(2):
                            h = 2 * a + h2
                            ins = nc.tensor.matmul(ps_pv[a // 2][64 * h2:64 * h2 + 64, (a % 2) * 2 * VW:(a % 2 + 1) * 2 * VW],
                                                   probs[:, m % 2, h, :],
                                                   v_bd[:, owner, m // 2, HALF * (m % 2) + h, :, :].rearrange("p b d -> p (b d)"),
                                                   start=True, stop=True)
                    ins.then_inc(S["pv_product"], 1)
                if live(s + 1, STEPS):
                    t_fill(s, par, u, 1)
                if live(n, 4 * STEPS):
                    wait(pe, S["max"], n + 1)
                    for a in range(4):
                        ins = nc.tensor.transpose(ps_x[0:2, a * P:(a + 1) * P], neg_max[:, u % 2, a, :], ident[:, :])
                    ins.then_inc(S["max_transposed"], 1)
                if live(s + 1, STEPS):
                    v_fill(s, par, u)
                done = {1: TPS * (s - 1) + 1, 3: TPS * s}.get(u)
                if done is not None and live(done, TILES):
                    wait(pe, S["o_copied"], 2 * done + 2)
                    wait(pe, S["xT_lo"], cap(s + 3, STEPS) if u == 1 else 0)
                    wait(pe, S["residual"], done)
                    t = int(u == 1)
                    for c in range(8):
                        ins = nc.tensor.matmul(ps_m[:, 0:P],
                                               oT[:, t, c // 4, c // 2 % 2, c % 2, :, :].rearrange("p b q -> p (b q)"),
                                               wo[:, c, :], start=(c == 0), stop=(c == 7))
                    ins.then_inc(S["out_product"], 1)
                if live(n, 4 * STEPS):
                    wait(pe, S["max_rows"], n + 1)
                    nc.tensor.matmul(st[:, :], pick[:, :], rows[:, u % 2, :], start=False, stop=True,
                                     skip_group_check=True).then_inc(S["shifted"], 1)

            def body(s, par):
                for u in range(4):
                    slot(s, par, u)

            pipeline(pe, -2, STEPS + 1, body)


E, HID = 8, 512
CH = HID // P
GROUP = 4


def router(nc, x_sb, xT_hi, xT_lo, gates, w, sem, sb, pb):
    f32 = lambda name, *shape: sb("ro_" + name, [P, *shape], FP32)
    wg, bg, rank = f32("wg", P), f32("bg", TILES, E), f32("rank", TILES, E)
    ident, half, eps = f32("ident", P), f32("half", TPS), f32("eps", TPS)
    stats, mean_var = f32("stats", 2, TPS, 6), f32("mean_var", 2, TPS, 2)
    var_eps, rstd, xn = f32("var_eps", TPS), f32("rstd", 2, TPS), f32("xn", 2, TPS, P)
    xT = f32("xT", 2, TOK)
    logits, prob, left, first, mask = (f32(n, TILES, E) for n in ("logits", "prob", "left", "first", "mask"))
    row = f32("row", TILES)
    ps_t, ps_l = [pb("t0"), pb("t1")], [pb("l0"), pb("l1")]
    names = ("loaded half stats mean_var var_eps rstd xn transposed xT_copied xT_hi xT_lo logits logits_copied chain "
             "shifted exp").split()
    S = {n: sem("ro_" + n) for n in names}
    LOADS = 4
    tile_of_x = lambda t: x_sb[:, bass.ds(t, 1), :].rearrange("p a n -> p (a n)")

    with nc.Block() as block:

        @block.sync
        def _(sp):
            for dst, src in ((wg[:, :], w["ff_wg"]), (bg[:, :, :], w["ff_bg"]), (rank[:, :, :], w["ff_rank"]),
                             (ident[:, :], w["ident"])):
                sp.dma_start(dst, src).then_inc(S["loaded"], 16)

        @block.gpsimd
        def _(pool):
            nc.gpsimd.memset(half[:, :], -0.5).then_inc(S["half"], 1)
            nc.gpsimd.memset(eps[:, :], EPS).then_inc(S["half"], 1)
            pool.wait_ge(S["half"], 2)

            def body(s, par):
                if live(s + 1, STEPS):
                    wait(pool, S["mean_var"], s + 2)
                    wait(pool, S["rstd"], s + 1)
                    nc.gpsimd.tensor_tensor(var_eps[:, :], mean_var[:, 1 - par, :, 1], eps[:, :], ALU.add)\
                      .then_inc(S["var_eps"], 1)
                    pool.wait_ge(S["var_eps"], s + 2)
                    nc.gpsimd.tensor_tensor(rstd[:, 1 - par, :], var_eps[:, :], half[:, :], ALU.pow).then_inc(S["rstd"], 1)

            pipeline(pool, -1, STEPS, body)

        @block.scalar
        def _(act):
            def body(s, par):
                if live(s, STEPS):
                    wait(act, S["transposed"], s + 1)
                    wait(act, S["logits"], s - 1)
                    nc.scalar.copy(xT[:, par, :], ps_t[par][:, 0:TOK]).then_inc(S["xT_copied"], 1)
                    nc.scalar.copy(xT_hi[:, bass.ds(TOK * s, TOK)], ps_t[par][:, 0:TOK]).then_inc(S["xT_hi"], 1)
                if live(s - 1, STEPS):
                    wait(act, S["logits"], s)
                    nc.scalar.copy(logits[:, bass.ds(TPS * (s - 1), TPS), :],
                                   ps_l[1 - par][:, 0:TPS * P].rearrange("p (t n) -> p t n", t=TPS)[:, :, 0:E])\
                      .then_inc(S["logits_copied"], 1)

            pipeline(act, 0, STEPS + 1, body)
            act.wait_ge(S["shifted"], 1)
            nc.scalar.activation(prob[:, :, :].rearrange("p t e -> p (t e)"), left[:, :, :].rearrange("p t e -> p (t e)"),
                                 ACT.Exp).then_inc(S["exp"], 1)

        @block.vector
        def _(dve):
            def body(s, par):
                if live(s + 2, STEPS):
                    for t in range(TPS):
                        ins = nc.vector.bn_stats(stats[:, par, t, :], tile_of_x(TPS * (s + 2) + t))
                    ins.then_inc(S["stats"], 1)
                    dve.wait_ge(S["stats"], s + 3)
                if live(s + 1, STEPS):
                    wait(dve, S["rstd"], s + 2)
                    wait(dve, S["transposed"], s)
                    for t in range(TPS):
                        ins = nc.vector.tensor_scalar(xn[:, 1 - par, t, :], tile_of_x(TPS * (s + 1) + t),
                                                      mean_var[:, 1 - par, t, 0:1], rstd[:, 1 - par, t:t + 1],
                                                      ALU.subtract, ALU.mult)
                    ins.then_inc(S["xn"], 1)
                if live(s + 2, STEPS):
                    for t in range(TPS):
                        ins = nc.vector.bn_aggr(mean_var[:, par, t, :], stats[:, par, t, :])
                    ins.then_inc(S["mean_var"], 1)
                if live(s, STEPS):
                    wait(dve, S["xT_hi"], s + 1)
                    hi = xT_hi[:, bass.ds(TOK * s, TOK)]
                    nc.vector.tensor_tensor(xT_lo[:, bass.ds(TOK * s, TOK)], xT[:, par, :], hi.bitcast(FP32),
                                            ALU.subtract).then_inc(S["xT_lo"], 1)

            pipeline(dve, -2, STEPS, body)

            chain = [0]

            def step(ins):
                chain[0] += 1
                ins.then_inc(S["chain"], 1)
                dve.wait_ge(S["chain"], chain[0])

            wide = lambda t: t[:, :].unsqueeze(2).broadcast_to([P, TILES, E])
            dve.wait_ge(S["logits_copied"], STEPS)
            dve.wait_ge(S["loaded"], 16 * LOADS)
            tt = nc.vector.tensor_tensor
            step(tt(logits[:, :, :], logits[:, :, :], bg[:, :, :], ALU.add))
            step(nc.vector.tensor_reduce(row[:, :], logits[:, :, :], axis=AX.X, op=ALU.max))
            tt(left[:, :, :], logits[:, :, :], wide(row), ALU.subtract).then_inc(S["shifted"], 1)
            dve.wait_ge(S["exp"], 1)
            step(nc.vector.tensor_reduce(row[:, :], prob[:, :, :], axis=AX.X, op=ALU.add))
            step(nc.vector.reciprocal(row[:, :], row[:, :]))
            step(tt(prob[:, :, :], prob[:, :, :], wide(row), ALU.mult))
            step(nc.vector.tensor_copy(left[:, :, :], prob[:, :, :]))
            for k in range(2):
                step(nc.vector.tensor_reduce(row[:, :], left[:, :, :], axis=AX.X, op=ALU.max))
                step(tt(first[:, :, :], left[:, :, :], wide(row), ALU.is_equal))
                step(tt(first[:, :, :], first[:, :, :], rank[:, :, :], ALU.mult))
                step(nc.vector.tensor_reduce(row[:, :], first[:, :, :], axis=AX.X, op=ALU.max))
                step(tt(first[:, :, :], first[:, :, :], wide(row), ALU.is_equal))
                if k == 0:
                    step(nc.vector.scalar_tensor_tensor(left[:, :, :], first[:, :, :], -2.0, left[:, :, :], ALU.mult, ALU.add))
                    step(nc.vector.tensor_copy(mask[:, :, :], first[:, :, :]))
                else:
                    step(tt(mask[:, :, :], mask[:, :, :], first[:, :, :], ALU.add))
            step(tt(prob[:, :, :], prob[:, :, :], mask[:, :, :], ALU.mult))
            step(nc.vector.tensor_reduce(row[:, :], prob[:, :, :], axis=AX.X, op=ALU.add))
            step(nc.vector.tensor_scalar(row[:, :], row[:, :], 1e-8, None, ALU.add))
            step(nc.vector.reciprocal(row[:, :], row[:, :]))
            step(tt(gates[:, :, :], prob[:, :, :], wide(row), ALU.mult))

        @block.tensor
        def _(pe):
            pe.wait_ge(S["loaded"], 16 * LOADS)

            def body(s, par):
                if live(s + 1, STEPS):
                    wait(pe, S["xn"], s + 2)
                    wait(pe, S["xT_hi"], s)
                    for t in range(TPS):
                        ins = nc.tensor.transpose(ps_t[1 - par][:, t * P:(t + 1) * P], xn[:, 1 - par, t, :], ident[:, :])
                    ins.then_inc(S["transposed"], 1)
                if live(s, STEPS):
                    wait(pe, S["xT_copied"], s + 1)
                    wait(pe, S["logits_copied"], s - 1)
                    for t in range(TPS):
                        ins = nc.tensor.matmul(ps_l[par][:, t * P:(t + 1) * P], xT[:, par, t * P:(t + 1) * P], wg[:, :],
                                               start=True, stop=True)
                    ins.then_inc(S["logits"], 1)

            pipeline(pe, -1, STEPS, body)


def experts(nc, x_sb, xT_hi, xT_lo, gates, w, sem, sb, pb):
    f32 = lambda name, *shape: sb("ff_" + name, [P, *shape], FP32)
    f32r = lambda name, *shape: sb("ff_" + name, [P, *shape], FP32R)
    w1_hi, w1_lo, w1_raw = f32r("w1_hi", E, HID), f32r("w1_lo", E, HID), f32("w1_raw", 2, HID)
    w2, b1, b2 = f32("w2", E, CH, P), f32("b1", E, CH), f32("b2", P)
    ident = f32("ident", P)
    hT = f32("hT", 2, CH, GROUP * P)
    gT = f32("gT", GROUP * P)
    ps_h = [pb(f"h{i}") for i in range(4)]
    ps_o = [pb("o0"), pb("o1")]
    ps_g = pb("g")
    GROUPS = TILES // GROUP
    g_now = f32("g_now", GROUP, E)
    names = "g_now w_loaded gelu hidden out summed gT_product gT_copied w1_hi w1_lo".split()
    S = {n: sem("ff_" + n) for n in names}
    s_w1 = [sem(f"ff_w1_{e}") for e in range(2)]

    with nc.Block() as block:

        @block.sync
        def _(sp):
            for e in range(E):
                wait(sp, S["w1_lo"], e - 1)
                sp.dma_start(w1_raw[:, e % 2, :], w["ff_w1"][:, e, :]).then_inc(s_w1[e % 2], 16)
                if e == 0:
                    for dst, src in ((w2[:, :, :, :], w["ff_w2"]), (b1[:, :, :], w["ff_b1"]), (b2[0:E, :], w["ff_b2"]),
                                     (ident[:, :], w["ident"])):
                        sp.dma_start(dst, src).then_inc(S["w_loaded"], 16)

        @block.scalar
        def _(act):
            act.wait_ge(S["w_loaded"], 64)

            def body(g):
                act.wait_ge(S["gT_product"], g + 1)
                nc.scalar.copy(gT[0:E, :], ps_g[0:E, :]).then_inc(S["gT_copied"], 1)
                for e in range(E):
                    v = E * g + e
                    for c in range(CH):
                        act.wait_ge(S["hidden"], CH * v + c + 1)
                        wait(act, S["out"], 9 * g + e - (e < 2))
                        nc.scalar.activation(hT[:, e % 2, c, :], ps_h[c][:, :], ACT.Gelu_apprx_tanh,
                                             bias=b1[:, e, c:c + 1]).then_inc(S["gelu"], 1)

            body(0)
            with act.Fori(1, GROUPS) as g:
                body(g)

        @block.vector
        def _(dve):
            for e in range(E):
                dve.wait_ge(s_w1[e % 2], 16 * (e // 2 + 1))
                nc.vector.tensor_copy(w1_hi[:, e, :], w1_raw[:, e % 2, :]).then_inc(S["w1_hi"], 1)
                dve.wait_ge(S["w1_hi"], e + 1)
                nc.vector.tensor_tensor(w1_lo[:, e, :], w1_raw[:, e % 2, :], w1_hi[:, e, :].bitcast(FP32),
                                        ALU.subtract).then_inc(S["w1_lo"], 1)

            def gates_now(g):
                wait(dve, S["gT_product"], g)
                nc.vector.tensor_scalar(g_now[:, :, :], gates[:, bass.ds(GROUP * g, GROUP), :], 1.0, None, ALU.mult)\
                  .then_inc(S["g_now"], 1)

            def body(g):
                for k in range(E + 1):
                    dve.wait_ge(S["out"], (E + 1) * g + k + 1)
                    if k:
                        dve.wait_ge(S["summed"], (E + 1) * g + k)
                    bank = ps_o[k % 2] if k < E else ps_o[0]
                    for t in range(GROUP):
                        row = x_sb[:, bass.ds(GROUP * g + t, 1), :].rearrange("p a n -> p (a n)")
                        acc = bank[:, t * P:(t + 1) * P]
                        if k == 0:
                            ins = nc.vector.tensor_tensor(row, acc, row, ALU.add)
                        else:
                            gate = gates[:, bass.ds(GROUP * g + t, 1), k - 1:k].rearrange("p a n -> p (a n)")
                            ins = nc.vector.scalar_tensor_tensor(row, acc, gate, row, ALU.mult, ALU.add)
                    ins.then_inc(S["summed"], 1)
                    if k == 4 and live(g + 1, GROUPS):
                        gates_now(g + 1)

            gates_now(0)
            with dve.Fori(0, GROUPS - 1) as g:
                body(g)
            body(GROUPS - 1)

        @block.tensor
        def _(pe):
            pe.wait_ge(S["w_loaded"], 64)

            def hidden(g, e):
                v = E * g + e
                tok = bass.ds(GROUP * P * g, GROUP * P)
                for c in range(CH):
                    wait(pe, S["gelu"], CH * (v - 1) + c + 1)
                    cols = slice(c * P, (c + 1) * P)
                    nc.tensor.matmul(ps_h[c][:, :], w1_hi[:, e, cols], xT_hi[:, tok], start=True, stop=False)
                    nc.tensor.matmul(ps_h[c][:, :], w1_lo[:, e, cols], xT_hi[:, tok], start=False, stop=False)
                    nc.tensor.matmul(ps_h[c][:, :], w1_hi[:, e, cols], xT_lo[:, tok], start=False, stop=True)\
                      .then_inc(S["hidden"], 1)

            def output(g, e):
                k = e + 1
                bank = ps_o[k % 2] if k < E else ps_o[0]
                wait(pe, S["summed"], (E + 1) * g + k - 1)
                for t in range(GROUP):
                    for c in range(CH):
                        wait(pe, S["gelu"], CH * (E * g + e) + c + 1)
                        ins = nc.tensor.matmul(bank[:, t * P:(t + 1) * P], hT[:, e % 2, c, t * P:(t + 1) * P],
                                               w2[:, e, c, :], start=(c == 0), stop=(c == CH - 1))
                ins.then_inc(S["out"], 1)

            def biases(g):
                wait(pe, S["gT_copied"], g + 1)
                wait(pe, S["summed"], (E + 1) * g)
                for t in range(GROUP):
                    ins = nc.tensor.matmul(ps_o[0][:, t * P:(t + 1) * P], gT[0:E, t * P:(t + 1) * P], b2[0:E, :],
                                           start=True, stop=True)
                ins.then_inc(S["out"], 1)

            def body(g):
                pe.wait_ge(S["g_now"], g + 1)
                wait(pe, S["gT_copied"], g)
                for t in range(GROUP):
                    ins = nc.tensor.transpose(ps_g[0:E, t * P:(t + 1) * P],
                                              g_now[:, t, :], ident[:, :])
                ins.then_inc(S["gT_product"], 1)
                for e in range(E):
                    if isinstance(g, int) and g == 0:
                        pe.wait_ge(S["w1_lo"], e + 1)
                    hidden(g, e)
                    if e == 0:
                        biases(g)
                    else:
                        output(g, e - 1)
                output(g, E - 1)

            body(0)
            with pe.Fori(1, GROUPS) as g:
                body(g)


def decoder(nc, x, w, out, phases=3):
    with ExitStack() as ctx:
        x_sb = ctx.enter_context(nc.sbuf_tensor("x_sb", [P, TILES, D], FP32))
        x_loaded = [ctx.enter_context(nc.semaphore(f"x_loaded_{s}")) for s in X_PARTS]
        x_dram = x.rearrange("b s d -> (b s) d").rearrange("(t p) d -> p t d", p=P)
        out_dram = out.rearrange("b s d -> (b s) d").rearrange("(t p) d -> p t d", p=P)
        with nc.Block() as block:
            @block.scalar
            def _(act):
                for s, end, loaded in zip(X_PARTS, X_PARTS[1:] + [STEPS], x_loaded):
                    act.dma_start(x_sb[:, TPS * s:TPS * end, :], x_dram[:, TPS * s:TPS * end, :]).then_inc(loaded, 16)
        with ExitStack() as inner:
            sem = lambda name: inner.enter_context(nc.semaphore(name))
            sb = lambda name, shape, dt: inner.enter_context(nc.sbuf_tensor(name, shape, dt))
            pb = lambda name: inner.enter_context(nc.psum_tensor("sa_" + name, [P, 512], FP32))
            self_attention(nc, x_sb, x_loaded, w, sem, sb, pb)
        with ExitStack() as inner:
            sem = lambda name: inner.enter_context(nc.semaphore(name))
            sb = lambda name, shape, dt: inner.enter_context(nc.sbuf_tensor(name, shape, dt))
            pb = lambda name: inner.enter_context(nc.psum_tensor("ca_" + name, [P, 512], FP32))
            cross_attention(nc, x_sb, w, sem, sb, pb)
        xT_hi = ctx.enter_context(nc.sbuf_tensor("xT_hi", [P, TILES * P], FP32R))
        xT_lo = ctx.enter_context(nc.sbuf_tensor("xT_lo", [P, TILES * P], FP32R))
        gates = ctx.enter_context(nc.sbuf_tensor("gates", [P, TILES, E], FP32))
        for part, name in ((router, "ro_"), (experts, "ff_")):
            with ExitStack() as inner:
                sem = lambda name: inner.enter_context(nc.semaphore(name))
                sb = lambda name, shape, dt: inner.enter_context(nc.sbuf_tensor(name, shape, dt))
                pb = lambda n: inner.enter_context(nc.psum_tensor(name + n, [P, 512], FP32))
                part(nc, x_sb, xT_hi, xT_lo, gates, w, sem, sb, pb)
        stored = ctx.enter_context(nc.semaphore("out_stored"))
        with nc.Block() as block:
            @block.sync
            def _(sp):
                sp.dma_start(out_dram, x_sb[:, :, :]).then_inc(stored, 16)
                sp.wait_ge(stored, 16)


def laid_out(inputs):
    import numpy as np
    import math
    f = np.float32
    arrays = {}
    wq, wk, wv, wo = (np.asarray(inputs[f"L0_attn_{n}"]) for n in ("Wq", "Wk", "Wv", "Wo"))
    q = np.zeros((D, HG, 4, G1, HD1), f)
    q[:, :, 0:3] = wq.reshape(D, G1, HG, HD1).transpose(0, 2, 1, 3)[:, :, None]
    arrays["sa_wq"] = q.reshape(D, HG * P)
    k = np.zeros((D, G1, 4, G1, HD1), f)
    for g in range(G1):
        k[:, g, 0:3, g] = wk.reshape(D, G1, HD1)[:, None, g]
    arrays["sa_wk"] = k.reshape(D, G1 * P)
    v = np.zeros((D, P), f)
    v[:, 0:32] = wv
    arrays["sa_wv"] = v
    arrays["sa_wo"] = np.ascontiguousarray(wo.reshape(G1, HG, HD1, D).transpose(1, 0, 2, 3).reshape(P, D))
    arrays["ident"] = np.eye(P, dtype=f)
    start = 2.0 ** (-2.0 ** (-(math.log2(H1) - 3)))
    slopes = np.array([start * start ** i for i in range(H1)], dtype=f).reshape(G1, HG)
    high = (slopes.view(np.uint32) & np.uint32(0xFFFFF000)).view(f)
    parts = np.stack([high, slopes - high], 1)
    q_rows = np.zeros((P, STEP, HG, SEQ), f)
    q_rows[ALIBI_ROW:ALIBI_ROW + 2 * G1] = parts.reshape(2 * G1, 1, HG, 1)
    k_rows = np.zeros((P, STEP, G1, SEQ), f)
    z = np.zeros((2, SEQ, 2, 2, P), f)
    ones = np.zeros((2, SEQ, 2, G1, HD1), f)
    for g in range(G1):
        k_rows[MAX_ROW + g, :, g] = 1.0
        k_rows[ALIBI_ROW + 2 * g:ALIBI_ROW + 2 * g + 2, :, g] = np.arange(SEQ, dtype=f)
        ones[g % 2, :, g // 2, g] = 1.0
        for part in range(2):
            z[:, :, :, :, ALIBI_ROW + 2 * g + part] = parts[g, part].reshape(2, 2).T[:, None, None, :]
    arrays["sa_q_rows"], arrays["sa_k_rows"] = q_rows.reshape(P, -1), k_rows.reshape(P, -1)
    arrays["sa_z"], arrays["sa_ones"] = z.reshape(P, 2, 2, P), ones.reshape(P, 2, 32)
    wq, wk, wv, wo = (np.asarray(inputs[f"L0_xattn_{n}"]) for n in ("Wq", "Wk", "Wv", "Wo"))
    for name, a in (("ca_wqT", wq), ("ca_wkT", wk)):
        arrays[name] = a.reshape(H2 // 2, 2, D, HD2).transpose(1, 3, 0, 2).reshape(P, H2 // 2, D)
    arrays["ca_wv"] = wv.transpose(1, 0, 2).reshape(D, H2 * HD2)
    arrays["ca_wo"] = wo.reshape(2, 2, 2, 2, HD2, D).transpose(2, 4, 0, 1, 3, 5).reshape(P, 8, D)
    key, query = np.arange(P)[:, None] % SEQ, np.arange(HALF * SEQ)[None] % SEQ
    arrays["ca_mask"] = np.where(key > query, f(-1e30), f(0))
    pick = np.zeros((P, P), f)
    pick[0, 0:SEQ] = pick[1, SEQ:P] = 1.0
    arrays["ca_pick"] = pick
    arrays["ctxT"] = np.asarray(inputs["ctx_1024"]).reshape(BATCH * SEQ, D).T
    wg = np.zeros((D, P), f)
    wg[:, 0:E] = inputs["L0_ffn_Wg"]
    arrays["ff_wg"] = wg
    arrays["ff_bg"] = np.broadcast_to(np.asarray(inputs["L0_ffn_bg"]), (P, TILES, E))
    arrays["ff_rank"] = np.broadcast_to(np.arange(E, 0, -1, dtype=f), (P, TILES, E))
    arrays["ff_w1"] = np.asarray(inputs["L0_ffn_W1"]).transpose(1, 0, 2)
    arrays["ff_w2"] = np.asarray(inputs["L0_ffn_W2"]).reshape(E, CH, P, D).transpose(2, 0, 1, 3)
    arrays["ff_b1"] = np.asarray(inputs["L0_ffn_b1"]).reshape(E, CH, P).transpose(2, 0, 1)
    arrays["ff_b2"] = np.asarray(inputs["L0_ffn_b2"])
    return arrays


def kernel(**inputs):
    import numpy as _np
    import concourse.bacc as _bacc
    from concourse import mybir as _mybir
    from concourse.bass_utils import run_bass_kernel_spmd as _run

    nc = _bacc.Bacc("TRN2", target_bir_lowering=False, num_devices=1)
    arrays = {"in_x": _np.ascontiguousarray(inputs["x"])}
    arrays.update((f"in_{n}", _np.ascontiguousarray(a)) for n, a in laid_out(inputs).items())
    aps = {n: nc.dram_tensor(n, a.shape, _mybir.dt.from_np(a.dtype), kind="ExternalInput").ap() for n, a in arrays.items()}
    out = nc.dram_tensor("out_x", (BATCH, SEQ, D), FP32, kind="ExternalOutput").ap()
    decoder(nc, aps.pop("in_x"), {n[3:]: a for n, a in aps.items()}, out)
    r = _run(nc, [arrays], core_ids=[0])
    return r.results[0]["out_x"]
```

```python
import concourse.bass as bass
from concourse import mybir
from contextlib import ExitStack

FP32 = mybir.dt.float32
FP32R = mybir.dt.float32r
BF16 = mybir.dt.bfloat16
ALU = mybir.AluOpType
ACT = mybir.ActivationFunctionType
AX = mybir.AxisListType

P = 128
BATCH, SEQ, D = 64, 64, 128
STEP = 4
TOK = STEP * SEQ
TPS = TOK // P
STEPS = BATCH // STEP
TILES = BATCH * SEQ // P
EPS = 1e-5
X_PARTS = [0, 1, 2, 3]

H1, G1, HD1 = 16, 4, 8
HG = H1 // G1
MAX_ROW, ALIBI_ROW = 96, 100


E, HID = 8, 512
CH = HID // P
TOPK = 2
ROWS = 2 * P
REGION = BATCH * SEQ + ROWS
RUNS = (TOPK * BATCH * SEQ + E * (ROWS - 1)) // ROWS
FULL = BATCH * SEQ // ROWS
META = D
WIDTH = D + 2


def live(i, n):
    return not isinstance(i, int) or 0 <= i < n


def wait(eng, sem, value):
    if not isinstance(value, int) or value > 0:
        eng.wait_ge(sem, value)


def cap(count, n):
    return min(count, n) if isinstance(count, int) else count


def pipeline(eng, first, last, body, ahead=2, behind=2, steps=STEPS, unroll=2):
    lo = -(-behind // unroll) * unroll
    hi = (steps - ahead) // unroll * unroll
    for s in range(first, lo):
        body(s, s % unroll)
    with eng.Fori(lo // unroll, hi // unroll) as turn:
        for n in range(unroll):
            body(unroll * turn + n, n)
    for s in range(hi, last):
        body(s, s % unroll)


def self_attention(nc, x_sb, x_loaded, w, sem, sb, pb):
    f32 = lambda name, *shape: sb(name, [P, *shape], FP32)
    f32r = lambda name, *shape: sb(name, [P, *shape], FP32R)

    wq_raw, wk_raw = f32("sa_wq_raw", HG * P), f32("sa_wk_raw", G1 * P)
    wq_hi, wq_lo = f32r("sa_wq_hi", HG, P), f32r("sa_wq_lo", HG, P)
    wk_hi, wk_lo = f32r("sa_wk_hi", G1, P), f32r("sa_wk_lo", G1, P)
    wv, wo = f32("sa_wv", P), f32("sa_wo", P)
    ident, ones_gd = f32("sa_ident", P), f32("sa_ones", 2, 32)
    q_rows, k_rows = f32("sa_q_rows", STEP * HG * SEQ), f32("sa_k_rows", STEP * G1 * SEQ)
    half, eps = f32("sa_half", TPS), f32("sa_eps", TPS)
    zeros = f32("sa_zeros", STEP * HG * SEQ)
    stats, mean_var = f32("sa_stats", 2, TPS, 6), f32("sa_mean_var", 2, TPS, 2)
    var_eps, rstd = f32("sa_var_eps", TPS), f32("sa_rstd", 2, TPS)
    xn = f32("sa_xn", 2, TPS, P)
    xT, xT_hi, xT_lo = f32("sa_xT", 2, TOK), f32r("sa_xT_hi", 2, TOK), f32r("sa_xT_lo", 2, TOK)
    q_st = f32r("sa_q_st", 2, STEP, HG, SEQ)
    k_st = f32r("sa_k_st", 2, STEP, G1, SEQ)
    v_bd = f32("sa_v_bd", 2, STEP, 96)
    z = f32("sa_z", 2, 2, P)
    probs = f32("sa_probs", 2, 2, HG * SEQ)
    recip, att = f32("sa_recip", HG * SEQ), f32("sa_att", 2, HG, SEQ)
    attT = f32("sa_attT", 2, TOK)

    ps_t = pb("ps_t")
    ps_proj = [pb("ps_proj0"), pb("ps_proj1")]
    ps_s, ps_z, ps_st = pb("ps_s"), pb("ps_z"), pb("ps_st")
    ps_pv = [pb("ps_pv0"), pb("ps_pv1")]

    s_wload = sem("sa_weights_loaded")
    s_prep = sem("sa_weights_split")
    s_zero = sem("sa_zeroed")
    s_stats, s_aggr = sem("sa_stats_done"), sem("sa_mean_var_done")
    s_vare, s_rstd, s_xn = sem("sa_var_eps_done"), sem("sa_rstd_done"), sem("sa_xn_done")
    s_T, s_V, s_proj = sem("sa_transposed"), sem("sa_v_product"), sem("sa_qk_product")
    s_xTf, s_xThi, s_xTlo = sem("sa_xT_copied"), sem("sa_xT_hi_done"), sem("sa_xT_lo_done")
    s_vbd = sem("sa_v_placed")
    s_hi, s_lo = sem("sa_qk_hi_done"), sem("sa_qk_lo_done")
    s_S, s_max, s_Z, s_rows = sem("sa_scores"), sem("sa_max"), sem("sa_max_transposed"), sem("sa_max_rows")
    s_ST, s_exp, s_PV = sem("sa_scoresT"), sem("sa_exp_done"), sem("sa_pv_product")
    s_rec, s_att = sem("sa_reciprocal"), sem("sa_normalised")
    s_move = [sem("sa_att_moved_even"), sem("sa_att_moved_odd")]
    s_out = [sem("sa_att_out_even"), sem("sa_att_out_odd")]
    moved = lambda s, par: 8 * (s - par) + 16
    by_batch, by_head = [], []
    for n in ("even", "odd"):
        scratch = nc.dram_tensor(f"sa_scratch_{n}", (HG, 32, STEP, SEQ), FP32).ap()
        by_batch.append(scratch.rearrange("h r b q -> r h b q"))
        by_head.append(scratch.rearrange("h r b q -> (h r) (b q)"))
    s_Wo, s_res, s_reset = sem("sa_out_product"), sem("sa_residual"), sem("sa_max_rows_reset")

    LOADS = 9

    with nc.Block() as block:

        @block.sync
        def _(sp):
            for dst, src in ((wq_raw[:, :], w["sa_wq"]), (wk_raw[:, :], w["sa_wk"]), (wv[:, :], w["sa_wv"]),
                             (ident[:, :], w["ident"]), (z[:, :, :, :], w["sa_z"]),
                             (q_rows[:, :], w["sa_q_rows"]), (k_rows[:, :], w["sa_k_rows"]),
                             (ones_gd[:, :, :], w["sa_ones"]), (wo[:, :], w["sa_wo"])):
                sp.dma_start(dst, src).then_inc(s_wload, 16)

            def body(s, par):
                if live(s - 1, STEPS):
                    wait(sp, s_att, s)
                    for b in range(STEP):
                        sp.dma_start(by_batch[1 - par][:, :, b, :], att[32 * b:32 * b + 32, 1 - par, :, :])\
                          .then_inc(s_out[1 - par], 16)
                    wait(sp, s_out[1 - par], STEP * moved(s - 1, 1 - par))
                    sp.dma_start(attT[:, 1 - par, :], by_head[1 - par]).then_inc(s_move[1 - par], 16)

            pipeline(sp, 1, STEPS + 1, body)

        @block.gpsimd
        def _(pool):
            nc.gpsimd.memset(half[:, :], -0.5).then_inc(s_zero, 1)
            nc.gpsimd.memset(v_bd[:, :, :, :], 0.0).then_inc(s_zero, 1)
            nc.gpsimd.memset(eps[:, :], EPS).then_inc(s_zero, 1)
            nc.gpsimd.memset(zeros[:, :], 0.0).then_inc(s_zero, 1)
            pool.wait_ge(s_zero, 4)

            def body(s, par):
                if live(s + 2, STEPS):
                    wait(pool, s_aggr, s + 3)
                    wait(pool, s_rstd, s + 2)
                    wait(pool, s_reset, s - 1)
                    nc.gpsimd.tensor_tensor(var_eps[:, :], mean_var[:, par, :, 1], eps[:, :], ALU.add).then_inc(s_vare, 1)
                    pool.wait_ge(s_vare, s + 3)
                    nc.gpsimd.tensor_tensor(rstd[:, par, :], var_eps[:, :], half[:, :], ALU.pow).then_inc(s_rstd, 1)
                if live(s - 1, STEPS) and live(s + 1, STEPS):
                    wait(pool, s_ST, STEP * s)
                    if live(s + 2, STEPS):
                        wait(pool, s_rstd, s + 3)
                    wait(pool, s_reset, s - 1)
                    nothing = zeros[MAX_ROW:ALIBI_ROW, :]
                    nc.gpsimd.tensor_tensor(q_st[MAX_ROW:ALIBI_ROW, 1 - par, :, :, :].rearrange("p b h q -> p (b h q)"),
                                            nothing, nothing, ALU.add).then_inc(s_reset, 1)

            pipeline(pool, -2, STEPS, body)

        @block.scalar
        def _(act):
            act.wait_ge(s_wload, 16 * LOADS)
            for par in range(2):
                nc.scalar.copy(q_st[MAX_ROW:P, par, :, :, :].rearrange("p b h q -> p (b h q)"),
                               q_rows[MAX_ROW:P, :]).then_inc(s_prep, 1)
                nc.scalar.copy(k_st[MAX_ROW:P, par, :, :, :].rearrange("p b h q -> p (b h q)"),
                               k_rows[MAX_ROW:P, :]).then_inc(s_prep, 1)

            def slot(s, par, b):
                n = STEP * s + b
                if live(n - 1, BATCH):
                    buf = par if b else 1 - par
                    wait(act, s_Z, n)
                    nc.scalar.copy(q_st[MAX_ROW:P, buf, (b - 1) % STEP, :, :].rearrange("p h q -> p (h q)"),
                                   ps_z[MAX_ROW:P, 0:256]).then_inc(s_rows, 1)
                if b == 1 and live(s + 1, STEPS):
                    wait(act, s_V, s + 2)
                    if isinstance(s, int) and s == -1:
                        act.wait_ge(s_zero, 4)
                    for g2 in range(2):
                        src = ps_t[64 * g2:64 * g2 + 64, :].rearrange("p (b r) -> p b r", b=STEP)[:, :, 0:32]
                        src = src.rearrange("p b (g c) -> p b g c", g=2)[:, :, :, HD1 * g2:HD1 * g2 + HD1]
                        dst = v_bd[64 * g2:64 * g2 + 64, 1 - par, :, :].rearrange("p b (g c) -> p b g c", g=2)
                        nc.scalar.copy(dst[:, :, :, HD1 * g2:HD1 * g2 + HD1], src).then_inc(s_vbd, 1)
                if b == 2 and live(s + 2, STEPS):
                    wait(act, s_T, s + 3)
                    nc.scalar.copy(xT[:, par, :], ps_t[:, 0:TOK]).then_inc(s_xTf, 1)
                    nc.scalar.copy(xT_hi[:, par, :], ps_t[:, 0:TOK]).then_inc(s_xThi, 1)
                if live(n - 1, BATCH):
                    wait(act, s_ST, n)
                    nc.scalar.activation(probs[:, (b - 1) % 2, :, :].rearrange("p g n -> p (g n)"), ps_st[:, :],
                                         ACT.Exp).then_inc(s_exp, 1)
                if live(s + 1, STEPS):
                    wait(act, s_proj, n + STEP + 1)
                    st = (q_st, k_st)[b // 2]
                    dst = st[0:96, 1 - par, :, 2 * (b % 2):2 * (b % 2) + 2, :].rearrange("p b h q -> p h b q")
                    nc.scalar.copy(dst, ps_proj[b % 2][0:96, :].rearrange("p (h b q) -> p h b q", h=2, b=STEP))\
                      .then_inc(s_hi, 1)

            def body(s, par):
                for b in range(STEP):
                    slot(s, par, b)

            pipeline(act, -2, STEPS + 1, body)

        @block.vector
        def _(dve):
            dve.wait_ge(s_wload, 16 * LOADS)
            for raw, hi, lo, scale in ((wq_raw, wq_hi, wq_lo, HD1 ** -0.5), (wk_raw, wk_hi, wk_lo, 1.0)):
                flat = lambda t: t[:, :, :].rearrange("p a n -> p (a n)")
                nc.vector.tensor_scalar(raw[:, :], raw[:, :], scale, None, ALU.mult).then_inc(s_prep, 1)
                dve.wait_ge(s_prep, 5 if raw is wq_raw else 8)
                nc.vector.tensor_copy(flat(hi), raw[:, :]).then_inc(s_prep, 1)
                dve.wait_ge(s_prep, 6 if raw is wq_raw else 9)
                nc.vector.tensor_tensor(flat(lo), raw[:, :], flat(hi).bitcast(FP32), ALU.subtract).then_inc(s_prep, 1)

            def slot(s, par, b):
                n = STEP * s + b
                u = n + STEP - 1
                if b == 1 and live(s + 2, STEPS):
                    dve.wait_ge(s_stats, s + 3)
                if live(u, STEP * STEPS):
                    st, rows = ((q_st, 64), (q_st, 64), (k_st, 32), (k_st, 32))[(b - 1) % STEP]
                    buf = 1 - par if b else par
                    j = (b - 1) % 2
                    wait(dve, s_hi, u + 1)
                    dst = st[rows:rows + 32, buf, :, 2 * j:2 * j + 2, :].rearrange("p b h q -> p h b q")
                    nc.vector.tensor_tensor(dst, ps_proj[j][rows:rows + 32, :].rearrange("p (h b q) -> p h b q", h=2, b=STEP),
                                            dst.bitcast(FP32), ALU.subtract).then_inc(s_lo, 1)
                if b == 1 and live(s + 2, STEPS):
                    for t in range(TPS):
                        ins = nc.vector.bn_aggr(mean_var[:, par, t, :], stats[:, par, t, :])
                    ins.then_inc(s_aggr, 1)
                if live(n, BATCH):
                    wait(dve, s_S, n + 1)
                    nc.vector.tensor_reduce(z[:, b % 2, :, MAX_ROW:MAX_ROW + G1],
                                            ps_s[:, :].rearrange("p (a g k) -> p a g k", a=2, g=G1),
                                            axis=AX.X, op=ALU.max, negate=True).then_inc(s_max, 1)
                if b == 0 and live(s + 2, STEPS):
                    if isinstance(s, int) and s + 2 in X_PARTS:
                        dve.wait_ge(x_loaded[X_PARTS.index(s + 2)], 16)
                    for t in range(TPS):
                        ins = nc.vector.bn_stats(stats[:, par, t, :], x_sb[:, bass.ds(TPS * (s + 2) + t, 1), :].rearrange("p a n -> p (a n)"))
                    ins.then_inc(s_stats, 1)
                if b == 0 and live(s - 2, STEPS):
                    wait(dve, s_Wo, s - 1)
                    rows = x_sb[:, bass.ds(TPS * (s - 2), TPS), :]
                    nc.vector.tensor_tensor(rows, ps_t[:, 0:TOK].rearrange("p (t n) -> p t n", t=TPS), rows, ALU.add)\
                      .then_inc(s_res, 1)
                if b == 2 and live(s + 2, STEPS):
                    wait(dve, s_rstd, s + 3)
                    for t in range(TPS):
                        ins = nc.vector.tensor_scalar(xn[:, par, t, :], x_sb[:, bass.ds(TPS * (s + 2) + t, 1), :].rearrange("p a n -> p (a n)"),
                                                      mean_var[:, par, t, 0:1], rstd[:, par, t:t + 1],
                                                      ALU.subtract, ALU.mult)
                    ins.then_inc(s_xn, 1)
                if b == 1 and live(s - 1, STEPS):
                    wait(dve, s_PV, STEP * s)
                    acc = ps_pv[1 - par]
                    nc.vector.reciprocal(recip[:, :], acc[:, 256:512]).then_inc(s_rec, 1)
                    wait(dve, s_rec, s)
                    nc.vector.tensor_tensor(att[:, 1 - par, :, :].rearrange("p h q -> p (h q)"), acc[:, 0:256],
                                            recip[:, :], ALU.mult).then_inc(s_att, 1)
                if b == 3 and live(s + 2, STEPS):
                    wait(dve, s_xThi, s + 3)
                    wait(dve, s_xTf, s + 3)
                    nc.vector.tensor_tensor(xT_lo[:, par, :], xT[:, par, :], xT_hi[:, par, :].bitcast(FP32),
                                            ALU.subtract).then_inc(s_xTlo, 1)

            def body(s, par):
                for b in range(STEP):
                    slot(s, par, b)

            pipeline(dve, -2, STEPS + 3, body)

        @block.tensor
        def _(pe):
            pe.wait_ge(s_wload, 16 * LOADS)
            pe.wait_ge(s_prep, 10)

            def slot(s, par, b):
                n = STEP * s + b
                prev = par if b else 1 - par
                if live(n - 1, BATCH):
                    wait(pe, s_max, n)
                    for a in range(2):
                        ins = nc.tensor.transpose(ps_z[:, a * P:(a + 1) * P], z[:, (b - 1) % 2, a, :], ident[:, :])
                    ins.then_inc(s_Z, 1)
                if live(n, BATCH):
                    wait(pe, s_lo, STEP * (s + 1))
                    wait(pe, s_reset, s - 1)
                    for a in range(2):
                        ins = nc.tensor.matmul(ps_s[:, a * 256:(a + 1) * 256],
                                               q_st[:, par, b, 2 * a:2 * a + 2, :].rearrange("p h q -> p (h q)"),
                                               k_st[:, par, b, :, :].rearrange("p g k -> p (g k)"), start=True, stop=True)
                    ins.then_inc(s_S, 1)
                if live(n - 2, BATCH):
                    m, owner = (b - 2) % STEP, par if b >= 2 else 1 - par
                    wait(pe, s_exp, n - 1)
                    if b == 2:
                        wait(pe, s_att, s - 1)
                    rows = slice(32 * m, 32 * m + 32)
                    for out, weights in ((0, v_bd[:, owner, m, :]), (256, ones_gd[:, :, :].rearrange("p g c -> p (g c)"))):
                        for gp in range(2):
                            ins = nc.tensor.matmul(ps_pv[owner][rows, out:out + 256], weights[:, 32 * gp:32 * gp + 32],
                                                   probs[:, m % 2, gp, :], start=(gp == 0), stop=(gp == 1),
                                                   tile_position=(0, 32 * m), skip_group_check=True)
                    ins.then_inc(s_PV, 1)
                if b == 0 and live(s - 2, STEPS):
                    wait(pe, s_move[par], moved(s - 2, par))
                    wait(pe, s_xThi, cap(s + 2, STEPS))
                    for t in range(TPS):
                        ins = nc.tensor.matmul(ps_t[:, t * P:(t + 1) * P], attT[:, par, t * P:(t + 1) * P], wo[:, :],
                                               start=True, stop=True)
                    ins.then_inc(s_Wo, 1)
                if b == 1 and live(s + 1, STEPS):
                    wait(pe, s_xTf, s + 2)
                    wait(pe, s_xThi, s + 2)
                    wait(pe, s_res, s - 1)
                    for m in range(STEP):
                        for g2 in range(2):
                            ins = nc.tensor.matmul(ps_t[64 * g2:64 * g2 + 64, m * P:(m + 1) * P],
                                                   xT[:, 1 - par, m * SEQ:(m + 1) * SEQ], wv[:, :], start=True, stop=True)
                    ins.then_inc(s_V, 1)
                if b == 2 and live(s + 2, STEPS):
                    wait(pe, s_xn, s + 3)
                    wait(pe, s_vbd, 2 * (s + 2))
                    for t in range(TPS):
                        ins = nc.tensor.transpose(ps_t[:, t * P:(t + 1) * P], xn[:, par, t, :], ident[:, :])
                    ins.then_inc(s_T, 1)
                if live(n - 1, BATCH):
                    wait(pe, s_rows, n)
                    wait(pe, s_exp, n - 1)
                    for gp in range(2):
                        ins = nc.tensor.matmul(ps_st[:, gp * 256:(gp + 1) * 256],
                                               k_st[:, prev, (b - 1) % STEP, 2 * gp:2 * gp + 2, :].rearrange("p g k -> p (g k)"),
                                               q_st[:, prev, (b - 1) % STEP, :, :].rearrange("p h q -> p (h q)"),
                                               start=True, stop=True)
                    ins.then_inc(s_ST, 1)
                if live(s + 1, STEPS):
                    wait(pe, s_xTlo, s + 2)
                    wait(pe, s_lo, n + STEP - 1)
                    hi, lo = ((wq_hi, wq_lo), (wk_hi, wk_lo))[b // 2]
                    for j in range(2):
                        h = 2 * (b % 2) + j
                        out = ps_proj[b % 2][:, j * TOK:(j + 1) * TOK]
                        nc.tensor.matmul(out, hi[:, h, :], xT_hi[:, 1 - par, :], start=True, stop=False)
                        nc.tensor.matmul(out, lo[:, h, :], xT_hi[:, 1 - par, :], start=False, stop=False)
                        ins = nc.tensor.matmul(out, hi[:, h, :], xT_lo[:, 1 - par, :], start=False, stop=True)
                    ins.then_inc(s_proj, 1)

            def body(s, par):
                for b in range(STEP):
                    slot(s, par, b)

            pipeline(pe, -2, STEPS + 2, body)


H2, HD2 = 16, 64
HALF = H2 // 2
VW = HD2 + 1


def cross_attention_and_routing(nc, x_sb, rows_dram, filled, starts, w1, w2, b1, b2, w, sem, sb, pb):
    f32 = lambda name, *shape: sb("ca_" + name, [P, *shape], FP32)
    f32r = lambda name, *shape: sb("ca_" + name, [P, *shape], FP32R)
    bf16 = lambda name, *shape: sb("ca_" + name, [P, *shape], BF16)

    a_hi, a_lo = f32r("a_hi", H2, P), f32r("a_lo", H2, P)
    a_raw = f32("a_raw", 4 * P)
    wv_hi, wv_lo = f32r("wv_hi", H2 * HD2), f32r("wv_lo", H2 * HD2)
    wo = f32("wo", 8, P)
    ident, ident_bf, mask_bf = f32("ident", P), bf16("ident_bf", P), bf16("mask_bf", HALF * SEQ)
    pick = f32r("pick", P)
    keys = f32("keys", 2, TOK)
    ctx_hi, ctx_lo = f32r("ctx_hi", 2, TOK), f32r("ctx_lo", 2, TOK)
    half, eps, zeros = f32("half", TPS), f32("eps", TPS), f32("zeros", TOK)
    stats, mean_var = f32("stats", 2, TPS, 6), f32("mean_var", 2, TPS, 2)
    var_eps, rstd = f32("var_eps", TPS), f32("rstd", 2, TPS)
    xn = f32("xn", 2, TPS, P)
    xT_hi, xT_lo = f32r("xT_hi", 2, TOK), f32r("xT_lo", 2, TOK)
    t_all = f32("t", 2, H2, TOK)
    v_bd = f32("v_bd", 2, TPS, H2, 2, VW)
    raw = f32("raw", 2, HALF * SEQ)
    neg_max = f32("neg_max", 2, 4, 2)
    rows = f32r("rows", 2, HALF * SEQ)
    probs = f32("probs", 2, HALF, SEQ)
    recip = f32("recip", 2, 2, 2)
    o = f32("o", 2, 2, 4, HD2)
    oT = f32("oT", 2, 2, 2, 2, 2, SEQ)
    wv_raw = t_all[:, 0, 0:4, :].rearrange("p h n -> p (h n)")
    mask_raw = t_all[:, 0, 4:6, :].rearrange("p h n -> p (h n)")
    pick_raw = t_all[:, 0, 6, 0:P]
    wqT, wkT = (t_all[:, 1, 4 * n:4 * n + 4, :].rearrange("p h (a n) -> p (h a) n", n=P) for n in range(2))

    rf = lambda name, *shape: sb("ro_" + name, [P, *shape], FP32)
    wg, bg, index, dest = rf("wg", P), rf("bg", TPS, E), rf("index", E), rf("dest", TILES, TOPK)
    tri, ones, tri_raw = sb("ro_tri", [P, P], BF16), sb("ro_ones", [P, P], BF16), t_all[:, 0, 7, 0:P]
    r_stats, r_mean_var = rf("stats", TPS, 6), rf("mean_var", TPS, 2)
    r_var_eps, r_rstd, nothing = rf("var_eps", TPS), rf("rstd", TPS), rf("nothing", TPS)
    r_xn, r_xT, out_rows = rf("xn", 2, TPS, P), rf("xT", TOK), rf("rows", 2, TPS, TOPK, WIDTH)
    logits, top, shifted, expd = (rf(n, TPS, E) for n in ("logits", "top", "shifted", "expd"))
    which, which_f = sb("ro_which", [P, TPS, E], mybir.dt.uint32), rf("which_f", TPS, TOPK)
    chosen, mask = rf("chosen", TPS, TOPK, E), sb("ro_mask", [P, TPS, E], BF16)
    place, place_sel, place_f = rf("place", TPS, E), rf("place_sel", TPS, TOPK, E), rf("place_f", TPS, TOPK)
    place_u = sb("ro_place_u", [P, 2, TPS, TOPK], mybir.dt.uint32)
    total, both, den = rf("total", TPS), rf("both", TPS), rf("den", TPS)

    ps_st = [pb("st0"), pb("st1")]
    ps_p = [pb("p0"), pb("p1")]
    ps_pv = [pb("pv0"), pb("pv1")]
    ps_x, ps_m = pb("x"), pb("m")

    names = ("loaded prep zeroed a_product a_scaled a_split stats mean_var var_eps rstd xn transposed xT_hi xT_lo "
             "ctx_hi ctx_lo scores raw_copied scores_transposed max max_transposed max_rows shifted exp pv_product "
             "reciprocal normalised o_transposed o_copied out_product residual fill fill_act fill_dve").split()
    S = {n: sem("ca_" + n) for n in names}
    s_keys = [sem("ca_keys_even"), sem("ca_keys_odd")]
    LOADS = 7
    names = ("loaded constants triangle w_loaded stats mean_var var_eps rstd xn transposed xT_copied xn_copied logits "
             "sorted shifted choices chosen mask exp gating counted placing places gates dest rows_whole").split()
    R = {n: sem("ro_" + n) for n in names}
    s_sent = [sem("ro_sent_even"), sem("ro_sent_odd")]
    sent = lambda s, par: 16 * TPS * TOPK * ((s - par) // 2 + 1) if isinstance(s, int) else \
        8 * TPS * TOPK * (s - par) + 16 * TPS * TOPK
    R_LOADS = 6
    tile_of_x = lambda t: x_sb[:, bass.ds(t, 1), :].rearrange("p a n -> p (a n)")

    with nc.Block() as block:

        @block.sync
        def _(sp):
            for dst, src in ((wqT[:, :, :], w["ca_wqT"]), (wkT[:, :, :], w["ca_wkT"]), (wv_raw, w["ca_wv"]),
                             (ident[:, :], w["ident"]), (mask_raw, w["ca_mask"]), (pick_raw, w["ca_pick"]),
                             (wo[:, :, :], w["ca_wo"])):
                sp.dma_start(dst, src).then_inc(S["loaded"], 16)
            for dst, src in ((wg[:, :], w["ff_wg"]), (bg[:, :, :], w["ff_bg"]), (index[:, :], w["ff_index"]),
                             (dest[:, :, :], w["ff_dest"]), (starts[:, :], w["ff_starts"]), (tri_raw, w["ff_tri"])):
                sp.dma_start(dst, src).then_inc(R["loaded"], 16)
            for dst, src in ((w1[:, :, :], w["ff_w1"]), (w2[:, :, :], w["ff_w2"]), (b1[:, :, :], w["ff_b1"]),
                             (b2[:, :, :], w["ff_b2"])):
                sp.dma_start(dst, src).then_inc(R["w_loaded"], 16)

            def body(s, par):
                if live(s + 2, STEPS):
                    wait(sp, S["scores"], 4 * (s + 1))
                    sp.dma_start(keys[:, par, :], w["ctxT"][:, bass.ds(TOK * (s + 2), TOK)]).then_inc(s_keys[par], 16)

            pipeline(sp, -2, STEPS, body, 3, 2)
            sp.wait_ge(R["w_loaded"], 64)

        @block.gpsimd
        def _(pool):
            nc.gpsimd.memset(half[:, :], -0.5).then_inc(S["zeroed"], 1)
            nc.gpsimd.memset(rows[:, :, :].bitcast(FP32), 0.0).then_inc(S["zeroed"], 1)
            nc.gpsimd.memset(v_bd[:, :, :, :, :, :], 0.0).then_inc(S["zeroed"], 1)
            nc.gpsimd.memset(eps[:, :], EPS).then_inc(S["zeroed"], 1)
            nc.gpsimd.memset(zeros[:, :], 0.0).then_inc(S["zeroed"], 1)
            pool.wait_ge(S["zeroed"], 5)
            for b in range(2):
                nc.gpsimd.memset(v_bd[64 * b:64 * b + 64, :, :, :, b, HD2:VW], 1.0).then_inc(S["zeroed"], 1)
            pool.wait_ge(S["zeroed"], 7)
            pool.wait_ge(S["loaded"], 16 * LOADS)

            def body(s, par):
                if live(s - 3, STEPS):
                    for part in ("xn_copied", "dest", "gates", "places"):
                        wait(pool, R[part], s - 2)
                    wait(pool, R["rows_whole"], s - 3)
                    nc.gpsimd.tensor_tensor(nothing[:, :], half[:, :], half[:, :], ALU.add).then_inc(R["rows_whole"], 1)
                    for t in range(TPS):
                        for k in range(TOPK):
                            at = bass.IndirectOffsetOnAxis(ap=place_u[:, 1 - par, t, k:k + 1], axis=0)
                            nc.gpsimd.indirect_dma_start(rows_dram, at, out_rows[:, 1 - par, t, k, :], None)\
                              .then_inc(s_sent[1 - par], 16)
                if live(s + 3, STEPS):
                    wait(pool, S["mean_var"], s + 4)
                    wait(pool, S["ctx_lo"], s + 2)
                    nc.gpsimd.tensor_tensor(var_eps[:, :], mean_var[:, 1 - par, :, 1], eps[:, :], ALU.add)\
                      .then_inc(S["var_eps"], 1)
                    pool.wait_ge(S["var_eps"], s + 4)
                    nc.gpsimd.tensor_tensor(rstd[:, 1 - par, :], var_eps[:, :], half[:, :], ALU.pow).then_inc(S["rstd"], 1)
                if live(s - 1, STEPS):
                    wait(pool, R["mean_var"], s)
                    nc.gpsimd.tensor_tensor(r_var_eps[:, :], r_mean_var[:, :, 1], eps[:, :], ALU.add)\
                      .then_inc(R["var_eps"], 1)
                    pool.wait_ge(R["var_eps"], s)
                    nc.gpsimd.tensor_tensor(r_rstd[:, :], r_var_eps[:, :], half[:, :], ALU.pow).then_inc(R["rstd"], 1)
                if live(s + 2, STEPS):
                    wait(pool, S["rstd"], cap(s + 4, STEPS))
                    wait(pool, S["ctx_lo"], s + 2)
                    wait(pool, S["fill"], 12 * (s + 1))
                    wait(pool, s_keys[par], 8 * (s + 2 - par) + 16)
                    src = keys[:, par, :]
                    nc.gpsimd.tensor_tensor(ctx_hi[:, par, :], src, zeros[:, :], ALU.add).then_inc(S["ctx_hi"], 1)
                    pool.wait_ge(S["ctx_hi"], s + 3)
                    nc.gpsimd.tensor_tensor(ctx_lo[:, par, :], src, ctx_hi[:, par, :].bitcast(FP32), ALU.subtract)\
                      .then_inc(S["ctx_lo"], 1)

            pipeline(pool, -3, STEPS + 3, body, 3, 4)
            for par in range(2):
                pool.wait_ge(s_sent[par], sent(STEPS - 2 + par, par))

        @block.scalar
        def _(act):
            act.wait_ge(S["loaded"], 16 * LOADS)
            nc.scalar.copy(ident_bf[:, :], ident[:, :]).then_inc(S["prep"], 1)
            nc.scalar.copy(mask_bf[:, :], mask_raw).then_inc(S["prep"], 1)
            nc.scalar.copy(pick[:, :], pick_raw).then_inc(S["prep"], 1)
            nc.scalar.copy(wv_hi[:, :], wv_raw).then_inc(S["prep"], 1)
            act.wait_ge(R["loaded"], 16 * R_LOADS)
            nc.scalar.copy(tri[:, :], tri_raw).then_inc(R["triangle"], 1)
            for c in range(4):
                act.wait_ge(S["a_product"], c + 1)
                wait(act, S["a_split"], 2 * c)
                nc.scalar.mul(a_raw[:, :], ps_p[c % 2][:, :], HD2 ** -0.5).then_inc(S["a_scaled"], 1)

            def slot(s, par, u):
                n = 4 * s + u
                f = n + 4
                if live(n - 1, 4 * STEPS):
                    wait(act, S["shifted"], n)
                    wait(act, S["pv_product"], n - 2)
                    nc.scalar.activation(probs[:, (u - 1) % 2, :, :].rearrange("p h q -> p (h q)"), ps_st[(u - 1) % 2][:, :],
                                         ACT.Exp).then_inc(S["exp"], 1)
                if live(n, 4 * STEPS):
                    wait(act, S["scores"], n + 1)
                    nc.scalar.copy(raw[:, u % 2, :], ps_st[u % 2][:, :]).then_inc(S["raw_copied"], 1)
                if live(s + 1, STEPS):
                    wait(act, S["fill"], 3 * f + 1)
                    nc.scalar.copy(t_all[:, 1 - par, 4 * u:4 * u + 2, :].rearrange("p h n -> p (h n)"), ps_p[u % 2][:, :])\
                      .then_inc(S["fill_act"], 1)
                if u == 0 and live(s + 2, STEPS):
                    wait(act, S["transposed"], s + 3)
                    nc.scalar.copy(xT_hi[:, par, :], ps_m[:, 0:TOK]).then_inc(S["xT_hi"], 1)
                if u == 0 and live(s - 3, STEPS):
                    wait(act, R["shifted"], s - 2)
                    nc.scalar.activation(expd[:, :, :].rearrange("p t e -> p (t e)"),
                                         shifted[:, :, :].rearrange("p t e -> p (t e)"), ACT.Exp).then_inc(R["exp"], 1)
                if u == 2 and live(s - 2, STEPS):
                    wait(act, R["transposed"], s - 1)
                    nc.scalar.copy(r_xT[:, :], ps_m[:, 0:TOK]).then_inc(R["xT_copied"], 1)
                if live(n, 4 * STEPS):
                    wait(act, S["max_transposed"], n + 1)
                    nc.scalar.copy(rows[0:2, u % 2, :], ps_x[0:2, :]).then_inc(S["max_rows"], 1)
                if live(s + 1, STEPS):
                    wait(act, S["fill"], 3 * f + 3)
                    nc.scalar.copy(v_bd[0:64, 1 - par, u // 2, HALF * (u % 2):HALF * (u % 2) + HALF, 0, 0:HD2],
                                   ps_p[u % 2][0:64, :].rearrange("p (h d) -> p h d", h=HALF)).then_inc(S["fill_act"], 1)
                if u == 2 and live(s - 2, STEPS):
                    if live(s - 4, STEPS):
                        wait(act, s_sent[par], sent(s - 4, par))
                    wait(act, R["xn"], s - 1)
                    nc.scalar.copy(out_rows[:, par, :, :, 0:D], r_xn[:, par, :, :].unsqueeze(2).broadcast_to([P, TPS, TOPK, D]))\
                      .then_inc(R["xn_copied"], 1)

            def body(s, par):
                for u in range(4):
                    slot(s, par, u)

            pipeline(act, -2, STEPS + 3, body, 2, 4)

        @block.vector
        def _(dve):
            tt = nc.vector.tensor_tensor
            dve.wait_ge(R["loaded"], 16 * R_LOADS)
            nc.vector.memset(ones[:, :], 1.0).then_inc(R["constants"], 1)
            nc.vector.tensor_copy(filled[:, 0, :], starts[:, :]).then_inc(R["constants"], 1)
            dve.wait_ge(R["constants"], 2)

            def chain(name, per, r, k, ins):
                ins.then_inc(R[name], 1)
                dve.wait_ge(R[name], per * r + k + 1)

            dve.wait_ge(S["prep"], 4)
            nc.vector.tensor_tensor(wv_lo[:, :], wv_raw, wv_hi[:, :].bitcast(FP32), ALU.subtract).then_inc(S["prep"], 1)
            for c in range(4):
                dve.wait_ge(S["a_scaled"], c + 1)
                heads = lambda t: t[:, :, :].rearrange("p (a b) n -> p a b n", b=2)[:, 4 * (c // 2):4 * (c // 2) + 4, c % 2, :]
                full = a_raw[:, :].rearrange("p (a n) -> p a n", a=4)
                nc.vector.tensor_copy(heads(a_hi), full).then_inc(S["a_split"], 1)
                dve.wait_ge(S["a_split"], 2 * c + 1)
                nc.vector.tensor_tensor(heads(a_lo), full, heads(a_hi).bitcast(FP32), ALU.subtract).then_inc(S["a_split"], 1)

            def slot(s, par, u):
                n = 4 * s + u
                f = n + 4
                if u == 1 and live(s - 3, STEPS):
                    r, q = s - 3, 1 - par
                    wait(dve, R["exp"], r + 1)
                    nc.vector.tensor_reduce(total[:, :], expd[:, :, :], axis=AX.X, op=ALU.add)
                    chain("gating", 3, r, 0, tt(both[:, :], expd[:, :, 0], expd[:, :, 1], ALU.add))
                    chain("gating", 3, r, 1,
                          nc.vector.scalar_tensor_tensor(den[:, :], total[:, :], 1e-8, both[:, :], ALU.mult, ALU.add))
                    nc.vector.reciprocal(den[:, :], den[:, :]).then_inc(R["gating"], 1)
                    wait(dve, R["counted"], r + 1)
                    nums = ps_m[:, 0:2 * TPS * E].rearrange("p (w t e) -> p w t e", w=2, t=TPS)
                    for t in range(TPS):
                        chain("placing", 6, r, t, tt(filled[:, t + 1, :], filled[:, t, :], nums[:, 1, t, :], ALU.add))
                    chain("placing", 6, r, 2, tt(place[:, :, :], filled[:, 0:TPS, :], nums[:, 0, :, :], ALU.add))
                    for t in range(TPS):
                        ins = tt(place_sel[:, t, :, :], chosen[:, t, :, :],
                                 place[:, t, :].unsqueeze(1).broadcast_to([P, TOPK, E]), ALU.mult)
                    chain("placing", 6, r, 3, ins)
                    chain("placing", 6, r, 4, nc.vector.tensor_reduce(place_f[:, :, :], place_sel[:, :, :, :],
                                                                      axis=AX.X, op=ALU.add))
                    nc.vector.tensor_copy(filled[:, 0, :], filled[:, TPS, :]).then_inc(R["placing"], 1)
                    nc.vector.tensor_copy(place_u[:, q, :, :], place_f[:, :, :]).then_inc(R["places"], 1)
                    wait(dve, R["xn_copied"], r + 1)
                    dve.wait_ge(R["gating"], 3 * r + 3)
                    tt(out_rows[:, q, :, :, META], expd[:, :, 0:TOPK],
                       den[:, :].unsqueeze(2).broadcast_to([P, TPS, TOPK]), ALU.mult).then_inc(R["gates"], 1)
                    nc.vector.tensor_copy(out_rows[:, q, :, :, META + 1], dest[:, bass.ds(TPS * r, TPS), :])\
                      .then_inc(R["dest"], 1)
                if u == 2 and live(s - 1, STEPS):
                    wait(dve, S["residual"], TPS * s)
                if live(n - 2, 4 * STEPS):
                    m, owner = (u - 2) % 4, par if u >= 2 else 1 - par
                    wait(dve, S["o_transposed"], n - 1)
                    wait(dve, S["out_product"], 2 * (s - (u < 2)) + m // 2 - 1)
                    dst = oT[:, m // 2, m % 2, :, :, :, :].rearrange("p j h b q -> p b j h q")
                    for b in range(2):
                        ins = nc.vector.tensor_copy(dst[:, b, :, :, :], ps_x[:, 256 * b:256 * b + 256]
                                                    .rearrange("p (j h q) -> p j h q", j=2, h=2))
                    ins.then_inc(S["o_copied"], 1)
                if u == 2 and live(s + 3, STEPS):
                    for t in range(TPS):
                        ins = nc.vector.bn_stats(stats[:, 1 - par, t, :], tile_of_x(TPS * (s + 3) + t))
                    ins.then_inc(S["stats"], 1)
                if u == 2 and live(s - 1, STEPS):
                    for t in range(TPS):
                        ins = nc.vector.bn_stats(r_stats[:, t, :], tile_of_x(TPS * (s - 1) + t))
                    ins.then_inc(R["stats"], 1)
                if u == 2:
                    if live(s + 3, STEPS):
                        dve.wait_ge(S["stats"], s + 4)
                    if live(s - 1, STEPS):
                        dve.wait_ge(R["stats"], s)
                if live(n, 4 * STEPS):
                    wait(dve, S["scores_transposed"], n + 1)
                    nc.vector.tensor_reduce(neg_max[:, u % 2, :, :], ps_x[:, :].rearrange("p (a b k) -> p a b k", a=4, b=2),
                                            axis=AX.X, op=ALU.max, negate=True).then_inc(S["max"], 1)
                if u == 2 and live(s + 3, STEPS):
                    for t in range(TPS):
                        ins = nc.vector.bn_aggr(mean_var[:, 1 - par, t, :], stats[:, 1 - par, t, :])
                    ins.then_inc(S["mean_var"], 1)
                if u == 2 and live(s - 1, STEPS):
                    for t in range(TPS):
                        ins = nc.vector.bn_aggr(r_mean_var[:, t, :], r_stats[:, t, :])
                    ins.then_inc(R["mean_var"], 1)
                if u == 3 and live(s - 2, STEPS):
                    wait(dve, R["logits"], s - 1)
                    chain("sorted", 2, s - 2, 0, tt(logits[:, :, :], ps_m[:, 0:TPS * P]
                          .rearrange("p (t n) -> p t n", t=TPS)[:, :, 0:E], bg[:, :, :], ALU.add))
                if u == 3 and live(s - 1, STEPS):
                    wait(dve, R["rstd"], s)
                    wait(dve, R["xn_copied"], s - 2)
                    for t in range(TPS):
                        ins = nc.vector.tensor_scalar(r_xn[:, 1 - par, t, :], tile_of_x(TPS * (s - 1) + t),
                                                      r_mean_var[:, t, 0:1], r_rstd[:, t:t + 1], ALU.subtract, ALU.mult)
                    ins.then_inc(R["xn"], 1)
                if u == 3 and live(s - 2, STEPS):
                    r = s - 2
                    for t in range(TPS):
                        ins = nc.vector.max(top[:, t, :], logits[:, t, :])
                    chain("sorted", 2, r, 1, ins)
                    tt(shifted[:, :, :], top[:, :, :], top[:, :, 0:1].broadcast_to([P, TPS, E]), ALU.subtract)\
                        .then_inc(R["shifted"], 1)
                    for t in range(TPS):
                        ins = nc.vector.max_index(which[:, t, :], top[:, t, :], logits[:, t, :])
                    chain("choices", 2, r, 0, ins)
                    chain("choices", 2, r, 1, nc.vector.tensor_copy(which_f[:, :, :], which[:, :, 0:TOPK]))
                    for t in range(TPS):
                        ins = tt(chosen[:, t, :, :], index[:, :].unsqueeze(1).broadcast_to([P, TOPK, E]),
                                 which_f[:, t, :].unsqueeze(2).broadcast_to([P, TOPK, E]), ALU.is_equal)
                    chain("chosen", 1, r, 0, ins)
                    tt(mask[:, :, :], chosen[:, :, 0, :], chosen[:, :, 1, :], ALU.add).then_inc(R["mask"], 1)
                if u == 3 and live(s + 3, STEPS):
                    wait(dve, S["rstd"], s + 4)
                    for t in range(TPS):
                        ins = nc.vector.tensor_scalar(xn[:, 1 - par, t, :], tile_of_x(TPS * (s + 3) + t),
                                                      mean_var[:, 1 - par, t, 0:1], rstd[:, 1 - par, t:t + 1],
                                                      ALU.subtract, ALU.mult)
                    ins.then_inc(S["xn"], 1)
                if live(n - 1, 4 * STEPS):
                    wait(dve, S["pv_product"], n)
                    for c in range(2):
                        acc = ps_pv[c][:, 0:4 * VW].rearrange("p (a b d) -> p a b d", a=2, b=2)
                        ins = nc.vector.reciprocal(recip[:, c, :, :], acc[:, :, :, HD2])
                    ins.then_inc(S["reciprocal"], 1)
                    dve.wait_ge(S["reciprocal"], n)
                    wait(dve, S["o_transposed"], n - 2)
                    for c in range(2):
                        acc = ps_pv[c][:, 0:4 * VW].rearrange("p (a b d) -> p a b d", a=2, b=2)
                        dst = o[:, (u - 1) % 2, :, 2 * c:2 * c + 2, :].rearrange("p b a d -> p a b d")
                        ins = nc.vector.tensor_tensor(dst, acc[:, :, :, 0:HD2],
                                                      recip[:, c, :, :].unsqueeze(3).broadcast_to([P, 2, 2, HD2]), ALU.mult)
                    ins.then_inc(S["normalised"], 1)
                if live(s + 1, STEPS):
                    wait(dve, S["fill"], 3 * f + 2)
                    nc.vector.tensor_copy(t_all[:, 1 - par, 4 * u + 2:4 * u + 4, :].rearrange("p h n -> p (h n)"),
                                          ps_p[(u + 1) % 2][:, :]).then_inc(S["fill_dve"], 1)
                if u == 0 and live(s + 2, STEPS):
                    wait(dve, S["xT_hi"], s + 3)
                    nc.vector.tensor_tensor(xT_lo[:, par, :], ps_m[:, 0:TOK], xT_hi[:, par, :].bitcast(FP32),
                                            ALU.subtract).then_inc(S["xT_lo"], 1)
                if live(s + 1, STEPS):
                    wait(dve, S["fill"], 3 * f + 3)
                    nc.vector.tensor_copy(v_bd[64:128, 1 - par, u // 2, HALF * (u % 2):HALF * (u % 2) + HALF, 1, 0:HD2],
                                          ps_p[u % 2][64:128, :].rearrange("p (h d) -> p h d", h=HALF)).then_inc(S["fill_dve"], 1)
                tile = {1: TPS * (s - 1) + 1, 3: TPS * s}.get(u)
                if tile is not None and live(tile, TILES):
                    wait(dve, S["out_product"], tile + 1)
                    row = tile_of_x(tile)
                    nc.vector.tensor_tensor(row, ps_m[:, 0:P], row, ALU.add).then_inc(S["residual"], 1)

            def body(s, par):
                for u in range(4):
                    slot(s, par, u)

            pipeline(dve, -3, STEPS + 3, body, 3, 4)

        @block.tensor
        def _(pe):
            pe.wait_ge(S["loaded"], 16 * LOADS)
            for c in range(4):
                wait(pe, S["a_scaled"], c - 1)
                for j in range(4):
                    pair, r = 4 * (c // 2) + j, slice(64 * (c % 2), 64 * (c % 2) + 64)
                    ins = nc.tensor.matmul(ps_p[c % 2][:, j * P:(j + 1) * P], wqT[r, pair, :], wkT[r, pair, :],
                                           start=True, stop=True)
                ins.then_inc(S["a_product"], 1)
            pe.wait_ge(S["prep"], 5)
            pe.wait_ge(S["a_split"], 8)
            pe.wait_ge(S["zeroed"], 7)
            pe.wait_ge(R["constants"], 2)
            pe.wait_ge(R["triangle"], 1)

            def t_fill(s, par, u, i):
                bank, f = ps_p[(u + i) % 2], 4 * s + u + 4
                if i == 0:
                    wait(pe, S["fill_dve"], 2 * f - 1)
                    wait(pe, S["xT_lo"], s + 2)
                else:
                    wait(pe, S["fill_act"], 2 * f)
                    wait(pe, S["fill_dve"], 2 * f)
                for j in range(2):
                    h, out = 4 * u + 2 * i + j, bank[:, j * TOK:(j + 1) * TOK]
                    nc.tensor.matmul(out, a_hi[:, h, :], xT_hi[:, 1 - par, :], start=True, stop=False)
                    nc.tensor.matmul(out, a_lo[:, h, :], xT_hi[:, 1 - par, :], start=False, stop=False)
                    ins = nc.tensor.matmul(out, a_hi[:, h, :], xT_lo[:, 1 - par, :], start=False, stop=True)
                ins.then_inc(S["fill"], 1)

            def v_fill(s, par, u):
                f = 4 * s + u + 4
                wait(pe, S["fill_act"], 2 * f + 1)
                wait(pe, S["ctx_lo"], s + 2)
                cols, tok = slice(512 * (u % 2), 512 * (u % 2) + 512), slice(P * (u // 2), P * (u // 2) + P)
                out = ps_p[u % 2][:, :]
                nc.tensor.matmul(out, ctx_hi[:, 1 - par, tok], wv_hi[:, cols], start=True, stop=False)
                nc.tensor.matmul(out, ctx_lo[:, 1 - par, tok], wv_hi[:, cols], start=False, stop=False)
                nc.tensor.matmul(out, ctx_hi[:, 1 - par, tok], wv_lo[:, cols], start=False, stop=True).then_inc(S["fill"], 1)

            def slot(s, par, u):
                n = 4 * s + u
                tile, hh = u // 2, u % 2
                st = ps_st[u % 2]
                if live(n, 4 * STEPS):
                    wait(pe, S["fill_act"], 8 * (s + 1))
                    wait(pe, S["fill_dve"], 8 * (s + 1))
                    wait(pe, S["exp"], n - 1)
                    nc.tensor.matmul(st[:, :], ident_bf[:, :], mask_bf[:, :], start=True, stop=False, skip_group_check=True)
                    for b in range(2):
                        tok = P * tile + SEQ * b
                        ins = nc.tensor.matmul(st[64 * b:64 * b + 64, :], keys[:, par, tok:tok + SEQ],
                                               t_all[:, par, HALF * hh:HALF * hh + HALF, tok:tok + SEQ],
                                               start=False, stop=True, skip_group_check=True)
                    ins.then_inc(S["scores"], 1)
                if live(n - 2, 4 * STEPS):
                    m = (u - 2) % 4
                    wait(pe, S["normalised"], n - 1)
                    wait(pe, S["max_rows"], cap(n, 4 * STEPS))
                    for b in range(2):
                        for j in range(2):
                            ins = nc.tensor.transpose(ps_x[:, (2 * b + j) * P:(2 * b + j + 1) * P],
                                                      o[:, m % 2, b, 2 * j:2 * j + 2, :].rearrange("p a d -> p (a d)"), ident[:, :])
                    ins.then_inc(S["o_transposed"], 1)
                if u == 0 and live(s + 2, STEPS):
                    wait(pe, S["xn"], s + 3)
                    wait(pe, S["residual"], 2 * s - 1)
                    for t in range(TPS):
                        ins = nc.tensor.transpose(ps_m[:, t * P:(t + 1) * P], xn[:, par, t, :], ident[:, :])
                    ins.then_inc(S["transposed"], 1)
                if u == 2 and live(s - 2, STEPS):
                    wait(pe, R["xn"], s - 1)
                    wait(pe, S["residual"], cap(TPS * s, TILES))
                    wait(pe, R["placing"], cap(6 * (s - 3) + 3, 6 * STEPS))
                    for t in range(TPS):
                        ins = nc.tensor.transpose(ps_m[:, t * P:(t + 1) * P], r_xn[:, par, t, :], ident[:, :])
                    ins.then_inc(R["transposed"], 1)
                if live(s + 1, STEPS):
                    t_fill(s, par, u, 0)
                if live(n, 4 * STEPS):
                    wait(pe, S["raw_copied"], n + 1)
                    wait(pe, S["o_copied"], n - 1)
                    for a in range(4):
                        ins = nc.tensor.transpose(ps_x[:, a * P:(a + 1) * P], raw[:, u % 2, a * P:(a + 1) * P], ident[:, :])
                    ins.then_inc(S["scores_transposed"], 1)
                if live(n - 1, 4 * STEPS):
                    m, owner = (u - 1) % 4, par if u else 1 - par
                    wait(pe, S["exp"], n)
                    wait(pe, S["normalised"], n - 1)
                    for a in range(4):
                        for h2 in range(2):
                            h = 2 * a + h2
                            ins = nc.tensor.matmul(ps_pv[a // 2][64 * h2:64 * h2 + 64, (a % 2) * 2 * VW:(a % 2 + 1) * 2 * VW],
                                                   probs[:, m % 2, h, :],
                                                   v_bd[:, owner, m // 2, HALF * (m % 2) + h, :, :].rearrange("p b d -> p (b d)"),
                                                   start=True, stop=True)
                    ins.then_inc(S["pv_product"], 1)
                if live(s + 1, STEPS):
                    t_fill(s, par, u, 1)
                if live(n, 4 * STEPS):
                    wait(pe, S["max"], n + 1)
                    for a in range(4):
                        ins = nc.tensor.transpose(ps_x[0:2, a * P:(a + 1) * P], neg_max[:, u % 2, a, :], ident[:, :])
                    ins.then_inc(S["max_transposed"], 1)
                if live(s + 1, STEPS):
                    v_fill(s, par, u)
                if u == 2 and live(s - 2, STEPS):
                    wait(pe, R["xT_copied"], s - 1)
                    for t in range(TPS):
                        ins = nc.tensor.matmul(ps_m[:, t * P:(t + 1) * P], r_xT[:, t * P:(t + 1) * P], wg[:, :],
                                               start=True, stop=True)
                    ins.then_inc(R["logits"], 1)
                if u == 0 and live(s - 3, STEPS):
                    wait(pe, R["mask"], s - 2)
                    wait(pe, S["xT_lo"], cap(s + 3, STEPS))
                    wait(pe, S["residual"], cap(TPS * s - 1, TILES))
                    by_expert = mask[:, :, :].rearrange("p t e -> p (t e)")
                    nc.tensor.matmul(ps_m[:, 0:TPS * E], tri[:, :], by_expert, start=True, stop=True)
                    nc.tensor.matmul(ps_m[:, TPS * E:2 * TPS * E], ones[:, :], by_expert, start=True, stop=True)\
                      .then_inc(R["counted"], 1)
                done = {1: TPS * (s - 1) + 1, 3: TPS * s}.get(u)
                if done is not None and live(done, TILES):
                    wait(pe, S["o_copied"], 2 * done + 2)
                    wait(pe, S["xT_lo"], cap(s + 3, STEPS) if u == 1 else 0)
                    wait(pe, S["residual"], done)
                    if u == 3:
                        wait(pe, R["sorted"], 2 * (s - 2) + 1)
                    else:
                        wait(pe, R["placing"], 6 * (s - 3) + 3)
                    t = int(u == 1)
                    for c in range(8):
                        ins = nc.tensor.matmul(ps_m[:, 0:P],
                                               oT[:, t, c // 4, c // 2 % 2, c % 2, :, :].rearrange("p b q -> p (b q)"),
                                               wo[:, c, :], start=(c == 0), stop=(c == 7))
                    ins.then_inc(S["out_product"], 1)
                if live(n, 4 * STEPS):
                    wait(pe, S["max_rows"], n + 1)
                    nc.tensor.matmul(st[:, :], pick[:, :], rows[:, u % 2, :], start=False, stop=True,
                                     skip_group_check=True).then_inc(S["shifted"], 1)

            def body(s, par):
                for u in range(4):
                    slot(s, par, u)

            pipeline(pe, -2, STEPS + 3, body, 2, 4)


def run_table(nc, rows_dram, filled, starts, table, w, sem, sb):
    f32 = lambda name, *shape: sb("rt_" + name, [P, *shape], FP32)
    thresholds, upto, run_no = f32("thresholds", E, FULL), f32("upto", E, E), f32("run_no", RUNS)
    pad = f32("pad", 2, WIDTH)
    count, over = f32("count", E), f32("over", E, FULL)
    runs, runs_upto, ended = f32("runs", E), f32("runs_upto", E, E), f32("ended", E)
    past, skip = f32("past", RUNS, E), f32("skip", E)
    first_row, run_expert = f32("first_row", RUNS), f32("run_expert", RUNS)
    ends = sb("rt_ends", [P, E], mybir.dt.int32)
    s_loaded, s_pad, s_ends = sem("rt_loaded"), sem("rt_pad_loaded"), sem("rt_ends_known")
    s_tabled, s_padded = sem("rt_tabled"), [sem("rt_padded_sp"), sem("rt_padded_act")]
    block_of = lambda first: rows_dram[bass.ds(first, ROWS), :].rearrange("(h p) n -> p h n", p=P)

    def write_padding(eng, experts, s_done):
        eng.wait_ge(s_pad, 16)
        eng.wait_ge(s_ends, 1)
        for e in experts:
            end = eng.value_load(ends[0:1, e:e + 1], min_val=0, max_val=E * REGION) if e < E else E * REGION
            eng.dma_start(block_of(end), pad[:, :, :]).then_inc(s_done, 16)
        eng.wait_ge(s_done, 16 * len(experts))

    with nc.Block() as block:

        @block.sync
        def _(sp):
            sp.dma_start(pad[:, :, :], w["ff_pad"]).then_inc(s_pad, 16)
            for dst, src in ((thresholds[:, :, :], w["ff_thresholds"]), (upto[:, :, :], w["ff_upto"]),
                             (run_no[:, :], w["ff_run_no"])):
                sp.dma_start(dst, src).then_inc(s_loaded, 16)
            write_padding(sp, range(0, 5), s_padded[0])

        @block.scalar
        def _(act):
            write_padding(act, range(5, E + 1), s_padded[1])

        @block.vector
        def _(dve):
            tt, ts = nc.vector.tensor_tensor, nc.vector.tensor_scalar
            nc.vector.tensor_copy(ends[:, :], filled[:, 0, :]).then_inc(s_ends, 1)
            dve.wait_ge(s_loaded, 48)
            n = [0]

            def step(ins):
                n[0] += 1
                ins.then_inc(s_tabled, 1)
                dve.wait_ge(s_tabled, n[0])

            across = lambda t, m: t[:, :].unsqueeze(2).broadcast_to([P, E, m])
            along = lambda t, m: t[:, :].unsqueeze(1).broadcast_to([P, m, E])
            step(tt(count[:, :], filled[:, 0, :], starts[:, :], ALU.subtract))
            step(tt(over[:, :, :], across(count, FULL), thresholds[:, :, :], ALU.is_gt))
            step(nc.vector.tensor_reduce(runs[:, :], over[:, :, :], axis=AX.X, op=ALU.add))
            step(tt(runs_upto[:, :, :], along(runs, E), upto[:, :, :], ALU.mult))
            step(nc.vector.tensor_reduce(ended[:, :], runs_upto[:, :, :], axis=AX.X, op=ALU.add))
            step(tt(past[:, :, :], run_no[:, :].unsqueeze(2).broadcast_to([P, RUNS, E]), along(ended, RUNS), ALU.is_ge))
            step(nc.vector.tensor_reduce(run_expert[:, :], past[:, :, :], axis=AX.X, op=ALU.add))
            ts(run_expert[:, :], run_expert[:, :], float(E - 1), None, ALU.min)
            step(ts(skip[:, :], runs[:, :], float(-ROWS), float(REGION), ALU.mult, ALU.add))
            step(tt(past[:, :, :], past[:, :, :], along(skip, RUNS), ALU.mult))
            step(nc.vector.tensor_reduce(first_row[:, :], past[:, :, :], axis=AX.X, op=ALU.add))
            step(nc.vector.scalar_tensor_tensor(first_row[:, :], run_no[:, :], float(ROWS), first_row[:, :], ALU.mult, ALU.add))
            step(ts(first_row[:, :], first_row[:, :], float(E * REGION), None, ALU.min))
            nc.vector.tensor_copy(table[:, 0, :], run_expert[:, :])
            nc.vector.tensor_copy(table[:, 1, :], first_row[:, :]).then_inc(s_tabled, 1)


def experts(nc, rows_dram, result_dram, table, w1, w2, b1, b2, w, sem, sb, pb):
    f32 = lambda name, *shape: sb("ex_" + name, [P, *shape], FP32)
    f32r = lambda name, *shape: sb("ex_" + name, [P, *shape], FP32R)
    HALVES, SLOTS = ROWS // P, 4
    ident, rows = f32("ident", P), f32("rows", SLOTS, HALVES, WIDTH)
    gate = f32("gate", SLOTS, HALVES)
    going, dest = (sb("ex_" + n, [P, SLOTS, HALVES], mybir.dt.uint32) for n in ("going", "dest"))
    nothing = sb("ex_nothing", [P, HALVES], mybir.dt.uint32)
    xT_hi, xT_lo = f32r("xT_hi", 2, ROWS), f32r("xT_lo", 2, ROWS)
    w1_now, w2_now, b1_now = f32r("w1_now", 2, 2 * HID), f32("w2_now", SLOTS, CH, P), f32("b1_now", 2, CH)
    hT, summed, y = f32("hT", 2, CH, ROWS), f32("summed", 2, HALVES, P), f32("y", SLOTS, HALVES, P)
    ps_t, ps_h, ps_o = [pb("t0"), pb("t1")], [pb(f"h{c}") for c in range(CH)], [pb("o0"), pb("o1")]
    names = ("ident nothing w1_hi w1_split w2_copied b1_copied meta transposed xT_hi xT_lo hidden gelu out "
             "summed scaled dest").split()
    S = {n: sem("ex_" + n) for n in names}
    s_rows = [sem(f"ex_rows_{n}") for n in range(SLOTS)]
    s_sent = [sem(f"ex_sent_{n}") for n in range(SLOTS)]
    loaded = lambda r, slot: 4 * (r - slot) + 16
    sent = lambda r, slot: HALVES * loaded(r, slot)

    AHEAD, BEHIND = 3, 7

    with nc.Block() as block:

        @block.sync
        def _(sp):
            sp.dma_start(ident[:, :], w["ident"]).then_inc(S["ident"], 16)

            def body(r, slot):
                par = slot % 2
                if live(r + 3, RUNS):
                    q = (slot + 3) % SLOTS
                    first = sp.value_load(table[0:1, 1, bass.ds(r + 3, 1)], min_val=0, max_val=E * REGION)
                    wait(sp, S["meta"], r)
                    sp.dma_start(rows[:, q, :, :], rows_dram[bass.ds(first, ROWS), :].rearrange("(h p) n -> p h n", p=P))\
                      .then_inc(s_rows[q], 16)

            pipeline(sp, -3, RUNS, body, ahead=AHEAD, behind=BEHIND, steps=RUNS, unroll=SLOTS)

        @block.gpsimd
        def _(pool):
            nc.gpsimd.memset(nothing[:, :], 0).then_inc(S["nothing"], 1)
            pool.wait_ge(S["nothing"], 1)

            def body(r, slot):
                par = slot % 2
                if live(r - 1, RUNS):
                    wait(pool, S["meta"], r)
                if live(r - 5, RUNS):
                    wait(pool, s_sent[(slot - 1) % SLOTS], sent(r - 5, (slot - 1) % SLOTS))
                wait(pool, S["dest"], r - 1)
                wait(pool, S["scaled"], HALVES * (r - 1))
                if live(r - 1, RUNS):
                    q = (slot - 1) % SLOTS
                    nc.gpsimd.tensor_tensor(dest[:, q, :], going[:, q, :], nothing[:, :], ALU.add).then_inc(S["dest"], 1)
                else:
                    nc.gpsimd.tensor_tensor(nothing[:, :], nothing[:, :], nothing[:, :], ALU.add).then_inc(S["dest"], 1)
                if live(r - 2, RUNS):
                    q = (slot - 2) % SLOTS
                    for h in range(HALVES):
                        at = bass.IndirectOffsetOnAxis(ap=dest[:, q, h:h + 1], axis=0)
                        nc.gpsimd.indirect_dma_start(result_dram, at, y[:, q, h, :], None,
                                                     bounds_check=TOPK * BATCH * SEQ - 1, oob_is_err=False)\
                          .then_inc(s_sent[q], 16)

            pipeline(pool, 1, RUNS + 2, body, ahead=AHEAD, behind=BEHIND, steps=RUNS, unroll=SLOTS)

        @block.scalar
        def _(act):
            def body(r, slot):
                par = slot % 2
                if live(r + 1, RUNS):
                    wait(act, S["transposed"], r + 2)
                    wait(act, S["hidden"], CH * r)
                    nc.scalar.copy(xT_hi[:, 1 - par, :], ps_t[1 - par][:, 0:ROWS]).then_inc(S["xT_hi"], 1)
                if live(r - 2, RUNS):
                    q = (slot - 2) % SLOTS
                    wait(act, S["summed"], r - 1)
                    if live(r - 6, RUNS):
                        wait(act, s_sent[q], sent(r - 6, q))
                    for h in range(HALVES):
                        nc.scalar.activation(y[:, q, h, :], summed[:, par, h, :], ACT.Copy, scale=gate[:, q, h:h + 1])\
                          .then_inc(S["scaled"], 1)
                if live(r, RUNS):
                    for c in range(CH):
                        wait(act, S["hidden"], CH * r + c + 1)
                        wait(act, S["out"], r - 1)
                        if c == 0:
                            wait(act, S["b1_copied"], r + 1)
                        nc.scalar.activation(hT[:, par, c, :], ps_h[c][:, 0:ROWS], ACT.Gelu_apprx_tanh,
                                             bias=b1_now[:, par, c:c + 1]).then_inc(S["gelu"], 1)

            pipeline(act, -1, RUNS + 2, body, ahead=AHEAD, behind=BEHIND, steps=RUNS, unroll=SLOTS)

        @block.vector
        def _(dve):
            tt = nc.vector.tensor_tensor

            def body(r, slot):
                par = slot % 2
                if live(r + 1, RUNS):
                    q = (slot + 1) % SLOTS
                    wait(dve, s_rows[q], loaded(r + 1, q))
                    wait(dve, S["transposed"], r + 2)
                    wait(dve, S["scaled"], HALVES * (r - 2))
                    wait(dve, S["dest"], r - 2)
                    nc.vector.tensor_copy(gate[:, q, :], rows[:, q, :, META])
                    nc.vector.tensor_copy(going[:, q, :], rows[:, q, :, META + 1]).then_inc(S["meta"], 1)
                    e = dve.value_load(table[0:1, 0, bass.ds(r + 1, 1)], min_val=0, max_val=E - 1)
                    wait(dve, S["hidden"], CH * r)
                    w1_e = w1[:, bass.ds(e, 1), :].rearrange("p a n -> p (a n)")
                    nc.vector.tensor_copy(w1_now[:, 1 - par, 0:HID], w1_e).then_inc(S["w1_hi"], 1)
                    wait(dve, S["gelu"], CH * r)
                    nc.vector.tensor_copy(b1_now[:, 1 - par, :], b1[:, bass.ds(e, 1), :].rearrange("p a n -> p (a n)"))\
                      .then_inc(S["b1_copied"], 1)
                    dve.wait_ge(S["w1_hi"], r + 2)
                    tt(w1_now[:, 1 - par, HID:2 * HID], w1_e, w1_now[:, 1 - par, 0:HID].bitcast(FP32), ALU.subtract)\
                        .then_inc(S["w1_split"], 1)
                    wait(dve, S["xT_hi"], r + 2)
                    tt(xT_lo[:, 1 - par, :], ps_t[1 - par][:, 0:ROWS], xT_hi[:, 1 - par, :].bitcast(FP32), ALU.subtract)\
                        .then_inc(S["xT_lo"], 1)
                if live(r - 2, RUNS):
                    last = dve.value_load(table[0:1, 0, bass.ds(r - 2, 1)], min_val=0, max_val=E - 1)
                    wait(dve, S["out"], r - 1)
                    wait(dve, S["scaled"], HALVES * (r - 3))
                    tt(summed[:, par, :, :], ps_o[par][:, 0:ROWS].rearrange("p (h n) -> p h n", h=HALVES),
                       b2[:, bass.ds(last, 1), :].broadcast_to([P, HALVES, P]), ALU.add).then_inc(S["summed"], 1)
                if live(r + 1, RUNS):
                    wait(dve, S["out"], r - 2)
                    nc.vector.tensor_copy(w2_now[:, q, :, :].rearrange("p c n -> p (c n)"),
                                          w2[:, bass.ds(e, 1), :].rearrange("p a n -> p (a n)")).then_inc(S["w2_copied"], 1)

            pipeline(dve, -1, RUNS + 2, body, ahead=AHEAD, behind=BEHIND, steps=RUNS, unroll=SLOTS)

        @block.tensor
        def _(pe):
            pe.wait_ge(S["ident"], 16)

            def body(r, slot):
                par = slot % 2
                if live(r + 1, RUNS):
                    q = (slot + 1) % SLOTS
                    wait(pe, s_rows[q], loaded(r + 1, q))
                    wait(pe, S["xT_lo"], r)
                    for h in range(HALVES):
                        ins = nc.tensor.transpose(ps_t[1 - par][:, h * P:(h + 1) * P], rows[:, q, h, 0:D], ident[:, :])
                    ins.then_inc(S["transposed"], 1)
                if live(r, RUNS):
                    wait(pe, S["w1_split"], r + 1)
                    wait(pe, S["xT_lo"], r + 1)
                    for c in range(CH):
                        wait(pe, S["gelu"], CH * (r - 1) + c + 1)
                        hi, lo = (w1_now[:, par, part * HID + c * P:part * HID + (c + 1) * P] for part in range(2))
                        for left, right in ((hi, xT_hi), (lo, xT_hi), (hi, xT_lo)):
                            ins = nc.tensor.matmul(ps_h[c][:, 0:ROWS], left, right[:, par, :],
                                                   start=left is hi and right is xT_hi, stop=right is xT_lo)
                        ins.then_inc(S["hidden"], 1)
                if live(r - 1, RUNS):
                    q = 1 - par
                    wait(pe, S["w2_copied"], r)
                    wait(pe, S["summed"], r - 2)
                    for h in range(HALVES):
                        for c in range(CH):
                            wait(pe, S["gelu"], CH * (r - 1) + c + 1)
                            ins = nc.tensor.matmul(ps_o[q][:, h * P:(h + 1) * P], hT[:, q, c, h * P:(h + 1) * P],
                                                   w2_now[:, (slot - 1) % SLOTS, c, :], start=(c == 0), stop=(c == CH - 1))
                    ins.then_inc(S["out"], 1)

            pipeline(pe, -1, RUNS + 1, body, ahead=AHEAD, behind=BEHIND, steps=RUNS, unroll=SLOTS)


def combine(nc, x_sb, result_dram, out_dram, sem, sb):
    PARTS = 8
    TPP = TILES // PARTS
    both = sb("co_both", [P, TILES, TOPK, D], FP32)
    s_both = [sem(f"co_loaded_{n}") for n in range(PARTS)]
    s_first, s_added, s_stored = sem("co_first_added"), sem("co_added"), sem("co_stored")
    result = result_dram[0:TOPK * BATCH * SEQ, :].rearrange("(t p k) n -> p t (k n)", p=P, k=TOPK)
    with nc.Block() as block:

        @block.sync
        def _(sp):
            for n in range(PARTS):
                tiles = slice(TPP * n, TPP * (n + 1))
                sp.dma_start(both[:, tiles, :, :].rearrange("p t k n -> p t (k n)"), result[:, tiles, :]).then_inc(s_both[n], 16)

        @block.vector
        def _(dve):
            for n in range(PARTS):
                tiles = slice(TPP * n, TPP * (n + 1))
                dve.wait_ge(s_both[n], 16)
                for k, s_done in enumerate((s_first, s_added)):
                    if k:
                        dve.wait_ge(s_first, n + 1)
                    nc.vector.tensor_tensor(x_sb[:, tiles, :], x_sb[:, tiles, :], both[:, tiles, k, :], ALU.add)\
                      .then_inc(s_done, 1)

        @block.scalar
        def _(act):
            for n in range(PARTS):
                tiles = slice(TPP * n, TPP * (n + 1))
                act.wait_ge(s_added, n + 1)
                act.dma_start(out_dram[:, tiles, :], x_sb[:, tiles, :]).then_inc(s_stored, 16)
            act.wait_ge(s_stored, 16 * PARTS)


def decoder(nc, x, w, out, phases=3):
    with ExitStack() as ctx:
        x_sb = ctx.enter_context(nc.sbuf_tensor("x_sb", [P, TILES, D], FP32))
        x_loaded = [ctx.enter_context(nc.semaphore(f"x_loaded_{s}")) for s in X_PARTS]
        x_dram = x.rearrange("b s d -> (b s) d").rearrange("(t p) d -> p t d", p=P)
        out_dram = out.rearrange("b s d -> (b s) d").rearrange("(t p) d -> p t d", p=P)
        with nc.Block() as block:
            @block.scalar
            def _(act):
                for s, end, loaded in zip(X_PARTS, X_PARTS[1:] + [STEPS], x_loaded):
                    act.dma_start(x_sb[:, TPS * s:TPS * end, :], x_dram[:, TPS * s:TPS * end, :]).then_inc(loaded, 16)
        with ExitStack() as inner:
            sem = lambda name: inner.enter_context(nc.semaphore(name))
            sb = lambda name, shape, dt: inner.enter_context(nc.sbuf_tensor(name, shape, dt))
            pb = lambda name: inner.enter_context(nc.psum_tensor("sa_" + name, [P, 512], FP32))
            self_attention(nc, x_sb, x_loaded, w, sem, sb, pb)
        rows_dram = nc.dram_tensor("rows_by_expert", (E * REGION + ROWS, WIDTH), FP32).ap()
        result_dram = nc.dram_tensor("results_by_token", (TOPK * BATCH * SEQ, D), FP32).ap()
        with ExitStack() as weights:
            keep = lambda name, shape, dt: weights.enter_context(nc.sbuf_tensor(name, shape, dt))
            table = keep("run_table", [P, 2, RUNS], mybir.dt.int32)
            filled, starts = keep("filled", [P, TPS + 1, E], FP32), keep("region_starts", [P, E], FP32)
            w1, w2 = keep("w1", [P, E, HID], FP32), keep("w2", [P, E, CH * P], FP32)
            b1, b2 = keep("b1", [P, E, CH], FP32), keep("b2", [P, E, P], FP32)
            with ExitStack() as inner:
                sem = lambda name: inner.enter_context(nc.semaphore(name))
                sb = lambda name, shape, dt: inner.enter_context(nc.sbuf_tensor(name, shape, dt))
                pb = lambda name: inner.enter_context(nc.psum_tensor("ca_" + name, [P, 512], FP32))
                cross_attention_and_routing(nc, x_sb, rows_dram, filled, starts, w1, w2, b1, b2, w, sem, sb, pb)
            with ExitStack() as inner:
                sem = lambda name: inner.enter_context(nc.semaphore(name))
                sb = lambda name, shape, dt: inner.enter_context(nc.sbuf_tensor(name, shape, dt))
                run_table(nc, rows_dram, filled, starts, table, w, sem, sb)
            with ExitStack() as inner:
                sem = lambda name: inner.enter_context(nc.semaphore(name))
                sb = lambda name, shape, dt: inner.enter_context(nc.sbuf_tensor(name, shape, dt))
                pb = lambda n: inner.enter_context(nc.psum_tensor("ex_" + n, [P, 512], FP32))
                experts(nc, rows_dram, result_dram, table, w1, w2, b1, b2, w, sem, sb, pb)
        with ExitStack() as inner:
            sem = lambda name: inner.enter_context(nc.semaphore(name))
            sb = lambda name, shape, dt: inner.enter_context(nc.sbuf_tensor(name, shape, dt))
            combine(nc, x_sb, result_dram, out_dram, sem, sb)


def laid_out(inputs):
    import numpy as np
    import math
    f = np.float32
    arrays = {}
    wq, wk, wv, wo = (np.asarray(inputs[f"L0_attn_{n}"]) for n in ("Wq", "Wk", "Wv", "Wo"))
    q = np.zeros((D, HG, 4, G1, HD1), f)
    q[:, :, 0:3] = wq.reshape(D, G1, HG, HD1).transpose(0, 2, 1, 3)[:, :, None]
    arrays["sa_wq"] = q.reshape(D, HG * P)
    k = np.zeros((D, G1, 4, G1, HD1), f)
    for g in range(G1):
        k[:, g, 0:3, g] = wk.reshape(D, G1, HD1)[:, None, g]
    arrays["sa_wk"] = k.reshape(D, G1 * P)
    v = np.zeros((D, P), f)
    v[:, 0:32] = wv
    arrays["sa_wv"] = v
    arrays["sa_wo"] = np.ascontiguousarray(wo.reshape(G1, HG, HD1, D).transpose(1, 0, 2, 3).reshape(P, D))
    arrays["ident"] = np.eye(P, dtype=f)
    start = 2.0 ** (-2.0 ** (-(math.log2(H1) - 3)))
    slopes = np.array([start * start ** i for i in range(H1)], dtype=f).reshape(G1, HG)
    high = (slopes.view(np.uint32) & np.uint32(0xFFFFF000)).view(f)
    parts = np.stack([high, slopes - high], 1)
    q_rows = np.zeros((P, STEP, HG, SEQ), f)
    q_rows[ALIBI_ROW:ALIBI_ROW + 2 * G1] = parts.reshape(2 * G1, 1, HG, 1)
    k_rows = np.zeros((P, STEP, G1, SEQ), f)
    z = np.zeros((2, SEQ, 2, 2, P), f)
    ones = np.zeros((2, SEQ, 2, G1, HD1), f)
    for g in range(G1):
        k_rows[MAX_ROW + g, :, g] = 1.0
        k_rows[ALIBI_ROW + 2 * g:ALIBI_ROW + 2 * g + 2, :, g] = np.arange(SEQ, dtype=f)
        ones[g % 2, :, g // 2, g] = 1.0
        for part in range(2):
            z[:, :, :, :, ALIBI_ROW + 2 * g + part] = parts[g, part].reshape(2, 2).T[:, None, None, :]
    arrays["sa_q_rows"], arrays["sa_k_rows"] = q_rows.reshape(P, -1), k_rows.reshape(P, -1)
    arrays["sa_z"], arrays["sa_ones"] = z.reshape(P, 2, 2, P), ones.reshape(P, 2, 32)
    wq, wk, wv, wo = (np.asarray(inputs[f"L0_xattn_{n}"]) for n in ("Wq", "Wk", "Wv", "Wo"))
    for name, a in (("ca_wqT", wq), ("ca_wkT", wk)):
        arrays[name] = a.reshape(H2 // 2, 2, D, HD2).transpose(1, 3, 0, 2).reshape(P, H2 // 2, D)
    arrays["ca_wv"] = wv.transpose(1, 0, 2).reshape(D, H2 * HD2)
    arrays["ca_wo"] = wo.reshape(2, 2, 2, 2, HD2, D).transpose(2, 4, 0, 1, 3, 5).reshape(P, 8, D)
    key, query = np.arange(P)[:, None] % SEQ, np.arange(HALF * SEQ)[None] % SEQ
    arrays["ca_mask"] = np.where(key > query, f(-1e30), f(0))
    pick = np.zeros((P, P), f)
    pick[0, 0:SEQ] = pick[1, SEQ:P] = 1.0
    arrays["ca_pick"] = pick
    arrays["ctxT"] = np.asarray(inputs["ctx_1024"]).reshape(BATCH * SEQ, D).T
    wg = np.zeros((D, P), f)
    wg[:, 0:E] = inputs["L0_ffn_Wg"]
    arrays["ff_wg"] = wg
    bcast = lambda a, *shape: np.broadcast_to(np.asarray(a, f), (P, *shape))
    arrays["ff_bg"] = bcast(inputs["L0_ffn_bg"], TPS, E)
    arrays["ff_index"] = bcast(np.arange(E), E)
    arrays["ff_dest"] = (TOPK * (P * np.arange(TILES)[None, :, None] + np.arange(P)[:, None, None])
                         + np.arange(TOPK)).astype(f)
    arrays["ff_starts"] = bcast(REGION * np.arange(E), E)
    arrays["ff_thresholds"] = bcast(ROWS * np.arange(FULL), E, FULL)
    arrays["ff_upto"] = bcast(np.tri(E), E, E)
    arrays["ff_run_no"] = bcast(np.arange(RUNS), RUNS)
    arrays["ff_tri"] = np.triu(np.ones((P, P), f), 1)
    pad = np.zeros((P, ROWS // P, WIDTH), f)
    pad[:, :, META + 1] = TOPK * BATCH * SEQ + np.arange(ROWS).reshape(-1, P).T
    arrays["ff_pad"] = pad
    arrays["ff_w1"] = np.asarray(inputs["L0_ffn_W1"]).transpose(1, 0, 2)
    arrays["ff_w2"] = np.asarray(inputs["L0_ffn_W2"]).reshape(E, CH, P, D).transpose(2, 0, 1, 3).reshape(P, E, CH * P)
    arrays["ff_b1"] = np.asarray(inputs["L0_ffn_b1"]).reshape(E, CH, P).transpose(2, 0, 1)
    arrays["ff_b2"] = bcast(inputs["L0_ffn_b2"], E, P)
    return arrays


def kernel(**inputs):
    import numpy as _np
    import concourse.bacc as _bacc
    from concourse import mybir as _mybir
    from concourse.bass_utils import run_bass_kernel_spmd as _run

    nc = _bacc.Bacc("TRN2", target_bir_lowering=False, num_devices=1)
    arrays = {"in_x": _np.ascontiguousarray(inputs["x"])}
    arrays.update((f"in_{n}", _np.ascontiguousarray(a)) for n, a in laid_out(inputs).items())
    aps = {n: nc.dram_tensor(n, a.shape, _mybir.dt.from_np(a.dtype), kind="ExternalInput").ap() for n, a in arrays.items()}
    out = nc.dram_tensor("out_x", (BATCH, SEQ, D), FP32, kind="ExternalOutput").ap()
    decoder(nc, aps.pop("in_x"), {n[3:]: a for n, a in aps.items()}, out)
    r = _run(nc, [arrays], core_ids=[0])
    return r.results[0]["out_x"]
```

```python
import concourse.bass as bass
from concourse import mybir
from contextlib import ExitStack

FP32 = mybir.dt.float32
FP32R = mybir.dt.float32r
BF16 = mybir.dt.bfloat16
ALU = mybir.AluOpType
ACT = mybir.ActivationFunctionType
AX = mybir.AxisListType

P = 128
BATCH, SEQ, D = 64, 64, 128
STEP = 4
TOK = STEP * SEQ
TPS = TOK // P
STEPS = BATCH // STEP
TILES = BATCH * SEQ // P
EPS = 1e-5
X_PARTS = [0, 1, 2, 3]

H2, HD2 = 16, 64
HALF = H2 // 2
VW = HD2 + 1

H1, G1, HD1 = 16, 4, 8
HG = H1 // G1
MAX_ROW, ALIBI_ROW = 96, 100


E, HID = 8, 512
CH = HID // P
TOPK = 2
ROWS = 2 * P
REGION = BATCH * SEQ + ROWS
RUNS = (TOPK * BATCH * SEQ + E * (ROWS - 1)) // ROWS
FULL = BATCH * SEQ // ROWS
META = D
WIDTH = D + 2


def live(i, n):
    return not isinstance(i, int) or 0 <= i < n


def wait(eng, sem, value):
    if not isinstance(value, int) or value > 0:
        eng.wait_ge(sem, value)


def cap(count, n):
    return min(count, n) if isinstance(count, int) else count


def pipeline(eng, first, last, body, ahead=2, behind=2, steps=STEPS, unroll=2):
    lo = -(-behind // unroll) * unroll
    hi = (steps - ahead) // unroll * unroll
    for s in range(first, lo):
        body(s, s % unroll)
    with eng.Fori(lo // unroll, hi // unroll) as turn:
        for n in range(unroll):
            body(unroll * turn + n, n)
    for s in range(hi, last):
        body(s, s % unroll)


class Later:

    def __init__(self, keep):
        f32 = lambda name, *shape: keep(name, [P, *shape], FP32)
        f32r = lambda name, *shape: keep(name, [P, *shape], FP32R)
        bf16 = lambda name, *shape: keep(name, [P, *shape], BF16)
        self.ident = f32("ident", P)
        self.a_hi = f32r("ca_a_hi", H2, P)
        self.a_lo = f32r("ca_a_lo", H2, P)
        self.wv_hi = f32r("ca_wv_hi", H2 * HD2)
        self.wv_lo = f32r("ca_wv_lo", H2 * HD2)
        self.wo = f32("ca_wo", 8, P)
        self.mask = f32("ca_mask", HALF * SEQ)
        self.own = f32("ca_own", 4, P)
        self.pick = f32r("ca_pick", P)
        self.v_bd = f32("ca_v_bd", 2, TPS, H2, 2, VW)
        self.rows = f32r("ca_rows", 2, HALF * SEQ)
        self.wg = f32("ro_wg", P)
        self.bg = f32("ro_bg", TPS, E)
        self.index = f32("ro_index", E)
        self.dest = f32("ro_dest", TILES, TOPK)
        self.tri = bf16("ro_tri", P)
        self.ones = bf16("ro_ones", P)
        self.thresholds, self.upto = f32("rt_thresholds", E, FULL), f32("rt_upto", E, E)
        self.run_no, self.pad = f32("rt_run_no", RUNS), f32("rt_pad", ROWS // P, WIDTH)
        self.table = keep("rt_table", [P, 2, RUNS], mybir.dt.int32)
        self.filled = f32("ro_filled", TPS + 1, E)
        self.starts = f32("ro_starts", E)


def self_attention(nc, x_sb, x_dram, x_loaded, later, w, sem, sb, pb):
    f32 = lambda name, *shape: sb(name, [P, *shape], FP32)
    f32r = lambda name, *shape: sb(name, [P, *shape], FP32R)

    wq_raw, wk_raw = f32("sa_wq_raw", HG * P), f32("sa_wk_raw", G1 * P)
    wq_hi, wq_lo = f32r("sa_wq_hi", HG, P), f32r("sa_wq_lo", HG, P)
    wk_hi, wk_lo = f32r("sa_wk_hi", G1, P), f32r("sa_wk_lo", G1, P)
    wv, wo = f32("sa_wv", P), f32("sa_wo", P)
    ident, ones_gd = later.ident, f32("sa_ones", 2, 32)
    q_rows, k_rows = f32("sa_q_rows", STEP * HG * SEQ), f32("sa_k_rows", STEP * G1 * SEQ)
    half, eps = f32("sa_half", TPS), f32("sa_eps", TPS)
    zeros = f32("sa_zeros", STEP * HG * SEQ)
    stats, mean_var = f32("sa_stats", 2, TPS, 6), f32("sa_mean_var", 2, TPS, 2)
    var_eps, rstd = f32("sa_var_eps", TPS), f32("sa_rstd", 2, TPS)
    xn = f32("sa_xn", 2, TPS, P)
    xT, xT_hi, xT_lo = f32("sa_xT", 2, TOK), f32r("sa_xT_hi", 2, TOK), f32r("sa_xT_lo", 2, TOK)
    q_st = f32r("sa_q_st", 2, STEP, HG, SEQ)
    k_st = f32r("sa_k_st", 2, STEP, G1, SEQ)
    v_bd = f32("sa_v_bd", 2, STEP, 96)
    z = f32("sa_z", 2, 2, P)
    probs = f32("sa_probs", 2, 2, HG * SEQ)
    recip, att = f32("sa_recip", HG * SEQ), f32("sa_att", 2, HG, SEQ)
    attT = f32("sa_attT", 2, TOK)

    ps_t = pb("ps_t")
    ps_proj = [pb("ps_proj0"), pb("ps_proj1")]
    ps_s, ps_z, ps_st = pb("ps_s"), pb("ps_z"), pb("ps_st")
    ps_pv = [pb("ps_pv0"), pb("ps_pv1")]

    s_wload = sem("sa_weights_loaded")
    s_prep = sem("sa_weights_split")
    s_zero = sem("sa_zeroed")
    s_stats, s_aggr = sem("sa_stats_done"), sem("sa_mean_var_done")
    s_vare, s_rstd, s_xn = sem("sa_var_eps_done"), sem("sa_rstd_done"), sem("sa_xn_done")
    s_T, s_V, s_proj = sem("sa_transposed"), sem("sa_v_product"), sem("sa_qk_product")
    s_xTf, s_xThi, s_xTlo = sem("sa_xT_copied"), sem("sa_xT_hi_done"), sem("sa_xT_lo_done")
    s_vbd = sem("sa_v_placed")
    s_hi, s_lo = sem("sa_qk_hi_done"), sem("sa_qk_lo_done")
    s_S, s_max, s_Z, s_rows = sem("sa_scores"), sem("sa_max"), sem("sa_max_transposed"), sem("sa_max_rows")
    s_ST, s_exp, s_PV = sem("sa_scoresT"), sem("sa_exp_done"), sem("sa_pv_product")
    s_rec, s_att = sem("sa_reciprocal"), sem("sa_normalised")
    s_move = [sem("sa_att_moved_even"), sem("sa_att_moved_odd")]
    s_out = [sem("sa_att_out_even"), sem("sa_att_out_odd")]
    moved = lambda s, par: 8 * (s - par) + 16
    by_batch, by_head = [], []
    for n in ("even", "odd"):
        scratch = nc.dram_tensor(f"sa_scratch_{n}", (HG, 32, STEP, SEQ), FP32).ap()
        by_batch.append(scratch.rearrange("h r b q -> r h b q"))
        by_head.append(scratch.rearrange("h r b q -> (h r) (b q)"))
    s_Wo, s_res, s_reset = sem("sa_out_product"), sem("sa_residual"), sem("sa_max_rows_reset")

    wqT, wkT, wv_raw = f32("ca_wqT", H2 // 2, P), f32("ca_wkT", H2 // 2, P), f32("ca_wv_raw", H2 * HD2)
    pick_raw, tri_raw = f32("ca_pick_raw", P), f32("ro_tri_raw", P)
    a_raw = f32("ca_a_raw", 4 * P)
    s_later, s_cleared, s_conv = sem("later_loaded"), sem("later_cleared"), sem("later_converted")
    s_aprod, s_ascaled, s_asplit = sem("ca_a_product"), sem("ca_a_scaled"), sem("ca_a_split")
    s_split = sem("sa_qk_weights_split")
    s_qk, s_rest = sem("sa_qk_weights_loaded"), sem("sa_constant_rows")

    LOADS, LATER = 7, 17

    with nc.Block() as block:

        @block.sync
        def _(sp):
            for dst, src in ((wq_raw[:, :], w["sa_wq"]), (wk_raw[:, :], w["sa_wk"])):
                sp.dma_start(dst, src).then_inc(s_qk, 16)
            for dst, src in ((ident[:, :], w["ident"]), (z[:, :, :, :], w["sa_z"]),
                             (q_rows[MAX_ROW:P, :], w["sa_q_rows"][MAX_ROW:P, :]),
                             (k_rows[MAX_ROW:P, :], w["sa_k_rows"][MAX_ROW:P, :]), (wv[:, :], w["sa_wv"]),
                             (ones_gd[:, :, :], w["sa_ones"]), (wo[:, :], w["sa_wo"])):
                sp.dma_start(dst, src).then_inc(s_wload, 16)
            rest = slice(TPS * X_PARTS[-1], TILES)
            sp.dma_start(x_sb[:, rest, :], x_dram[:, rest, :]).then_inc(x_loaded[-1], 16)
            for dst, src in ((wqT[:, :, :], w["ca_wqT"]), (wkT[:, :, :], w["ca_wkT"]), (wv_raw[:, :], w["ca_wv"]),
                             (later.mask[:, :], w["ca_mask"]), (later.own[0:8, :, :], w["ca_own"]),
                             (pick_raw[:, :], w["ca_pick"]),
                             (later.wo[:, :, :], w["ca_wo"]), (later.wg[:, :], w["ff_wg"]),
                             (later.bg[:, :, :], w["ff_bg"]), (later.index[:, :], w["ff_index"]),
                             (later.dest[:, :, :], w["ff_dest"]), (later.starts[:, :], w["ff_starts"]),
                             (tri_raw[:, :], w["ff_tri"]), (later.thresholds[:, :, :], w["ff_thresholds"]),
                             (later.upto[:, :, :], w["ff_upto"]), (later.run_no[:, :], w["ff_run_no"]),
                             (later.pad[:, :, :], w["ff_pad"])):
                sp.dma_start(dst, src).then_inc(s_later, 16)

            def body(s, par):
                if live(s - 1, STEPS):
                    wait(sp, s_att, s)
                    for b in range(STEP):
                        sp.dma_start(by_batch[1 - par][:, :, b, :], att[32 * b:32 * b + 32, 1 - par, :, :])\
                          .then_inc(s_out[1 - par], 16)
                    wait(sp, s_out[1 - par], STEP * moved(s - 1, 1 - par))
                    sp.dma_start(attT[:, 1 - par, :], by_head[1 - par]).then_inc(s_move[1 - par], 16)

            pipeline(sp, 1, STEPS + 1, body)

        @block.gpsimd
        def _(pool):
            nc.gpsimd.memset(half[:, :], -0.5).then_inc(s_zero, 1)
            nc.gpsimd.memset(v_bd[:, :, :, :], 0.0).then_inc(s_zero, 1)
            nc.gpsimd.memset(eps[:, :], EPS).then_inc(s_zero, 1)
            nc.gpsimd.memset(zeros[:, :], 0.0).then_inc(s_zero, 1)
            pool.wait_ge(s_zero, 4)
            def constant_rows():
                pool.wait_ge(s_wload, 16 * LOADS)
                for st, rows in ((q_st, q_rows), (k_st, k_rows)):
                    nc.gpsimd.tensor_tensor(st[MAX_ROW:P, 1, :, :, :].rearrange("p b h q -> p (b h q)"), rows[MAX_ROW:P, :],
                                            zeros[MAX_ROW:P, :], ALU.add).then_inc(s_rest, 1)
                pool.wait_ge(s_rest, 2)

            def body(s, par):
                if live(s + 2, STEPS):
                    wait(pool, s_aggr, s + 3)
                    wait(pool, s_rstd, s + 2)
                    wait(pool, s_reset, s - 1)
                    nc.gpsimd.tensor_tensor(var_eps[:, :], mean_var[:, par, :, 1], eps[:, :], ALU.add).then_inc(s_vare, 1)
                    pool.wait_ge(s_vare, s + 3)
                    nc.gpsimd.tensor_tensor(rstd[:, par, :], var_eps[:, :], half[:, :], ALU.pow).then_inc(s_rstd, 1)
                if isinstance(s, int) and s == -1:
                    pool.wait_ge(s_rstd, 2)
                    constant_rows()
                if live(s - 1, STEPS) and live(s + 1, STEPS):
                    wait(pool, s_ST, STEP * s)
                    if live(s + 2, STEPS):
                        wait(pool, s_rstd, s + 3)
                    wait(pool, s_reset, s - 1)
                    nothing = zeros[MAX_ROW:ALIBI_ROW, :]
                    nc.gpsimd.tensor_tensor(q_st[MAX_ROW:ALIBI_ROW, 1 - par, :, :, :].rearrange("p b h q -> p (b h q)"),
                                            nothing, nothing, ALU.add).then_inc(s_reset, 1)

            pipeline(pool, -2, STEPS, body)
            pool.wait_ge(s_reset, STEPS - 2)
            nc.gpsimd.memset(later.v_bd[:, :, :, :, :, :], 0.0).then_inc(s_cleared, 1)
            nc.gpsimd.memset(later.rows[0:64, :, :].bitcast(FP32), 0.0).then_inc(s_cleared, 1)
            pool.wait_ge(s_cleared, 2)
            for b in range(2):
                nc.gpsimd.memset(later.v_bd[64 * b:64 * b + 64, :, :, :, b, HD2:VW], 1.0).then_inc(s_cleared, 1)

        @block.scalar
        def _(act):
            def constant_rows():
                act.wait_ge(s_wload, 16 * LOADS)
                for st, rows in ((q_st, q_rows), (k_st, k_rows)):
                    nc.scalar.copy(st[MAX_ROW:P, 0, :, :, :].rearrange("p b h q -> p (b h q)"),
                                   rows[MAX_ROW:P, :]).then_inc(s_prep, 1)

            def high_part(s, par, b):
                wait(act, s_proj, STEP * (s + 1) + b + 1)
                if b == 0:
                    wait(act, s_ST, STEP * s)
                st = (q_st, k_st)[b // 2]
                dst = st[0:96, 1 - par, :, 2 * (b % 2):2 * (b % 2) + 2, :].rearrange("p b h q -> p h b q")
                nc.scalar.copy(dst, ps_proj[b % 2][0:96, :].rearrange("p (h b q) -> p h b q", h=2, b=STEP))\
                  .then_inc(s_hi, 1)

            def slot(s, par, b):
                n = STEP * s + b
                if live(n - 2, BATCH):
                    wait(act, s_ST, n - 1)
                    nc.scalar.activation(probs[:, b % 2, :, :].rearrange("p g n -> p (g n)"), ps_st[:, :],
                                         ACT.Exp).then_inc(s_exp, 1)
                if live(n - 1, BATCH):
                    buf = par if b else 1 - par
                    wait(act, s_Z, n)
                    nc.scalar.copy(q_st[MAX_ROW:P, buf, (b - 1) % STEP, :, :].rearrange("p h q -> p (h q)"),
                                   ps_z[MAX_ROW:P, 0:256]).then_inc(s_rows, 1)
                if live(s + 1, STEPS):
                    for unit in ((), (0, 1), (2,), (3,))[b]:
                        high_part(s, par, unit)
                if b == 1 and live(s + 1, STEPS):
                    wait(act, s_V, s + 2)
                    if isinstance(s, int) and s == -1:
                        act.wait_ge(s_zero, 4)
                    for g2 in range(2):
                        src = ps_t[64 * g2:64 * g2 + 64, :].rearrange("p (b r) -> p b r", b=STEP)[:, :, 0:32]
                        src = src.rearrange("p b (g c) -> p b g c", g=2)[:, :, :, HD1 * g2:HD1 * g2 + HD1]
                        dst = v_bd[64 * g2:64 * g2 + 64, 1 - par, :, :].rearrange("p b (g c) -> p b g c", g=2)
                        nc.scalar.copy(dst[:, :, :, HD1 * g2:HD1 * g2 + HD1], src).then_inc(s_vbd, 1)
                if b == 2 and live(s + 2, STEPS):
                    wait(act, s_T, s + 3)
                    nc.scalar.copy(xT[:, par, :], ps_t[:, 0:TOK]).then_inc(s_xTf, 1)
                    nc.scalar.copy(xT_hi[:, par, :], ps_t[:, 0:TOK]).then_inc(s_xThi, 1)

            def body(s, par):
                for b in range(STEP):
                    slot(s, par, b)
                if isinstance(s, int) and s == -2:
                    constant_rows()

            pipeline(act, -2, STEPS + 1, body)
            act.wait_ge(s_later, 16 * LATER)
            nc.scalar.copy(later.wv_hi[:, :], wv_raw[:, :]).then_inc(s_conv, 1)
            for c in range(4):
                act.wait_ge(s_aprod, c + 1)
                wait(act, s_asplit, 2 * c)
                nc.scalar.mul(a_raw[:, :], ps_proj[c % 2][:, :], HD2 ** -0.5).then_inc(s_ascaled, 1)
            for dst, src in ((later.pick, pick_raw), (later.tri, tri_raw)):
                nc.scalar.copy(dst[:, :], src[:, :]).then_inc(s_conv, 1)
            for buf in range(2):
                nc.scalar.copy(later.rows[64:P, buf, :], later.mask[64:P, :]).then_inc(s_conv, 1)

        @block.vector
        def _(dve):
            def split_weights():
                dve.wait_ge(s_qk, 32)
                flat = lambda t: t[:, :, :].rearrange("p a n -> p (a n)")
                for n, (raw, hi, lo, scale) in enumerate(((wq_raw, wq_hi, wq_lo, HD1 ** -0.5), (wk_raw, wk_hi, wk_lo, 1.0))):
                    nc.vector.tensor_scalar(raw[:, :], raw[:, :], scale, None, ALU.mult).then_inc(s_split, 1)
                    dve.wait_ge(s_split, 3 * n + 1)
                    nc.vector.tensor_copy(flat(hi), raw[:, :]).then_inc(s_split, 1)
                    dve.wait_ge(s_split, 3 * n + 2)
                    nc.vector.tensor_tensor(flat(lo), raw[:, :], flat(hi).bitcast(FP32), ALU.subtract).then_inc(s_split, 1)

            def fold_weights():
                dve.wait_ge(s_conv, 1)
                dve.wait_ge(s_later, 16 * LATER)
                nc.vector.tensor_tensor(later.wv_lo[:, :], wv_raw[:, :], later.wv_hi[:, :].bitcast(FP32), ALU.subtract)
                nc.vector.memset(later.ones[:, :], 1.0)
                nc.vector.tensor_copy(later.filled[:, 0, :], later.starts[:, :])
                for c in range(4):
                    dve.wait_ge(s_ascaled, c + 1)
                    heads = lambda t: t[:, :, :].rearrange("p (a b) n -> p a b n", b=2)[:, 4 * (c // 2):4 * (c // 2) + 4, c % 2, :]
                    full = a_raw[:, :].rearrange("p (a n) -> p a n", a=4)
                    nc.vector.tensor_copy(heads(later.a_hi), full).then_inc(s_asplit, 1)
                    dve.wait_ge(s_asplit, 2 * c + 1)
                    nc.vector.tensor_tensor(heads(later.a_lo), full, heads(later.a_hi).bitcast(FP32), ALU.subtract)\
                        .then_inc(s_asplit, 1)

            def slot(s, par, b):
                n = STEP * s + b
                if b == 1 and live(s + 2, STEPS):
                    dve.wait_ge(s_stats, s + 3)
                def low_part(b):
                    st, rows, j = (q_st, k_st)[b // 2], (64, 32)[b // 2], b % 2
                    wait(dve, s_hi, STEP * (s + 1) + b + 1)
                    dst = st[rows:rows + 32, 1 - par, :, 2 * j:2 * j + 2, :].rearrange("p b h q -> p h b q")
                    nc.vector.tensor_tensor(dst, ps_proj[j][rows:rows + 32, :].rearrange("p (h b q) -> p h b q", h=2, b=STEP),
                                            dst.bitcast(FP32), ALU.subtract).then_inc(s_lo, 1)

                def maxima():
                    if live(n, BATCH):
                        wait(dve, s_S, n + 1)
                        nc.vector.tensor_reduce(z[:, b % 2, :, MAX_ROW:MAX_ROW + G1],
                                                ps_s[:, :].rearrange("p (a g k) -> p a g k", a=2, g=G1),
                                                axis=AX.X, op=ALU.max, negate=True).then_inc(s_max, 1)

                maxima()
                if b == 1 and live(s + 1, STEPS):
                    low_part(0)
                if b == 1 and live(s + 2, STEPS):
                    for t in range(TPS):
                        ins = nc.vector.bn_aggr(mean_var[:, par, t, :], stats[:, par, t, :])
                    ins.then_inc(s_aggr, 1)
                if b == 0 and live(s + 2, STEPS):
                    if isinstance(s, int) and s + 2 in X_PARTS:
                        dve.wait_ge(x_loaded[X_PARTS.index(s + 2)], 16)
                    for t in range(TPS):
                        ins = nc.vector.bn_stats(stats[:, par, t, :], x_sb[:, bass.ds(TPS * (s + 2) + t, 1), :].rearrange("p a n -> p (a n)"))
                    ins.then_inc(s_stats, 1)
                if b == 0 and live(s - 3, STEPS):
                    wait(dve, s_Wo, s - 2)
                    rows = x_sb[:, bass.ds(TPS * (s - 3), TPS), :]
                    nc.vector.tensor_tensor(rows, ps_t[:, 0:TOK].rearrange("p (t n) -> p t n", t=TPS), rows, ALU.add)\
                      .then_inc(s_res, 1)
                if b == 2 and live(s + 2, STEPS):
                    wait(dve, s_rstd, s + 3)
                    for t in range(TPS):
                        ins = nc.vector.tensor_scalar(xn[:, par, t, :], x_sb[:, bass.ds(TPS * (s + 2) + t, 1), :].rearrange("p a n -> p (a n)"),
                                                      mean_var[:, par, t, 0:1], rstd[:, par, t:t + 1],
                                                      ALU.subtract, ALU.mult)
                    ins.then_inc(s_xn, 1)
                if b == 3 and live(s + 2, STEPS):
                    wait(dve, s_xThi, s + 3)
                    wait(dve, s_xTf, s + 3)
                    nc.vector.tensor_tensor(xT_lo[:, par, :], xT[:, par, :], xT_hi[:, par, :].bitcast(FP32),
                                            ALU.subtract).then_inc(s_xTlo, 1)
                if b and live(s + 1, STEPS):
                    low_part(b)
                if b in (1, 2) and live(s - 1, STEPS):
                    wait(dve, s_PV, STEP * s)
                    cols = slice(P * (b - 1), P * b)
                    nc.vector.reciprocal(recip[:, cols], ps_pv[1 - par][:, 256:512][:, cols]).then_inc(s_rec, 1)
                if b == 2 and live(s - 1, STEPS):
                    wait(dve, s_rec, 2 * s)
                    nc.vector.tensor_tensor(att[:, 1 - par, :, :].rearrange("p h q -> p (h q)"), ps_pv[1 - par][:, 0:256],
                                            recip[:, :], ALU.mult).then_inc(s_att, 1)

            def body(s, par):
                for b in range(STEP):
                    slot(s, par, b)
                    if isinstance(s, int) and s == -2 and b == 1:
                        split_weights()
                if isinstance(s, int) and s == -1:
                    dve.wait_ge(s_wload, 16 * LOADS)
                if isinstance(s, int) and s == STEPS + 1:
                    fold_weights()

            pipeline(dve, -2, STEPS + 3, body, 2, 4)

        @block.tensor
        def _(pe):
            pe.wait_ge(s_wload, 16 * LOADS)

            def fold_weights():
                pe.wait_ge(s_later, 16 * LATER)
                pe.wait_ge(s_lo, STEP * STEPS)
                for c in range(4):
                    wait(pe, s_ascaled, c - 1)
                    for j in range(4):
                        pair, r = 4 * (c // 2) + j, slice(64 * (c % 2), 64 * (c % 2) + 64)
                        ins = nc.tensor.matmul(ps_proj[c % 2][:, j * P:(j + 1) * P], wqT[r, pair, :], wkT[r, pair, :],
                                               start=True, stop=True)
                    ins.then_inc(s_aprod, 1)

            def slot(s, par, b):
                if isinstance(s, int) and s == -1 and b == 0:
                    pe.wait_ge(s_split, 6)
                if isinstance(s, int) and s == 0 and b == 0:
                    pe.wait_ge(s_prep, 2)
                    pe.wait_ge(s_rest, 2)
                n = STEP * s + b
                prev = par if b else 1 - par
                if live(n - 1, BATCH):
                    wait(pe, s_max, n)
                    for a in range(2):
                        ins = nc.tensor.transpose(ps_z[:, a * P:(a + 1) * P], z[:, (b - 1) % 2, a, :], ident[:, :])
                    ins.then_inc(s_Z, 1)
                if live(n, BATCH):
                    wait(pe, s_lo, STEP * (s + 1))
                    wait(pe, s_reset, s - 1)
                    for a in range(2):
                        ins = nc.tensor.matmul(ps_s[:, a * 256:(a + 1) * 256],
                                               q_st[:, par, b, 2 * a:2 * a + 2, :].rearrange("p h q -> p (h q)"),
                                               k_st[:, par, b, :, :].rearrange("p g k -> p (g k)"), start=True, stop=True)
                    ins.then_inc(s_S, 1)
                if live(s + 1, STEPS):
                    wait(pe, s_xTlo, s + 2)
                    wait(pe, s_lo, n + STEP - 1)
                    hi, lo = ((wq_hi, wq_lo), (wk_hi, wk_lo))[b // 2]
                    for j in range(2):
                        h = 2 * (b % 2) + j
                        out = ps_proj[b % 2][:, j * TOK:(j + 1) * TOK]
                        nc.tensor.matmul(out, hi[:, h, :], xT_hi[:, 1 - par, :], start=True, stop=False)
                        nc.tensor.matmul(out, lo[:, h, :], xT_hi[:, 1 - par, :], start=False, stop=False)
                        ins = nc.tensor.matmul(out, hi[:, h, :], xT_lo[:, 1 - par, :], start=False, stop=True)
                    ins.then_inc(s_proj, 1)
                if live(n - 2, BATCH):
                    m, owner = (b - 2) % STEP, par if b >= 2 else 1 - par
                    wait(pe, s_exp, n - 1)
                    if b == 2:
                        wait(pe, s_att, s - 1)
                    rows = slice(32 * m, 32 * m + 32)
                    for out, weights in ((0, v_bd[:, owner, m, :]), (256, ones_gd[:, :, :].rearrange("p g c -> p (g c)"))):
                        for gp in range(2):
                            ins = nc.tensor.matmul(ps_pv[owner][rows, out:out + 256], weights[:, 32 * gp:32 * gp + 32],
                                                   probs[:, m % 2, gp, :], start=(gp == 0), stop=(gp == 1),
                                                   tile_position=(0, 32 * m), skip_group_check=True)
                    ins.then_inc(s_PV, 1)
                if b == 1 and live(s + 1, STEPS):
                    wait(pe, s_xTf, s + 2)
                    wait(pe, s_xThi, s + 2)
                    wait(pe, s_res, s - 2)
                    for m in range(STEP):
                        for g2 in range(2):
                            ins = nc.tensor.matmul(ps_t[64 * g2:64 * g2 + 64, m * P:(m + 1) * P],
                                                   xT[:, 1 - par, m * SEQ:(m + 1) * SEQ], wv[:, :], start=True, stop=True)
                    ins.then_inc(s_V, 1)
                if b == 2 and live(s + 2, STEPS):
                    wait(pe, s_xn, s + 3)
                    wait(pe, s_vbd, 2 * (s + 2))
                    for t in range(TPS):
                        ins = nc.tensor.transpose(ps_t[:, t * P:(t + 1) * P], xn[:, par, t, :], ident[:, :])
                    ins.then_inc(s_T, 1)
                if b == 3 and live(s - 2, STEPS):
                    wait(pe, s_move[par], moved(s - 2, par))
                    wait(pe, s_res, s - 2)
                    wait(pe, s_xTf, cap(s + 3, STEPS))
                    wait(pe, s_xThi, cap(s + 3, STEPS))
                    for t in range(TPS):
                        ins = nc.tensor.matmul(ps_t[:, t * P:(t + 1) * P], attT[:, par, t * P:(t + 1) * P], wo[:, :],
                                               start=True, stop=True)
                    ins.then_inc(s_Wo, 1)
                if live(n - 1, BATCH):
                    wait(pe, s_rows, n)
                    wait(pe, s_exp, n - 1)
                    for gp in range(2):
                        ins = nc.tensor.matmul(ps_st[:, gp * 256:(gp + 1) * 256],
                                               k_st[:, prev, (b - 1) % STEP, 2 * gp:2 * gp + 2, :].rearrange("p g k -> p (g k)"),
                                               q_st[:, prev, (b - 1) % STEP, :, :].rearrange("p h q -> p (h q)"),
                                               start=True, stop=True)
                    ins.then_inc(s_ST, 1)

            def body(s, par):
                for b in range(STEP):
                    slot(s, par, b)
                if isinstance(s, int) and s == STEPS:
                    fold_weights()

            pipeline(pe, -2, STEPS + 2, body, 2, 4)


def cross_attention_and_routing(nc, x_sb, rows_dram, later, w1, w2, b1, b2, w, sem, sb, pb):
    f32 = lambda name, *shape: sb("ca_" + name, [P, *shape], FP32)
    f32r = lambda name, *shape: sb("ca_" + name, [P, *shape], FP32R)

    a_hi, a_lo, wv_hi, wv_lo, wo = later.a_hi, later.a_lo, later.wv_hi, later.wv_lo, later.wo
    ident, mask, own, pick = later.ident, later.mask, later.own, later.pick
    v_bd, rows = later.v_bd, later.rows
    keys = f32("keys", 2, TOK)
    ctx_hi, ctx_lo = f32r("ctx_hi", 2, TOK), f32r("ctx_lo", 2, TOK)
    half, eps, zeros = f32("half", TPS), f32("eps", TPS), f32("zeros", TOK)
    stats, mean_var = f32("stats", 2, TPS, 6), f32("mean_var", 2, TPS, 2)
    var_eps, rstd = f32("var_eps", TPS), f32("rstd", 2, TPS)
    xn = f32("xn", 2, TPS, P)
    xT_hi, xT_lo = f32r("xT_hi", 2, TOK), f32r("xT_lo", 2, TOK)
    t_all = f32("t", 2, H2, TOK)
    raw = f32("raw", 2, HALF * SEQ)
    neg_max = f32("neg_max", 2, 4, 2)
    probs = f32("probs", 2, HALF, SEQ)
    recip = f32("recip", 2, 2, 2)
    o = f32("o", 2, 2, 4, HD2)
    oT = f32("oT", 2, 2, 2, 2, 2, SEQ)

    tf = lambda name, *shape: sb("rt_" + name, [P, *shape], FP32)
    count, over = tf("count", E), tf("over", E, FULL)
    runs, runs_upto, ended = tf("runs", E), tf("runs_upto", E, E), tf("ended", E)
    past, skip = tf("past", RUNS, E), tf("skip", E)
    first_row, run_expert = tf("first_row", RUNS), tf("run_expert", RUNS)
    ends = sb("rt_ends", [P, E], mybir.dt.int32)
    starts, thresholds, upto, run_no, table = later.starts, later.thresholds, later.upto, later.run_no, later.table
    s_ends, s_tabled, s_padded = sem("rt_ends_known"), sem("rt_tabled"), [sem("rt_padded_sp"), sem("rt_padded_act")]

    def write_padding(eng, experts, s_done):
        block_of = lambda first: rows_dram[bass.ds(first, ROWS), :].rearrange("(h p) n -> p h n", p=P)
        eng.wait_ge(s_ends, 1)
        for e in experts:
            end = eng.value_load(ends[0:1, e:e + 1], min_val=0, max_val=E * REGION) if e < E else E * REGION
            eng.dma_start(block_of(end), later.pad[:, :, :]).then_inc(s_done, 16)
        eng.wait_ge(s_done, 16 * len(experts))

    rf = lambda name, *shape: sb("ro_" + name, [P, *shape], FP32)
    wg, bg, index, dest = later.wg, later.bg, later.index, later.dest
    tri, ones, filled = later.tri, later.ones, later.filled
    r_stats, r_mean_var = rf("stats", TPS, 6), rf("mean_var", TPS, 2)
    r_var_eps, r_rstd, nothing = rf("var_eps", TPS), rf("rstd", TPS), rf("nothing", TPS)
    r_xn, r_xT, out_rows = rf("xn", 2, TPS, P), rf("xT", TOK), rf("rows", 2, TPS, TOPK, WIDTH)
    logits, top, shifted, expd = (rf(n, TPS, E) for n in ("logits", "top", "shifted", "expd"))
    which, which_f = sb("ro_which", [P, TPS, E], mybir.dt.uint32), rf("which_f", TPS, TOPK)
    chosen, taken = rf("chosen", TPS, TOPK, E), sb("ro_mask", [P, TPS, E], BF16)
    place, place_sel, place_f = rf("place", TPS, E), rf("place_sel", TPS, TOPK, E), rf("place_f", TPS, TOPK)
    place_u = sb("ro_place_u", [P, 2, TPS, TOPK], mybir.dt.uint32)
    total, both, den = rf("total", TPS), rf("both", TPS), rf("den", TPS)

    ps_st = [pb("st0"), pb("st1")]
    ps_p = [pb("p0"), pb("p1")]
    ps_pv = [pb("pv0"), pb("pv1")]
    ps_x, ps_m = pb("x"), pb("m")

    names = ("zeroed stats mean_var var_eps rstd xn transposed xT_hi xT_lo "
             "ctx_hi ctx_lo scores raw_copied scores_transposed max max_transposed max_rows shifted exp pv_product "
             "reciprocal normalised o_transposed o_copied out_product residual fill filled").split()
    S = {n: sem("ca_" + n) for n in names}
    s_keys = [sem("ca_keys_even"), sem("ca_keys_odd")]
    names = ("w_loaded stats mean_var var_eps rstd xn transposed xT_copied xn_copied logits "
             "sorted shifted choices chosen mask exp gating counted placing places gates dest rows_whole").split()
    R = {n: sem("ro_" + n) for n in names}
    s_sent = [sem("ro_sent_even"), sem("ro_sent_odd")]
    sent = lambda s, par: 16 * TPS * TOPK * ((s - par) // 2 + 1) if isinstance(s, int) else \
        8 * TPS * TOPK * (s - par) + 16 * TPS * TOPK
    tile_of_x = lambda t: x_sb[:, bass.ds(t, 1), :].rearrange("p a n -> p (a n)")

    with nc.Block() as block:

        @block.sync
        def _(sp):
            def body(s, par):
                if live(s + 2, STEPS):
                    wait(sp, S["scores"], 4 * (s + 1))
                    sp.dma_start(keys[:, par, :], w["ctxT"][:, bass.ds(TOK * (s + 2), TOK)]).then_inc(s_keys[par], 16)
                if isinstance(s, int) and s == 0:
                    for dst, src in ((w1[:, :, :], w["ff_w1"]), (w2[:, :, :], w["ff_w2"]), (b1[:, :, :], w["ff_b1"]),
                                     (b2[:, :, :], w["ff_b2"])):
                        sp.dma_start(dst, src).then_inc(R["w_loaded"], 16)

            pipeline(sp, -2, STEPS, body, 3, 2)
            sp.wait_ge(R["w_loaded"], 64)
            write_padding(sp, range(0, 5), s_padded[0])

        @block.gpsimd
        def _(pool):
            nc.gpsimd.memset(half[:, :], -0.5).then_inc(S["zeroed"], 1)
            nc.gpsimd.memset(eps[:, :], EPS).then_inc(S["zeroed"], 1)
            nc.gpsimd.memset(zeros[:, :], 0.0).then_inc(S["zeroed"], 1)
            pool.wait_ge(S["zeroed"], 3)

            def body(s, par):
                if live(s - 3, STEPS):
                    for part in ("xn_copied", "dest", "gates", "places"):
                        wait(pool, R[part], s - 2)
                    wait(pool, R["rows_whole"], s - 3)
                    nc.gpsimd.tensor_tensor(nothing[:, :], half[:, :], half[:, :], ALU.add).then_inc(R["rows_whole"], 1)
                    for t in range(TPS):
                        for k in range(TOPK):
                            at = bass.IndirectOffsetOnAxis(ap=place_u[:, 1 - par, t, k:k + 1], axis=0)
                            nc.gpsimd.indirect_dma_start(rows_dram, at, out_rows[:, 1 - par, t, k, :], None)\
                              .then_inc(s_sent[1 - par], 16)
                if live(s + 3, STEPS):
                    wait(pool, S["mean_var"], s + 4)
                    wait(pool, S["ctx_lo"], s + 2)
                    nc.gpsimd.tensor_tensor(var_eps[:, :], mean_var[:, 1 - par, :, 1], eps[:, :], ALU.add)\
                      .then_inc(S["var_eps"], 1)
                    pool.wait_ge(S["var_eps"], s + 4)
                    nc.gpsimd.tensor_tensor(rstd[:, 1 - par, :], var_eps[:, :], half[:, :], ALU.pow).then_inc(S["rstd"], 1)
                if live(s - 1, STEPS):
                    wait(pool, R["mean_var"], s)
                    nc.gpsimd.tensor_tensor(r_var_eps[:, :], r_mean_var[:, :, 1], eps[:, :], ALU.add)\
                      .then_inc(R["var_eps"], 1)
                    pool.wait_ge(R["var_eps"], s)
                    nc.gpsimd.tensor_tensor(r_rstd[:, :], r_var_eps[:, :], half[:, :], ALU.pow).then_inc(R["rstd"], 1)
                if live(s + 2, STEPS):
                    wait(pool, S["rstd"], cap(s + 4, STEPS))
                    wait(pool, S["ctx_lo"], s + 2)
                    wait(pool, S["fill"], 12 * (s + 1))
                    wait(pool, s_keys[par], 8 * (s + 2 - par) + 16)
                    src = keys[:, par, :]
                    nc.gpsimd.tensor_tensor(ctx_hi[:, par, :], src, zeros[:, :], ALU.add).then_inc(S["ctx_hi"], 1)
                    pool.wait_ge(S["ctx_hi"], s + 3)
                    nc.gpsimd.tensor_tensor(ctx_lo[:, par, :], src, ctx_hi[:, par, :].bitcast(FP32), ALU.subtract)\
                      .then_inc(S["ctx_lo"], 1)

            pipeline(pool, -3, STEPS + 3, body, 3, 4)
            for par in range(2):
                pool.wait_ge(s_sent[par], sent(STEPS - 2 + par, par))

        @block.scalar
        def _(act):
            def slot(s, par, u):
                n = 4 * s + u
                f = n + 4
                if live(n - 1, 4 * STEPS):
                    wait(act, S["shifted"], n)
                    wait(act, S["pv_product"], n - 2)
                    nc.scalar.activation(probs[:, (u - 1) % 2, :, :].rearrange("p h q -> p (h q)"), ps_st[(u - 1) % 2][:, :],
                                         ACT.Exp).then_inc(S["exp"], 1)
                if live(s + 1, STEPS):
                    wait(act, S["fill"], 3 * f + 1)
                    nc.scalar.copy(t_all[:, 1 - par, 4 * u:4 * u + 2, :].rearrange("p h n -> p (h n)"), ps_p[u % 2][:, :])\
                      .then_inc(S["filled"], 1)
                if u == 0 and live(s + 2, STEPS):
                    wait(act, S["transposed"], s + 3)
                    nc.scalar.copy(xT_hi[:, par, :], ps_m[:, 0:TOK]).then_inc(S["xT_hi"], 1)
                if u == 0 and live(s - 3, STEPS):
                    wait(act, R["shifted"], s - 2)
                    nc.scalar.activation(expd[:, :, :].rearrange("p t e -> p (t e)"),
                                         shifted[:, :, :].rearrange("p t e -> p (t e)"), ACT.Exp).then_inc(R["exp"], 1)
                if u == 2 and live(s - 2, STEPS):
                    wait(act, R["transposed"], s - 1)
                    nc.scalar.copy(r_xT[:, :], ps_m[:, 0:TOK]).then_inc(R["xT_copied"], 1)
                if live(s + 1, STEPS):
                    wait(act, S["fill"], 3 * f + 2)
                    nc.scalar.copy(t_all[:, 1 - par, 4 * u + 2:4 * u + 4, :].rearrange("p h n -> p (h n)"),
                                   ps_p[(u + 1) % 2][:, :]).then_inc(S["filled"], 1)
                if live(s + 1, STEPS):
                    wait(act, S["fill"], 3 * f + 3)
                    for b in range(2):
                        nc.scalar.copy(v_bd[64 * b:64 * b + 64, 1 - par, u // 2, HALF * (u % 2):HALF * (u % 2) + HALF, b, 0:HD2],
                                       ps_p[u % 2][64 * b:64 * b + 64, :].rearrange("p (h d) -> p h d", h=HALF))\
                          .then_inc(S["filled"], 1)
                if u == 2 and live(s - 2, STEPS):
                    if live(s - 4, STEPS):
                        wait(act, s_sent[par], sent(s - 4, par))
                    wait(act, R["xn"], s - 1)
                    nc.scalar.copy(out_rows[:, par, :, :, 0:D], r_xn[:, par, :, :].unsqueeze(2).broadcast_to([P, TPS, TOPK, D]))\
                      .then_inc(R["xn_copied"], 1)

            def body(s, par):
                for u in range(4):
                    slot(s, par, u)

            pipeline(act, -2, STEPS + 3, body, 2, 4)
            write_padding(act, range(5, E + 1), s_padded[1])

        @block.vector
        def _(dve):
            tt = nc.vector.tensor_tensor
            def chain(name, per, r, k, ins):
                ins.then_inc(R[name], 1)
                dve.wait_ge(R[name], per * r + k + 1)

            def slot(s, par, u):
                n = 4 * s + u
                f = n + 4
                if u == 2 and live(s - 1, STEPS):
                    wait(dve, S["residual"], TPS * s)
                if live(n, 4 * STEPS):
                    wait(dve, S["scores"], n + 1)
                    tt(raw[:, u % 2, :], ps_st[u % 2][:, :], mask[:, :], ALU.add).then_inc(S["raw_copied"], 1)
                if u == 1 and live(s - 3, STEPS):
                    r = s - 3
                    wait(dve, R["exp"], r + 1)
                    nc.vector.tensor_reduce(total[:, :], expd[:, :, :], axis=AX.X, op=ALU.add)
                    chain("gating", 3, r, 0, tt(both[:, :], expd[:, :, 0], expd[:, :, 1], ALU.add))
                    chain("gating", 3, r, 1,
                          nc.vector.scalar_tensor_tensor(den[:, :], total[:, :], 1e-8, both[:, :], ALU.mult, ALU.add))
                    nc.vector.reciprocal(den[:, :], den[:, :]).then_inc(R["gating"], 1)
                if live(n - 2, 4 * STEPS):
                    m, owner = (u - 2) % 4, par if u >= 2 else 1 - par
                    wait(dve, S["o_transposed"], n - 1)
                    wait(dve, S["out_product"], 2 * (s - (u < 2)) + m // 2 - 1)
                    dst = oT[:, m // 2, m % 2, :, :, :, :].rearrange("p j h b q -> p b j h q")
                    for b in range(2):
                        ins = nc.vector.tensor_copy(dst[:, b, :, :, :], ps_x[:, 256 * b:256 * b + 256]
                                                    .rearrange("p (j h q) -> p j h q", j=2, h=2))
                    ins.then_inc(S["o_copied"], 1)
                if u == 0 and live(s - 3, STEPS):
                    r = s - 3
                    for t in range(TPS):
                        ins = nc.vector.max(top[:, t, :], logits[:, t, :])
                    chain("sorted", 2, r, 1, ins)
                    tt(shifted[:, :, :], top[:, :, :], top[:, :, 0:1].broadcast_to([P, TPS, E]), ALU.subtract)\
                        .then_inc(R["shifted"], 1)
                    for t in range(TPS):
                        ins = nc.vector.max_index(which[:, t, :], top[:, t, :], logits[:, t, :])
                    chain("choices", 2, r, 0, ins)
                    chain("choices", 2, r, 1, nc.vector.tensor_copy(which_f[:, :, :], which[:, :, 0:TOPK]))
                    for t in range(TPS):
                        ins = tt(chosen[:, t, :, :], index[:, :].unsqueeze(1).broadcast_to([P, TOPK, E]),
                                 which_f[:, t, :].unsqueeze(2).broadcast_to([P, TOPK, E]), ALU.is_equal)
                    chain("chosen", 1, r, 0, ins)
                    tt(taken[:, :, :], chosen[:, :, 0, :], chosen[:, :, 1, :], ALU.add).then_inc(R["mask"], 1)
                if u == 1 and live(s - 3, STEPS):
                    r, q = s - 3, 1 - par
                    wait(dve, R["counted"], r + 1)
                    nums = ps_m[:, 0:2 * TPS * E].rearrange("p (w t e) -> p w t e", w=2, t=TPS)
                    for t in range(TPS):
                        chain("placing", 6, r, t, tt(filled[:, t + 1, :], filled[:, t, :], nums[:, 1, t, :], ALU.add))
                    chain("placing", 6, r, 2, tt(place[:, :, :], filled[:, 0:TPS, :], nums[:, 0, :, :], ALU.add))
                    for t in range(TPS):
                        ins = tt(place_sel[:, t, :, :], chosen[:, t, :, :],
                                 place[:, t, :].unsqueeze(1).broadcast_to([P, TOPK, E]), ALU.mult)
                    chain("placing", 6, r, 3, ins)
                    chain("placing", 6, r, 4, nc.vector.tensor_reduce(place_f[:, :, :], place_sel[:, :, :, :],
                                                                      axis=AX.X, op=ALU.add))
                    nc.vector.tensor_copy(filled[:, 0, :], filled[:, TPS, :]).then_inc(R["placing"], 1)
                    nc.vector.tensor_copy(place_u[:, q, :, :], place_f[:, :, :]).then_inc(R["places"], 1)
                    wait(dve, R["xn_copied"], r + 1)
                    dve.wait_ge(R["gating"], 3 * r + 3)
                    tt(out_rows[:, q, :, :, META], expd[:, :, 0:TOPK],
                       den[:, :].unsqueeze(2).broadcast_to([P, TPS, TOPK]), ALU.mult).then_inc(R["gates"], 1)
                    nc.vector.tensor_copy(out_rows[:, q, :, :, META + 1], dest[:, bass.ds(TPS * r, TPS), :])\
                      .then_inc(R["dest"], 1)
                if u == 2 and live(s + 3, STEPS):
                    for t in range(TPS):
                        ins = nc.vector.bn_stats(stats[:, 1 - par, t, :], tile_of_x(TPS * (s + 3) + t))
                    ins.then_inc(S["stats"], 1)
                if u == 2 and live(s - 1, STEPS):
                    for t in range(TPS):
                        ins = nc.vector.bn_stats(r_stats[:, t, :], tile_of_x(TPS * (s - 1) + t))
                    ins.then_inc(R["stats"], 1)
                if u == 2:
                    if live(s + 3, STEPS):
                        dve.wait_ge(S["stats"], s + 4)
                    if live(s - 1, STEPS):
                        dve.wait_ge(R["stats"], s)
                if live(n, 4 * STEPS):
                    wait(dve, S["scores_transposed"], n + 1)
                    nc.vector.tensor_reduce(neg_max[:, u % 2, :, :], ps_x[:, :].rearrange("p (a b k) -> p a b k", a=4, b=2),
                                            axis=AX.X, op=ALU.max, negate=True).then_inc(S["max"], 1)
                if u == 3 and live(s - 2, STEPS):
                    wait(dve, R["logits"], s - 1)
                    chain("sorted", 2, s - 2, 0, tt(logits[:, :, :], ps_m[:, 0:TPS * P]
                          .rearrange("p (t n) -> p t n", t=TPS)[:, :, 0:E], bg[:, :, :], ALU.add))
                if live(n - 1, 4 * STEPS):
                    wait(dve, S["pv_product"], n)
                    for c in range(2):
                        acc = ps_pv[c][:, 0:4 * VW].rearrange("p (a b d) -> p a b d", a=2, b=2)
                        ins = nc.vector.reciprocal(recip[:, c, :, :], acc[:, :, :, HD2])
                    ins.then_inc(S["reciprocal"], 1)
                    dve.wait_ge(S["reciprocal"], n)
                    wait(dve, S["o_transposed"], n - 2)
                    for c in range(2):
                        acc = ps_pv[c][:, 0:4 * VW].rearrange("p (a b d) -> p a b d", a=2, b=2)
                        dst = o[:, (u - 1) % 2, :, 2 * c:2 * c + 2, :].rearrange("p b a d -> p a b d")
                        ins = nc.vector.tensor_tensor(dst, acc[:, :, :, 0:HD2],
                                                      recip[:, c, :, :].unsqueeze(3).broadcast_to([P, 2, 2, HD2]), ALU.mult)
                    ins.then_inc(S["normalised"], 1)
                if live(n, 4 * STEPS):
                    wait(dve, S["max_transposed"], n + 1)
                    tt(rows[0:8, u % 2, :].rearrange("p (a n) -> p a n", a=4),
                       ps_x[0:8, 0:P].unsqueeze(1).broadcast_to([8, 4, P]), own[0:8, :, :], ALU.mult)\
                        .then_inc(S["max_rows"], 1)
                if u == 0 and live(s + 2, STEPS):
                    wait(dve, S["xT_hi"], s + 3)
                    nc.vector.tensor_tensor(xT_lo[:, par, :], ps_m[:, 0:TOK], xT_hi[:, par, :].bitcast(FP32),
                                            ALU.subtract).then_inc(S["xT_lo"], 1)
                if u == 2 and live(s + 3, STEPS):
                    for t in range(TPS):
                        ins = nc.vector.bn_aggr(mean_var[:, 1 - par, t, :], stats[:, 1 - par, t, :])
                    ins.then_inc(S["mean_var"], 1)
                if u == 2 and live(s - 1, STEPS):
                    for t in range(TPS):
                        ins = nc.vector.bn_aggr(r_mean_var[:, t, :], r_stats[:, t, :])
                    ins.then_inc(R["mean_var"], 1)
                if u == 3 and live(s + 3, STEPS):
                    wait(dve, S["rstd"], s + 4)
                    for t in range(TPS):
                        ins = nc.vector.tensor_scalar(xn[:, 1 - par, t, :], tile_of_x(TPS * (s + 3) + t),
                                                      mean_var[:, 1 - par, t, 0:1], rstd[:, 1 - par, t:t + 1],
                                                      ALU.subtract, ALU.mult)
                    ins.then_inc(S["xn"], 1)
                if u == 3 and live(s - 1, STEPS):
                    wait(dve, R["rstd"], s)
                    wait(dve, R["xn_copied"], s - 2)
                    for t in range(TPS):
                        ins = nc.vector.tensor_scalar(r_xn[:, 1 - par, t, :], tile_of_x(TPS * (s - 1) + t),
                                                      r_mean_var[:, t, 0:1], r_rstd[:, t:t + 1], ALU.subtract, ALU.mult)
                    ins.then_inc(R["xn"], 1)
                tile = {1: TPS * (s - 1) + 1, 3: TPS * s}.get(u)
                if tile is not None and live(tile, TILES):
                    wait(dve, S["out_product"], tile + 1)
                    row = tile_of_x(tile)
                    nc.vector.tensor_tensor(row, ps_m[:, 0:P], row, ALU.add).then_inc(S["residual"], 1)

            def body(s, par):
                for u in range(4):
                    slot(s, par, u)

            pipeline(dve, -3, STEPS + 3, body, 3, 4)
            ts = nc.vector.tensor_scalar
            dve.wait_ge(R["placing"], 6 * STEPS)
            nc.vector.tensor_copy(ends[:, :], filled[:, 0, :]).then_inc(s_ends, 1)

            n = [0]

            def step(ins):
                n[0] += 1
                ins.then_inc(s_tabled, 1)
                dve.wait_ge(s_tabled, n[0])

            across = lambda t, m: t[:, :].unsqueeze(2).broadcast_to([P, E, m])
            along = lambda t, m: t[:, :].unsqueeze(1).broadcast_to([P, m, E])
            step(tt(count[:, :], filled[:, 0, :], starts[:, :], ALU.subtract))
            step(tt(over[:, :, :], across(count, FULL), thresholds[:, :, :], ALU.is_gt))
            step(nc.vector.tensor_reduce(runs[:, :], over[:, :, :], axis=AX.X, op=ALU.add))
            step(tt(runs_upto[:, :, :], along(runs, E), upto[:, :, :], ALU.mult))
            step(nc.vector.tensor_reduce(ended[:, :], runs_upto[:, :, :], axis=AX.X, op=ALU.add))
            step(tt(past[:, :, :], run_no[:, :].unsqueeze(2).broadcast_to([P, RUNS, E]), along(ended, RUNS), ALU.is_ge))
            step(nc.vector.tensor_reduce(run_expert[:, :], past[:, :, :], axis=AX.X, op=ALU.add))
            ts(run_expert[:, :], run_expert[:, :], float(E - 1), None, ALU.min)
            step(ts(skip[:, :], runs[:, :], float(-ROWS), float(REGION), ALU.mult, ALU.add))
            step(tt(past[:, :, :], past[:, :, :], along(skip, RUNS), ALU.mult))
            step(nc.vector.tensor_reduce(first_row[:, :], past[:, :, :], axis=AX.X, op=ALU.add))
            step(nc.vector.scalar_tensor_tensor(first_row[:, :], run_no[:, :], float(ROWS), first_row[:, :], ALU.mult, ALU.add))
            step(ts(first_row[:, :], first_row[:, :], float(E * REGION), None, ALU.min))
            nc.vector.tensor_copy(table[:, 0, :], run_expert[:, :])
            nc.vector.tensor_copy(table[:, 1, :], first_row[:, :]).then_inc(s_tabled, 1)

        @block.tensor
        def _(pe):
            def t_fill(s, par, u, i):
                bank, f = ps_p[(u + i) % 2], 4 * s + u + 4
                if i == 0:
                    wait(pe, S["filled"], 4 * f - 2)
                    wait(pe, S["xT_lo"], s + 2)
                else:
                    wait(pe, S["filled"], 4 * f)
                for j in range(2):
                    h, out = 4 * u + 2 * i + j, bank[:, j * TOK:(j + 1) * TOK]
                    nc.tensor.matmul(out, a_hi[:, h, :], xT_hi[:, 1 - par, :], start=True, stop=False)
                    nc.tensor.matmul(out, a_lo[:, h, :], xT_hi[:, 1 - par, :], start=False, stop=False)
                    ins = nc.tensor.matmul(out, a_hi[:, h, :], xT_lo[:, 1 - par, :], start=False, stop=True)
                ins.then_inc(S["fill"], 1)

            def v_fill(s, par, u):
                f = 4 * s + u + 4
                wait(pe, S["filled"], 4 * f + 1)
                wait(pe, S["ctx_lo"], s + 2)
                cols, tok = slice(512 * (u % 2), 512 * (u % 2) + 512), slice(P * (u // 2), P * (u // 2) + P)
                out = ps_p[u % 2][:, :]
                nc.tensor.matmul(out, ctx_hi[:, 1 - par, tok], wv_hi[:, cols], start=True, stop=False)
                nc.tensor.matmul(out, ctx_lo[:, 1 - par, tok], wv_hi[:, cols], start=False, stop=False)
                nc.tensor.matmul(out, ctx_hi[:, 1 - par, tok], wv_lo[:, cols], start=False, stop=True).then_inc(S["fill"], 1)

            def slot(s, par, u):
                n = 4 * s + u
                tile, hh = u // 2, u % 2
                st = ps_st[u % 2]
                if live(n, 4 * STEPS):
                    wait(pe, S["filled"], 16 * (s + 1))
                    wait(pe, S["exp"], n - 1)
                    for b in range(2):
                        tok = P * tile + SEQ * b
                        ins = nc.tensor.matmul(st[64 * b:64 * b + 64, :], keys[:, par, tok:tok + SEQ],
                                               t_all[:, par, HALF * hh:HALF * hh + HALF, tok:tok + SEQ],
                                               start=True, stop=True, skip_group_check=True)
                    ins.then_inc(S["scores"], 1)
                if live(n - 1, 4 * STEPS):
                    wait(pe, S["max_rows"], n)
                    nc.tensor.matmul(ps_st[1 - u % 2][:, :], pick[:, :], rows[:, 1 - u % 2, :], start=False, stop=True,
                                     skip_group_check=True).then_inc(S["shifted"], 1)
                if live(n - 2, 4 * STEPS):
                    m = (u - 2) % 4
                    wait(pe, S["normalised"], n - 1)
                    wait(pe, S["max_rows"], cap(n, 4 * STEPS))
                    for b in range(2):
                        for j in range(2):
                            ins = nc.tensor.transpose(ps_x[:, (2 * b + j) * P:(2 * b + j + 1) * P],
                                                      o[:, m % 2, b, 2 * j:2 * j + 2, :].rearrange("p a d -> p (a d)"), ident[:, :])
                    ins.then_inc(S["o_transposed"], 1)
                if u == 1 and live(s - 3, STEPS):
                    wait(pe, R["mask"], s - 2)
                    wait(pe, S["xT_lo"], cap(s + 3, STEPS))
                    wait(pe, S["residual"], cap(TPS * s - 1, TILES))
                    by_expert = taken[:, :, :].rearrange("p t e -> p (t e)")
                    nc.tensor.matmul(ps_m[:, 0:TPS * E], tri[:, :], by_expert, start=True, stop=True)
                    nc.tensor.matmul(ps_m[:, TPS * E:2 * TPS * E], ones[:, :], by_expert, start=True, stop=True)\
                      .then_inc(R["counted"], 1)
                if u == 0 and live(s + 2, STEPS):
                    wait(pe, S["xn"], s + 3)
                    wait(pe, S["residual"], 2 * s - 1)
                    for t in range(TPS):
                        ins = nc.tensor.transpose(ps_m[:, t * P:(t + 1) * P], xn[:, par, t, :], ident[:, :])
                    ins.then_inc(S["transposed"], 1)
                if u == 2 and live(s - 2, STEPS):
                    wait(pe, R["xn"], s - 1)
                    wait(pe, S["residual"], cap(TPS * s, TILES))
                    wait(pe, R["placing"], cap(6 * (s - 3) + 3, 6 * STEPS))
                    for t in range(TPS):
                        ins = nc.tensor.transpose(ps_m[:, t * P:(t + 1) * P], r_xn[:, par, t, :], ident[:, :])
                    ins.then_inc(R["transposed"], 1)
                if live(s + 1, STEPS):
                    t_fill(s, par, u, 0)
                if live(n - 1, 4 * STEPS):
                    m, owner = (u - 1) % 4, par if u else 1 - par
                    wait(pe, S["exp"], n)
                    wait(pe, S["normalised"], n - 1)
                    for a in range(4):
                        for h2 in range(2):
                            h = 2 * a + h2
                            ins = nc.tensor.matmul(ps_pv[a // 2][64 * h2:64 * h2 + 64, (a % 2) * 2 * VW:(a % 2 + 1) * 2 * VW],
                                                   probs[:, m % 2, h, :],
                                                   v_bd[:, owner, m // 2, HALF * (m % 2) + h, :, :].rearrange("p b d -> p (b d)"),
                                                   start=True, stop=True)
                    ins.then_inc(S["pv_product"], 1)
                if live(n, 4 * STEPS):
                    wait(pe, S["raw_copied"], n + 1)
                    wait(pe, S["o_copied"], n - 1)
                    for a in range(4):
                        ins = nc.tensor.transpose(ps_x[:, a * P:(a + 1) * P], raw[:, u % 2, a * P:(a + 1) * P], ident[:, :])
                    ins.then_inc(S["scores_transposed"], 1)
                if live(s + 1, STEPS):
                    t_fill(s, par, u, 1)
                if live(s + 1, STEPS):
                    v_fill(s, par, u)
                if live(n, 4 * STEPS):
                    wait(pe, S["max"], n + 1)
                    nc.tensor.transpose(ps_x[0:8, 0:P], neg_max[:, u % 2, :, :].rearrange("p a b -> p (a b)"), ident[:, :])\
                      .then_inc(S["max_transposed"], 1)
                if u == 2 and live(s - 2, STEPS):
                    wait(pe, R["xT_copied"], s - 1)
                    for t in range(TPS):
                        ins = nc.tensor.matmul(ps_m[:, t * P:(t + 1) * P], r_xT[:, t * P:(t + 1) * P], wg[:, :],
                                               start=True, stop=True)
                    ins.then_inc(R["logits"], 1)
                done = {1: TPS * (s - 1) + 1, 3: TPS * s}.get(u)
                if done is not None and live(done, TILES):
                    wait(pe, S["o_copied"], 2 * done + 2)
                    wait(pe, S["xT_lo"], cap(s + 3, STEPS) if u == 1 else 0)
                    wait(pe, S["residual"], done)
                    if u == 3:
                        wait(pe, R["sorted"], 2 * (s - 2) + 1)
                    else:
                        wait(pe, R["placing"], 6 * (s - 3) + 3)
                    t = int(u == 1)
                    for c in range(8):
                        ins = nc.tensor.matmul(ps_m[:, 0:P],
                                               oT[:, t, c // 4, c // 2 % 2, c % 2, :, :].rearrange("p b q -> p (b q)"),
                                               wo[:, c, :], start=(c == 0), stop=(c == 7))
                    ins.then_inc(S["out_product"], 1)
            def body(s, par):
                for u in range(4):
                    slot(s, par, u)

            pipeline(pe, -2, STEPS + 3, body, 2, 4)


def experts(nc, rows_dram, result_dram, later, w1, w2, b1, b2, w, sem, sb, pb):
    f32 = lambda name, *shape: sb("ex_" + name, [P, *shape], FP32)
    f32r = lambda name, *shape: sb("ex_" + name, [P, *shape], FP32R)
    HALVES, SLOTS = ROWS // P, 4
    ident, table, rows = later.ident, later.table, f32("rows", SLOTS, HALVES, WIDTH)
    warm = f32("warm", 1)
    gate = f32("gate", SLOTS, HALVES)
    going, dest = (sb("ex_" + n, [P, SLOTS, HALVES], mybir.dt.uint32) for n in ("going", "dest"))
    nothing = sb("ex_nothing", [P, HALVES], mybir.dt.uint32)
    xT_hi, xT_lo = f32r("xT_hi", 2, ROWS), f32r("xT_lo", 2, ROWS)
    w1_now, w2_now, b1_now = f32r("w1_now", 2, 2 * HID), f32("w2_now", SLOTS, CH, P), f32("b1_now", 2, CH)
    hT, summed, y = f32("hT", 2, CH, ROWS), f32("summed", 2, HALVES, P), f32("y", SLOTS, HALVES, P)
    ps_t, ps_h, ps_o = [pb("t0"), pb("t1")], [pb(f"h{c}") for c in range(CH)], [pb("o0"), pb("o1")]
    names = ("warm nothing w1_hi w1_split w2_copied b1_copied meta transposed xT_hi xT_lo hidden gelu out "
             "summed scaled dest").split()
    S = {n: sem("ex_" + n) for n in names}
    s_rows = [sem(f"ex_rows_{n}") for n in range(SLOTS)]
    s_sent = [sem(f"ex_sent_{n}") for n in range(SLOTS)]
    loaded = lambda r, slot: 4 * (r - slot) + 16
    sent = lambda r, slot: HALVES * loaded(r, slot)

    AHEAD, BEHIND = 3, 7

    with nc.Block() as block:

        @block.sync
        def _(sp):
            def body(r, slot):
                par = slot % 2
                if live(r + 3, RUNS):
                    q = (slot + 3) % SLOTS
                    first = sp.value_load(table[0:1, 1, bass.ds(r + 3, 1)], min_val=0, max_val=E * REGION)
                    wait(sp, S["meta"], r)
                    sp.dma_start(rows[:, q, :, :], rows_dram[bass.ds(first, ROWS), :].rearrange("(h p) n -> p h n", p=P))\
                      .then_inc(s_rows[q], 16)

            pipeline(sp, -3, RUNS, body, ahead=AHEAD, behind=BEHIND, steps=RUNS, unroll=SLOTS)

        @block.gpsimd
        def _(pool):
            nc.gpsimd.memset(nothing[:, :], 0).then_inc(S["nothing"], 1)
            pool.wait_ge(S["nothing"], 1)

            def body(r, slot):
                par = slot % 2
                if live(r - 1, RUNS):
                    wait(pool, S["meta"], r)
                if live(r - 5, RUNS):
                    wait(pool, s_sent[(slot - 1) % SLOTS], sent(r - 5, (slot - 1) % SLOTS))
                wait(pool, S["dest"], r - 1)
                wait(pool, S["scaled"], HALVES * (r - 1))
                if live(r - 1, RUNS):
                    q = (slot - 1) % SLOTS
                    nc.gpsimd.tensor_tensor(dest[:, q, :], going[:, q, :], nothing[:, :], ALU.add).then_inc(S["dest"], 1)
                else:
                    nc.gpsimd.tensor_tensor(nothing[:, :], nothing[:, :], nothing[:, :], ALU.add).then_inc(S["dest"], 1)
                if live(r - 2, RUNS):
                    q = (slot - 2) % SLOTS
                    for h in range(HALVES):
                        at = bass.IndirectOffsetOnAxis(ap=dest[:, q, h:h + 1], axis=0)
                        nc.gpsimd.indirect_dma_start(result_dram, at, y[:, q, h, :], None,
                                                     bounds_check=TOPK * BATCH * SEQ - 1, oob_is_err=False)\
                          .then_inc(s_sent[q], 16)

            pipeline(pool, 1, RUNS + 2, body, ahead=AHEAD, behind=BEHIND, steps=RUNS, unroll=SLOTS)

        @block.scalar
        def _(act):
            nc.scalar.activation(warm[:, :], ident[:, 0:1], ACT.Gelu_apprx_tanh).then_inc(S["warm"], 1)

            def body(r, slot):
                par = slot % 2
                if live(r + 1, RUNS):
                    wait(act, S["transposed"], r + 2)
                    wait(act, S["hidden"], CH * r)
                    nc.scalar.copy(xT_hi[:, 1 - par, :], ps_t[1 - par][:, 0:ROWS]).then_inc(S["xT_hi"], 1)
                if live(r, RUNS):
                    for c in range(CH):
                        wait(act, S["hidden"], CH * r + c + 1)
                        wait(act, S["out"], r - 1)
                        if c == 0:
                            wait(act, S["b1_copied"], r + 1)
                        nc.scalar.activation(hT[:, par, c, :], ps_h[c][:, 0:ROWS], ACT.Gelu_apprx_tanh,
                                             bias=b1_now[:, par, c:c + 1]).then_inc(S["gelu"], 1)
                if live(r - 2, RUNS):
                    q = (slot - 2) % SLOTS
                    wait(act, S["summed"], r - 1)
                    if live(r - 6, RUNS):
                        wait(act, s_sent[q], sent(r - 6, q))
                    for h in range(HALVES):
                        nc.scalar.activation(y[:, q, h, :], summed[:, par, h, :], ACT.Copy, scale=gate[:, q, h:h + 1])\
                          .then_inc(S["scaled"], 1)

            pipeline(act, -1, RUNS + 2, body, ahead=AHEAD, behind=BEHIND, steps=RUNS, unroll=SLOTS)

        @block.vector
        def _(dve):
            tt = nc.vector.tensor_tensor

            def body(r, slot):
                par = slot % 2
                if live(r - 2, RUNS):
                    last = dve.value_load(table[0:1, 0, bass.ds(r - 2, 1)], min_val=0, max_val=E - 1)
                    wait(dve, S["out"], r - 1)
                    wait(dve, S["scaled"], HALVES * (r - 3))
                    tt(summed[:, par, :, :], ps_o[par][:, 0:ROWS].rearrange("p (h n) -> p h n", h=HALVES),
                       b2[:, bass.ds(last, 1), :].broadcast_to([P, HALVES, P]), ALU.add).then_inc(S["summed"], 1)
                if live(r + 1, RUNS):
                    q = (slot + 1) % SLOTS
                    wait(dve, s_rows[q], loaded(r + 1, q))
                    wait(dve, S["transposed"], r + 2)
                    wait(dve, S["scaled"], HALVES * (r - 2))
                    wait(dve, S["dest"], r - 2)
                    nc.vector.tensor_copy(gate[:, q, :], rows[:, q, :, META])
                    nc.vector.tensor_copy(going[:, q, :], rows[:, q, :, META + 1]).then_inc(S["meta"], 1)
                    e = dve.value_load(table[0:1, 0, bass.ds(r + 1, 1)], min_val=0, max_val=E - 1)
                    wait(dve, S["hidden"], CH * r)
                    w1_e = w1[:, bass.ds(e, 1), :].rearrange("p a n -> p (a n)")
                    nc.vector.tensor_copy(w1_now[:, 1 - par, 0:HID], w1_e).then_inc(S["w1_hi"], 1)
                    wait(dve, S["gelu"], CH * r)
                    nc.vector.tensor_copy(b1_now[:, 1 - par, :], b1[:, bass.ds(e, 1), :].rearrange("p a n -> p (a n)"))\
                      .then_inc(S["b1_copied"], 1)
                    dve.wait_ge(S["w1_hi"], r + 2)
                    tt(w1_now[:, 1 - par, HID:2 * HID], w1_e, w1_now[:, 1 - par, 0:HID].bitcast(FP32), ALU.subtract)\
                        .then_inc(S["w1_split"], 1)
                    wait(dve, S["xT_hi"], r + 2)
                    tt(xT_lo[:, 1 - par, :], ps_t[1 - par][:, 0:ROWS], xT_hi[:, 1 - par, :].bitcast(FP32), ALU.subtract)\
                        .then_inc(S["xT_lo"], 1)
                if live(r + 1, RUNS):
                    wait(dve, S["out"], r - 2)
                    nc.vector.tensor_copy(w2_now[:, q, :, :].rearrange("p c n -> p (c n)"),
                                          w2[:, bass.ds(e, 1), :].rearrange("p a n -> p (a n)")).then_inc(S["w2_copied"], 1)

            pipeline(dve, -1, RUNS + 2, body, ahead=AHEAD, behind=BEHIND, steps=RUNS, unroll=SLOTS)

        @block.tensor
        def _(pe):
            def body(r, slot):
                par = slot % 2
                if live(r + 1, RUNS):
                    q = (slot + 1) % SLOTS
                    wait(pe, s_rows[q], loaded(r + 1, q))
                    wait(pe, S["xT_lo"], r)
                    for h in range(HALVES):
                        ins = nc.tensor.transpose(ps_t[1 - par][:, h * P:(h + 1) * P], rows[:, q, h, 0:D], ident[:, :])
                    ins.then_inc(S["transposed"], 1)
                if live(r, RUNS):
                    wait(pe, S["w1_split"], r + 1)
                    wait(pe, S["xT_lo"], r + 1)
                    for c in range(CH):
                        wait(pe, S["gelu"], CH * (r - 1) + c + 1)
                        hi, lo = (w1_now[:, par, part * HID + c * P:part * HID + (c + 1) * P] for part in range(2))
                        for left, right in ((hi, xT_hi), (lo, xT_hi), (hi, xT_lo)):
                            ins = nc.tensor.matmul(ps_h[c][:, 0:ROWS], left, right[:, par, :],
                                                   start=left is hi and right is xT_hi, stop=right is xT_lo)
                        ins.then_inc(S["hidden"], 1)
                if live(r - 1, RUNS):
                    q = 1 - par
                    wait(pe, S["w2_copied"], r)
                    wait(pe, S["summed"], r - 2)
                    for h in range(HALVES):
                        for c in range(CH):
                            wait(pe, S["gelu"], CH * (r - 1) + c + 1)
                            ins = nc.tensor.matmul(ps_o[q][:, h * P:(h + 1) * P], hT[:, q, c, h * P:(h + 1) * P],
                                                   w2_now[:, (slot - 1) % SLOTS, c, :], start=(c == 0), stop=(c == CH - 1))
                    ins.then_inc(S["out"], 1)

            pipeline(pe, -1, RUNS + 1, body, ahead=AHEAD, behind=BEHIND, steps=RUNS, unroll=SLOTS)


def combine(nc, x_sb, result_dram, out_dram, sem, sb):
    PARTS = 8
    TPP = TILES // PARTS
    both = sb("co_both", [P, TILES, TOPK, D], FP32)
    s_both = [sem(f"co_loaded_{n}") for n in range(PARTS)]
    s_first, s_added, s_stored = sem("co_first_added"), sem("co_added"), sem("co_stored")
    result = result_dram[0:TOPK * BATCH * SEQ, :].rearrange("(t p k) n -> p t (k n)", p=P, k=TOPK)
    with nc.Block() as block:

        @block.sync
        def _(sp):
            for n in range(PARTS):
                tiles = slice(TPP * n, TPP * (n + 1))
                sp.dma_start(both[:, tiles, :, :].rearrange("p t k n -> p t (k n)"), result[:, tiles, :]).then_inc(s_both[n], 16)

        @block.vector
        def _(dve):
            for n in range(PARTS):
                tiles = slice(TPP * n, TPP * (n + 1))
                dve.wait_ge(s_both[n], 16)
                for k, s_done in enumerate((s_first, s_added)):
                    if k:
                        dve.wait_ge(s_first, n + 1)
                    nc.vector.tensor_tensor(x_sb[:, tiles, :], x_sb[:, tiles, :], both[:, tiles, k, :], ALU.add)\
                      .then_inc(s_done, 1)

        @block.scalar
        def _(act):
            for n in range(PARTS):
                tiles = slice(TPP * n, TPP * (n + 1))
                act.wait_ge(s_added, n + 1)
                act.dma_start(out_dram[:, tiles, :], x_sb[:, tiles, :]).then_inc(s_stored, 16)
            act.wait_ge(s_stored, 16 * PARTS)


def decoder(nc, x, w, out, phases=3):
    with ExitStack() as ctx:
        x_sb = ctx.enter_context(nc.sbuf_tensor("x_sb", [P, TILES, D], FP32))
        x_loaded = [ctx.enter_context(nc.semaphore(f"x_loaded_{s}")) for s in X_PARTS]
        x_dram = x.rearrange("b s d -> (b s) d").rearrange("(t p) d -> p t d", p=P)
        out_dram = out.rearrange("b s d -> (b s) d").rearrange("(t p) d -> p t d", p=P)
        with nc.Block() as block:
            @block.scalar
            def _(act):
                for s, end, loaded in zip(X_PARTS, X_PARTS[1:], x_loaded):
                    act.dma_start(x_sb[:, TPS * s:TPS * end, :], x_dram[:, TPS * s:TPS * end, :]).then_inc(loaded, 16)
        rows_dram = nc.dram_tensor("rows_by_expert", (E * REGION + ROWS, WIDTH), FP32).ap()
        result_dram = nc.dram_tensor("results_by_token", (TOPK * BATCH * SEQ, D), FP32).ap()

        def stage(part, prefix, *operands):
            with ExitStack() as inner:
                sem = lambda name: inner.enter_context(nc.semaphore(name))
                sb = lambda name, shape, dt: inner.enter_context(nc.sbuf_tensor(name, shape, dt))
                pb = lambda name: inner.enter_context(nc.psum_tensor(prefix + name, [P, 512], FP32))
                part(nc, *operands, w, sem, sb, pb)

        with ExitStack() as weights:
            keep = lambda name, shape, dt: weights.enter_context(nc.sbuf_tensor(name, shape, dt))
            later = Later(keep)
            stage(self_attention, "sa_", x_sb, x_dram, x_loaded, later)
            w1, w2 = keep("w1", [P, E, HID], FP32), keep("w2", [P, E, CH * P], FP32)
            b1, b2 = keep("b1", [P, E, CH], FP32), keep("b2", [P, E, P], FP32)
            stage(cross_attention_and_routing, "ca_", x_sb, rows_dram, later, w1, w2, b1, b2)
            stage(experts, "ex_", rows_dram, result_dram, later, w1, w2, b1, b2)
        with ExitStack() as inner:
            sem = lambda name: inner.enter_context(nc.semaphore(name))
            sb = lambda name, shape, dt: inner.enter_context(nc.sbuf_tensor(name, shape, dt))
            combine(nc, x_sb, result_dram, out_dram, sem, sb)


def laid_out(inputs):
    import numpy as np
    import math
    f = np.float32
    arrays = {}
    wq, wk, wv, wo = (np.asarray(inputs[f"L0_attn_{n}"]) for n in ("Wq", "Wk", "Wv", "Wo"))
    q = np.zeros((D, HG, 4, G1, HD1), f)
    q[:, :, 0:3] = wq.reshape(D, G1, HG, HD1).transpose(0, 2, 1, 3)[:, :, None]
    arrays["sa_wq"] = q.reshape(D, HG * P)
    k = np.zeros((D, G1, 4, G1, HD1), f)
    for g in range(G1):
        k[:, g, 0:3, g] = wk.reshape(D, G1, HD1)[:, None, g]
    arrays["sa_wk"] = k.reshape(D, G1 * P)
    v = np.zeros((D, P), f)
    v[:, 0:32] = wv
    arrays["sa_wv"] = v
    arrays["sa_wo"] = np.ascontiguousarray(wo.reshape(G1, HG, HD1, D).transpose(1, 0, 2, 3).reshape(P, D))
    arrays["ident"] = np.eye(P, dtype=f)
    start = 2.0 ** (-2.0 ** (-(math.log2(H1) - 3)))
    slopes = np.array([start * start ** i for i in range(H1)], dtype=f).reshape(G1, HG)
    high = (slopes.view(np.uint32) & np.uint32(0xFFFFF000)).view(f)
    parts = np.stack([high, slopes - high], 1)
    q_rows = np.zeros((P, STEP, HG, SEQ), f)
    q_rows[ALIBI_ROW:ALIBI_ROW + 2 * G1] = parts.reshape(2 * G1, 1, HG, 1)
    k_rows = np.zeros((P, STEP, G1, SEQ), f)
    z = np.zeros((2, SEQ, 2, 2, P), f)
    ones = np.zeros((2, SEQ, 2, G1, HD1), f)
    for g in range(G1):
        k_rows[MAX_ROW + g, :, g] = 1.0
        k_rows[ALIBI_ROW + 2 * g:ALIBI_ROW + 2 * g + 2, :, g] = np.arange(SEQ, dtype=f)
        ones[g % 2, :, g // 2, g] = 1.0
        for part in range(2):
            z[:, :, :, :, ALIBI_ROW + 2 * g + part] = parts[g, part].reshape(2, 2).T[:, None, None, :]
    arrays["sa_q_rows"], arrays["sa_k_rows"] = q_rows.reshape(P, -1), k_rows.reshape(P, -1)
    arrays["sa_z"], arrays["sa_ones"] = z.reshape(P, 2, 2, P), ones.reshape(P, 2, 32)
    wq, wk, wv, wo = (np.asarray(inputs[f"L0_xattn_{n}"]) for n in ("Wq", "Wk", "Wv", "Wo"))
    for name, a in (("ca_wqT", wq), ("ca_wkT", wk)):
        arrays[name] = a.reshape(H2 // 2, 2, D, HD2).transpose(1, 3, 0, 2).reshape(P, H2 // 2, D)
    arrays["ca_wv"] = wv.transpose(1, 0, 2).reshape(D, H2 * HD2)
    arrays["ca_wo"] = wo.reshape(2, 2, 2, 2, HD2, D).transpose(2, 4, 0, 1, 3, 5).reshape(P, 8, D)
    key, query = np.arange(P)[:, None] % SEQ, np.arange(HALF * SEQ)[None] % SEQ
    arrays["ca_mask"] = np.where(key > query, f(-1e30), f(0))
    pick = np.zeros((P, P), f)
    pick[0:8:2, 0:SEQ] = pick[1:8:2, SEQ:P] = 1.0
    pick[SEQ:P] = np.tile(np.eye(SEQ, dtype=f), 2)
    arrays["ca_own"] = np.ascontiguousarray(np.broadcast_to(np.repeat(np.eye(4, dtype=f), 2, 0)[:, :, None], (8, 4, P)))
    arrays["ca_pick"] = pick
    arrays["ctxT"] = np.asarray(inputs["ctx_1024"]).reshape(BATCH * SEQ, D).T
    wg = np.zeros((D, P), f)
    wg[:, 0:E] = inputs["L0_ffn_Wg"]
    arrays["ff_wg"] = wg
    bcast = lambda a, *shape: np.broadcast_to(np.asarray(a, f), (P, *shape))
    arrays["ff_bg"] = bcast(inputs["L0_ffn_bg"], TPS, E)
    arrays["ff_index"] = bcast(np.arange(E), E)
    arrays["ff_dest"] = (TOPK * (P * np.arange(TILES)[None, :, None] + np.arange(P)[:, None, None])
                         + np.arange(TOPK)).astype(f)
    arrays["ff_starts"] = bcast(REGION * np.arange(E), E)
    arrays["ff_thresholds"] = bcast(ROWS * np.arange(FULL), E, FULL)
    arrays["ff_upto"] = bcast(np.tri(E), E, E)
    arrays["ff_run_no"] = bcast(np.arange(RUNS), RUNS)
    arrays["ff_tri"] = np.triu(np.ones((P, P), f), 1)
    pad = np.zeros((P, ROWS // P, WIDTH), f)
    pad[:, :, META + 1] = TOPK * BATCH * SEQ + np.arange(ROWS).reshape(-1, P).T
    arrays["ff_pad"] = pad
    arrays["ff_w1"] = np.asarray(inputs["L0_ffn_W1"]).transpose(1, 0, 2)
    arrays["ff_w2"] = np.asarray(inputs["L0_ffn_W2"]).reshape(E, CH, P, D).transpose(2, 0, 1, 3).reshape(P, E, CH * P)
    arrays["ff_b1"] = np.asarray(inputs["L0_ffn_b1"]).reshape(E, CH, P).transpose(2, 0, 1)
    arrays["ff_b2"] = bcast(inputs["L0_ffn_b2"], E, P)
    return arrays


def kernel(**inputs):
    import numpy as _np
    import concourse.bacc as _bacc
    from concourse import mybir as _mybir
    from concourse.bass_utils import run_bass_kernel_spmd as _run

    nc = _bacc.Bacc("TRN2", target_bir_lowering=False, num_devices=1)
    arrays = {"in_x": _np.ascontiguousarray(inputs["x"])}
    arrays.update((f"in_{n}", _np.ascontiguousarray(a)) for n, a in laid_out(inputs).items())
    aps = {n: nc.dram_tensor(n, a.shape, _mybir.dt.from_np(a.dtype), kind="ExternalInput").ap() for n, a in arrays.items()}
    out = nc.dram_tensor("out_x", (BATCH, SEQ, D), FP32, kind="ExternalOutput").ap()
    decoder(nc, aps.pop("in_x"), {n[3:]: a for n, a in aps.items()}, out)
    r = _run(nc, [arrays], core_ids=[0])
    return r.results[0]["out_x"]
```
